# Optimizing a Trainium2 kernel written in Bass

```python
import numpy as np
import jax
import jax.numpy as jnp

def _softmax(x, axis=-1):
    return jax.nn.softmax(x, axis=axis)
def _gelu(x):
    return jax.nn.gelu(x, approximate=True)
def _silu(x):
    return jax.nn.silu(x)
def _sigmoid(x):
    return jax.nn.sigmoid(x)
def _layernorm(x, axis=-1, eps=1e-5):
    m = jnp.mean(x, axis=axis, keepdims=True)
    v = jnp.var(x, axis=axis, keepdims=True)
    return (x - m) / jnp.sqrt(v + eps)
def _scatter_add(tgt, idx, src, axis=0):
    return tgt.at[idx].add(src)
def _segment_sum(src, seg, n):
    return jax.ops.segment_sum(src, seg, n)

kernel_name = 'mk_conv_seq_d4_conv_nchw192_3a8723'

def setup_inputs(seed: int = 0):
    np.random.seed(seed)
    _w = jnp.asarray
    def _rec_inputs():
        import jax
        import jax.numpy as jnp
        _gk = jax.random.key(seed)
        x = -0.0005963 + 1.001 * jax.random.normal(jax.random.fold_in(_gk, 1), (4, 192, 64, 64), jnp.float32)
        return x
    x = _rec_inputs()
    def _L0_conv_setup():
        import jax, jax.numpy as jnp
        import numpy as np
        D_MODEL = 192
        D_STATE = 16
        D_CONV = 4
        EXPAND = 2
        D_INNER = EXPAND * D_MODEL
        DT_RANK = (D_MODEL + 15) // 16
        B_SZ, H_IMG, W_IMG = (4, 64, 64)
        LN_EPS = 1e-05

        def _mamba(x, W_in, conv_w, conv_b, W_xproj, W_dt, b_dt, A_log, D, W_out):
            Bb, L, _ = x.shape
            xz = x @ W_in
            xr, z = jnp.split(xz, 2, axis=-1)
            xc = jnp.transpose(xr, (0, 2, 1))
            xc = jax.lax.conv_general_dilated(xc, conv_w[:, None, :], (1,), [(D_CONV - 1, 0)], dimension_numbers=('NCH', 'OIH', 'NCH'), feature_group_count=D_INNER)
            xr = jax.nn.silu(jnp.transpose(xc + conv_b[None, :, None], (0, 2, 1)))
            dbl = xr @ W_xproj
            dt = jax.nn.softplus(dbl[..., :DT_RANK] @ W_dt + b_dt)
            Bm = dbl[..., DT_RANK:DT_RANK + D_STATE]
            Cm = dbl[..., DT_RANK + D_STATE:]
            A = -jnp.exp(A_log)

            def step(h, inp):
                dt_t, B_t, C_t, x_t = inp
                h = jnp.exp(dt_t[:, :, None] * A) * h + (dt_t * x_t)[:, :, None] * B_t[:, None, :]
                y_t = jnp.einsum('ben,bn->be', h, C_t)
                return (h, y_t)
            h0 = jnp.zeros((Bb, D_INNER, D_STATE), x.dtype)
            xs = (dt.transpose(1, 0, 2), Bm.transpose(1, 0, 2), Cm.transpose(1, 0, 2), xr.transpose(1, 0, 2))
            _, ys = jax.lax.scan(step, h0, xs)
            y = ys.transpose(1, 0, 2) + xr * D
            y = y * jax.nn.silu(z)
            return y @ W_out
        key = jax.random.key(seed)
        ks = jax.random.split(key, 8)
        s = lambda k, shape, sc: jax.random.normal(k, shape, jnp.float32) * sc
        dt_bias = float(np.log(np.expm1(0.01)))
        return {'x': jax.random.normal(ks[0], (B_SZ, D_MODEL, H_IMG, W_IMG), jnp.float32), 'gamma': jnp.ones((D_MODEL,), jnp.float32), 'beta': jnp.zeros((D_MODEL,), jnp.float32), 'W_in': s(ks[1], (D_MODEL, 2 * D_INNER), 0.05), 'conv_w': s(ks[2], (D_INNER, D_CONV), 0.3), 'conv_b': jnp.zeros((D_INNER,), jnp.float32), 'W_xproj': s(ks[3], (D_INNER, DT_RANK + 2 * D_STATE), 0.05), 'W_dt': s(ks[4], (DT_RANK, D_INNER), 0.1), 'b_dt': jnp.full((D_INNER,), dt_bias, jnp.float32), 'A_log': jnp.log(jnp.tile(jnp.arange(1, D_STATE + 1, dtype=jnp.float32), (D_INNER, 1))), 'D': jnp.ones((D_INNER,), jnp.float32), 'W_out': s(ks[5], (D_INNER, D_MODEL), 0.05)}
    _L0_conv_all = _L0_conv_setup()
    _L0_conv_in = {k: v for k, v in _L0_conv_all.items() if k in ('gamma', 'beta', 'W_in', 'conv_w', 'conv_b', 'W_xproj', 'W_dt', 'b_dt', 'A_log', 'D', 'W_out', )}
    del _L0_conv_all

    def _L1_conv_setup():
        import jax, jax.numpy as jnp
        import numpy as np
        from jax import lax
        C_IN = 192
        NUM_WINDOWS = 8
        WINDOWS = [NUM_WINDOWS // 2, NUM_WINDOWS, NUM_WINDOWS + NUM_WINDOWS // 2]
        CB = C_IN // len(WINDOWS)

        def _conv1x1(x, w, b=None):
            y = jnp.einsum('nchw,oc->nohw', x, w)
            if b is not None:
                y = y + b[None, :, None, None]
            return y

        def _se(x, wse1, wse2):
            y = jnp.mean(x, axis=(2, 3))
            y = jax.nn.relu(jnp.einsum('bc,oc->bo', y, wse1))
            y = jax.nn.sigmoid(jnp.einsum('bc,oc->bo', y, wse2))
            return x * y[:, :, None, None]

        def _dwconv3x3(x, w, b):
            y = lax.conv_general_dilated(x, w, window_strides=(1, 1), padding=((1, 1), (1, 1)), feature_group_count=CB, dimension_numbers=('NCHW', 'OIHW', 'NCHW'))
            return y + b[None, :, None, None]
        key = jax.random.key(seed)
        ks = jax.random.split(key, 8)
        N, H, W = (16, 100, 100)
        rn = lambda k, s, sc: jax.random.normal(k, s, jnp.float32) * sc
        return {'x': rn(ks[0], (N, C_IN, H, W), 1.0), 'w1': rn(ks[1], (CB, C_IN), 0.05), 'b1': jnp.zeros((CB,), jnp.float32), 'w2': rn(ks[2], (CB, CB), 0.05), 'b2': jnp.zeros((CB,), jnp.float32), 'w3': rn(ks[3], (C_IN, 3 * CB), 0.05), 'b3': jnp.zeros((C_IN,), jnp.float32), 'wpos': rn(ks[4], (CB, 1, 3, 3), 0.1), 'bpos': jnp.zeros((CB,), jnp.float32), 'wse1': rn(ks[5], (CB // 16, CB), 0.1), 'wse2': rn(ks[6], (CB, CB // 16), 0.1)}
    _L1_conv_all = _L1_conv_setup()
    _L1_conv_in = {k: v for k, v in _L1_conv_all.items() if k in ('w1', 'b1', 'w2', 'b2', 'w3', 'b3', 'wpos', 'bpos', 'wse1', 'wse2', )}
    del _L1_conv_all

    def _L2_conv_setup():
        import jax, jax.numpy as jnp
        import numpy as np
        key = jax.random.key(seed)
        k1, k2, k3, k4, k5 = jax.random.split(key, 5)
        B, C, H, W = (4, 192, 64, 64)
        Ci = C // 8
        return {'x': jax.random.normal(k1, (B, C, H, W), dtype=jnp.float32), 'Wq': jax.random.normal(k2, (Ci, C), dtype=jnp.float32) * 0.05, 'Wk': jax.random.normal(k3, (Ci, C), dtype=jnp.float32) * 0.05, 'Wv': jax.random.normal(k4, (Ci, C), dtype=jnp.float32) * 0.05, 'Wout': jax.random.normal(k5, (C, Ci), dtype=jnp.float32) * 0.05}
    _L2_conv_all = _L2_conv_setup()
    _L2_conv_in = {k: v for k, v in _L2_conv_all.items() if k in ('Wq', 'Wk', 'Wv', 'Wout', )}
    del _L2_conv_all

    def _L3_conv_setup():
        import jax, jax.numpy as jnp
        import numpy as np
        LATENT = 96
        RDK = LATENT ** 0.5
        key = jax.random.key(seed)
        k1, k2, k3, k4, k5 = jax.random.split(key, 5)
        B, C, H, W = (8, 192, 64, 64)
        x = jax.random.normal(k1, (B, C, H, W), dtype=jnp.float32)
        Wt = jax.random.normal(k2, (3 * LATENT, C), dtype=jnp.float32) * 0.05
        bt = jax.random.normal(k3, (3 * LATENT,), dtype=jnp.float32) * 0.05
        Wd = jax.random.normal(k4, (C, LATENT), dtype=jnp.float32) * 0.05
        bd = jax.random.normal(k5, (C,), dtype=jnp.float32) * 0.05
        return {'x': x, 'Wt': Wt, 'bt': bt, 'Wd': Wd, 'bd': bd}
    _L3_conv_all = _L3_conv_setup()
    _L3_conv_in = {k: v for k, v in _L3_conv_all.items() if k in ('Wt', 'bt', 'Wd', 'bd', )}
    del _L3_conv_all

    return {
        "x": x,
        "L0_conv_gamma": _L0_conv_in["gamma"],
        "L0_conv_beta": _L0_conv_in["beta"],
        "L0_conv_W_in": _L0_conv_in["W_in"],
        "L0_conv_conv_w": _L0_conv_in["conv_w"],
        "L0_conv_conv_b": _L0_conv_in["conv_b"],
        "L0_conv_W_xproj": _L0_conv_in["W_xproj"],
        "L0_conv_W_dt": _L0_conv_in["W_dt"],
        "L0_conv_b_dt": _L0_conv_in["b_dt"],
        "L0_conv_A_log": _L0_conv_in["A_log"],
        "L0_conv_D": _L0_conv_in["D"],
        "L0_conv_W_out": _L0_conv_in["W_out"],
        "L1_conv_w1": _L1_conv_in["w1"],
        "L1_conv_b1": _L1_conv_in["b1"],
        "L1_conv_w2": _L1_conv_in["w2"],
        "L1_conv_b2": _L1_conv_in["b2"],
        "L1_conv_w3": _L1_conv_in["w3"],
        "L1_conv_b3": _L1_conv_in["b3"],
        "L1_conv_wpos": _L1_conv_in["wpos"],
        "L1_conv_bpos": _L1_conv_in["bpos"],
        "L1_conv_wse1": _L1_conv_in["wse1"],
        "L1_conv_wse2": _L1_conv_in["wse2"],
        "L2_conv_Wq": _L2_conv_in["Wq"],
        "L2_conv_Wk": _L2_conv_in["Wk"],
        "L2_conv_Wv": _L2_conv_in["Wv"],
        "L2_conv_Wout": _L2_conv_in["Wout"],
        "L3_conv_Wt": _L3_conv_in["Wt"],
        "L3_conv_bt": _L3_conv_in["bt"],
        "L3_conv_Wd": _L3_conv_in["Wd"],
        "L3_conv_bd": _L3_conv_in["bd"],
    }

def reference(x, L0_conv_gamma, L0_conv_beta, L0_conv_W_in, L0_conv_conv_w, L0_conv_conv_b, L0_conv_W_xproj, L0_conv_W_dt, L0_conv_b_dt, L0_conv_A_log, L0_conv_D, L0_conv_W_out, L1_conv_w1, L1_conv_b1, L1_conv_w2, L1_conv_b2, L1_conv_w3, L1_conv_b3, L1_conv_wpos, L1_conv_bpos, L1_conv_wse1, L1_conv_wse2, L2_conv_Wq, L2_conv_Wk, L2_conv_Wv, L2_conv_Wout, L3_conv_Wt, L3_conv_bt, L3_conv_Wd, L3_conv_bd):
    import jax
    import jax.numpy as jnp
    def _L0_conv_ref(x, gamma, beta, W_in, conv_w, conv_b, W_xproj, W_dt, b_dt, A_log, D, W_out):
        import jax, jax.numpy as jnp
        import numpy as np
        D_MODEL = 192
        D_STATE = 16
        D_CONV = 4
        EXPAND = 2
        D_INNER = EXPAND * D_MODEL
        DT_RANK = (D_MODEL + 15) // 16
        B_SZ, H_IMG, W_IMG = (4, 64, 64)
        LN_EPS = 1e-05

        def _mamba(x, W_in, conv_w, conv_b, W_xproj, W_dt, b_dt, A_log, D, W_out):
            Bb, L, _ = x.shape
            xz = x @ W_in
            xr, z = jnp.split(xz, 2, axis=-1)
            xc = jnp.transpose(xr, (0, 2, 1))
            xc = jax.lax.conv_general_dilated(xc, conv_w[:, None, :], (1,), [(D_CONV - 1, 0)], dimension_numbers=('NCH', 'OIH', 'NCH'), feature_group_count=D_INNER)
            xr = jax.nn.silu(jnp.transpose(xc + conv_b[None, :, None], (0, 2, 1)))
            dbl = xr @ W_xproj
            dt = jax.nn.softplus(dbl[..., :DT_RANK] @ W_dt + b_dt)
            Bm = dbl[..., DT_RANK:DT_RANK + D_STATE]
            Cm = dbl[..., DT_RANK + D_STATE:]
            A = -jnp.exp(A_log)

            def step(h, inp):
                dt_t, B_t, C_t, x_t = inp
                h = jnp.exp(dt_t[:, :, None] * A) * h + (dt_t * x_t)[:, :, None] * B_t[:, None, :]
                y_t = jnp.einsum('ben,bn->be', h, C_t)
                return (h, y_t)
            h0 = jnp.zeros((Bb, D_INNER, D_STATE), x.dtype)
            xs = (dt.transpose(1, 0, 2), Bm.transpose(1, 0, 2), Cm.transpose(1, 0, 2), xr.transpose(1, 0, 2))
            _, ys = jax.lax.scan(step, h0, xs)
            y = ys.transpose(1, 0, 2) + xr * D
            y = y * jax.nn.silu(z)
            return y @ W_out
        Bb, C, Hh, Ww = x.shape
        x_flat = x.reshape(Bb, C, Hh * Ww).transpose(0, 2, 1)
        mu = x_flat.mean(-1, keepdims=True)
        var = ((x_flat - mu) ** 2).mean(-1, keepdims=True)
        x_norm = (x_flat - mu) * jax.lax.rsqrt(var + LN_EPS) * gamma + beta
        x_in = jnp.concatenate([x_norm, x_norm[:, ::-1]], axis=0)
        out2 = _mamba(x_in, W_in, conv_w, conv_b, W_xproj, W_dt, b_dt, A_log, D, W_out)
        out_fwd, out_rev = (out2[:Bb], out2[Bb:, ::-1])
        out = (out_fwd + out_rev) * 0.5 + x_flat
        return out.transpose(0, 2, 1).reshape(Bb, C, Hh, Ww)

    def _L1_conv_ref(x, w1, b1, w2, b2, w3, b3, wpos, bpos, wse1, wse2):
        import jax, jax.numpy as jnp
        import numpy as np
        from jax import lax
        C_IN = 192
        NUM_WINDOWS = 8
        WINDOWS = [NUM_WINDOWS // 2, NUM_WINDOWS, NUM_WINDOWS + NUM_WINDOWS // 2]
        CB = C_IN // len(WINDOWS)

        def _conv1x1(x, w, b=None):
            y = jnp.einsum('nchw,oc->nohw', x, w)
            if b is not None:
                y = y + b[None, :, None, None]
            return y

        def _se(x, wse1, wse2):
            y = jnp.mean(x, axis=(2, 3))
            y = jax.nn.relu(jnp.einsum('bc,oc->bo', y, wse1))
            y = jax.nn.sigmoid(jnp.einsum('bc,oc->bo', y, wse2))
            return x * y[:, :, None, None]

        def _dwconv3x3(x, w, b):
            y = lax.conv_general_dilated(x, w, window_strides=(1, 1), padding=((1, 1), (1, 1)), feature_group_count=CB, dimension_numbers=('NCHW', 'OIHW', 'NCHW'))
            return y + b[None, :, None, None]
        xc = _conv1x1(x, w1, b1)
        N, C, H, W = xc.shape
        out_list = []
        for nw in WINDOWS:
            s = H // nw
            k = s + H % nw
            hi = (jnp.arange(nw) * s)[:, None] + jnp.arange(k)[None, :]
            patches = xc[:, :, hi][..., hi]
            u3 = patches.transpose(0, 1, 3, 5, 2, 4).reshape(N, C * k * k, nw * nw)
            u4 = u3.reshape(-1, C, k, k)
            a = _se(_conv1x1(u4, w2, b2), wse1, wse2) + _dwconv3x3(u4, wpos, bpos)
            a3 = a.reshape(N, C * k * k, nw * nw)
            p = a3.reshape(N, C, k, k, nw, nw).transpose(0, 1, 4, 2, 5, 3)
            hidx = hi[:, :, None, None]
            widx = hi[None, None, :, :]
            folded = jnp.zeros((N, C, H, W), xc.dtype).at[:, :, hidx, widx].add(p)
            cnt = jnp.zeros((H, W), xc.dtype).at[hidx, widx].add(jnp.ones((nw, k, nw, k), xc.dtype))
            out_list.append(folded / cnt[None, None, :, :])
        out = _conv1x1(jnp.concatenate(out_list, axis=1) + x, w3, b3)
        return out

    def _L2_conv_ref(x, Wq, Wk, Wv, Wout):
        import jax, jax.numpy as jnp
        import numpy as np
        q = jnp.einsum('oc,bchw->bohw', Wq, x)
        k = jnp.einsum('oc,bchw->bohw', Wk, x)
        v = jnp.einsum('oc,bchw->bohw', Wv, x)
        B, Ci, H, W = k.shape
        kf = k.reshape(B, Ci, H * W)
        vf = v.reshape(B, Ci, H * W)
        beta = jnp.einsum('bchw,bcL->bLhw', q, kf)
        beta = jax.nn.softmax(beta, axis=1)
        out = jnp.einsum('bLhw,bcL->bchw', beta, vf)
        att = jax.nn.sigmoid(jnp.einsum('oc,bchw->bohw', Wout, out))
        return att * x + x

    def _L3_conv_ref(x, Wt, bt, Wd, bd):
        import jax, jax.numpy as jnp
        import numpy as np
        LATENT = 96
        RDK = LATENT ** 0.5
        B, C, H, W = x.shape
        N = H * W
        t = jnp.einsum('bchw,oc->bohw', x, Wt) + bt[None, :, None, None]
        Q = t[:, :LATENT]
        V = t[:, LATENT:2 * LATENT]
        K = t[:, 2 * LATENT:]
        Qf = Q.reshape(B, LATENT, N)
        Vf = V.reshape(B, LATENT, N)
        Kf = K.reshape(B, LATENT, N)
        score = jnp.einsum('bcq,bck->bqk', Qf, Kf) / jnp.asarray(RDK, x.dtype)
        index = jax.nn.softmax(score, axis=1)
        out = jnp.einsum('bcq,bqk->bck', Vf, index).reshape(B, LATENT, H, W)
        out = jnp.einsum('bchw,oc->bohw', out, Wd) + bd[None, :, None, None]
        return out + x

    def _gn(v, G=32, eps=1e-5):
        B_, C_, H_, W_ = v.shape
        g = v.reshape(B_, G, C_ // G, H_, W_)
        m = jnp.mean(g, axis=(2, 3, 4), keepdims=True)
        s = jnp.var(g, axis=(2, 3, 4), keepdims=True)
        return ((g - m) / jnp.sqrt(s + eps)).reshape(v.shape)

    def _ln_c(v, eps=1e-6):
        m = jnp.mean(v, axis=1, keepdims=True)
        s = jnp.var(v, axis=1, keepdims=True)
        return (v - m) / jnp.sqrt(s + eps)

    def _ln_t(v, eps=1e-5):
        m = jnp.mean(v, axis=-1, keepdims=True)
        s = jnp.var(v, axis=-1, keepdims=True)
        return (v - m) / jnp.sqrt(s + eps)

    def _to_tokens(v):
        B_, C_, H_, W_ = v.shape
        return v.reshape(B_, C_, H_ * W_).transpose(0, 2, 1)
    def _from_tokens(t, like):
        B_, C_, H_, W_ = like.shape
        return t.transpose(0, 2, 1).reshape(B_, C_, H_, W_)

    x = _L0_conv_ref(x, L0_conv_gamma, L0_conv_beta, L0_conv_W_in, L0_conv_conv_w, L0_conv_conv_b, L0_conv_W_xproj, L0_conv_W_dt, L0_conv_b_dt, L0_conv_A_log, L0_conv_D, L0_conv_W_out)
    x = _L1_conv_ref(x, L1_conv_w1, L1_conv_b1, L1_conv_w2, L1_conv_b2, L1_conv_w3, L1_conv_b3, L1_conv_wpos, L1_conv_bpos, L1_conv_wse1, L1_conv_wse2)
    x = _L2_conv_ref(x, L2_conv_Wq, L2_conv_Wk, L2_conv_Wv, L2_conv_Wout)
    x = _L3_conv_ref(x, L3_conv_Wt, L3_conv_bt, L3_conv_Wd, L3_conv_bd)
    return x


_drawn_inputs = setup_inputs


def setup_inputs(seed=0):
    import zlib

    import numpy as np

    out = dict(_drawn_inputs(seed))
    spreads = {'L0_conv_gamma': (1.0, 0.6),
     'L0_conv_beta': (0.0, 0.626),
     'L0_conv_conv_b': (0.0, 0.369),
     'L0_conv_b_dt': (-4.600165843963623, 0.6),
     'L0_conv_D': (1.0, 0.6),
     'L1_conv_b1': (0.0, 0.1),
     'L1_conv_b2': (0.0, 0.1),
     'L1_conv_b3': (0.0, 0.1),
     'L1_conv_bpos': (0.0, 0.1)}
    factors = {'L0_conv_W_xproj': 8.0,
     'L0_conv_W_dt': 8.0,
     'L0_conv_A_log': 8.0,
     'L1_conv_wse1': 8.0,
     'L1_conv_wse2': 8.0,
     'L2_conv_Wq': 8.0,
     'L2_conv_Wk': 8.0,
     'L2_conv_Wv': 8.0,
     'L2_conv_Wout': 8.0,
     'L3_conv_bd': 64.0}
    for name, (base, spread) in spreads.items():
        noise = np.random.default_rng([zlib.crc32(name.encode()), seed]).standard_normal(out[name].shape)
        drawn = base * np.exp(spread * noise) if base else spread * noise
        out[name] = jnp.asarray(drawn.astype(out[name].dtype))
    for name, factor in factors.items():
        out[name] = (out[name] * factor).astype(out[name].dtype)
    return out
```

```python
import concourse.bass as bass
from concourse import mybir
from contextlib import ExitStack

FP32 = mybir.dt.float32
BF16 = mybir.dt.bfloat16
ALU = mybir.AluOpType
ACT = mybir.ActivationFunctionType
AX = mybir.AxisListType

B, C, L = 4, 192, 4096
CH = C // 2
E, EB = 384, 3
NST = 16
RANK = 12
TT = 512
NT = L // TT
CK = 1024
NC = L // CK
SEQ = 2 * B


def freed(b, t, depth, per_tile, tiles):
    base = b * (per_tile * tiles)
    return base + (t - depth + 1) * per_tile if t >= depth else base


def hold(engine, go, semaphore, value):
    engine.wait_ge(semaphore, value)
    engine.sem_inc(go, 1)


def mamba_inputs(nc, sem, x, gamma, beta, w_in, conv_w, conv_b, w_xproj, w_dt, b_dt,
                 dt_d, dtx_d, xs_d, bc_d, gate_d):
    with ExitStack() as ctx:
        def sb(name, shape, dt=FP32):
            return ctx.enter_context(nc.sbuf_tensor("a_" + name, shape, dt))

        def pb(name, shape):
            return ctx.enter_context(nc.psum_tensor("a_" + name, shape, FP32))

        PAD = 3
        ones = sb("ones_mean", [CH, CH])
        eps = sb("eps", [CH, 1])
        w_in_sb = sb("w_in_sb", [CH, 2, 2 * E])
        gam = sb("gam", [CH, 2])
        bet = sb("bet", [CH, 2])
        bias_in = sb("bias_in", [128, 6])
        cw = sb("cw", [128, EB, 4])
        cb = sb("cb", [128, EB])
        bdt = sb("bdt", [128, EB])
        wx = sb("wx", [128, 2, EB, 128])
        wdt = sb("wdt", [128, E])
        xt = sb("xt", [CH, 2, 2, TT])
        xc = sb("xc", [CH, 2, 2, TT])
        sq = sb("sq", [CH, 2, TT])
        lnv = sb("lnv", [CH, TT])
        rstd = sb("rstd", [CH, TT])
        xr = sb("xr", [128, EB, L + 2 * PAD])
        gate = sb("gate", [128, 2, EB, TT])
        xs = sb("xs", [128, 2, 6, TT])
        dbl = sb("dbl", [128, 2, TT])
        part = sb("part", [64, 2, 3, TT], BF16)
        rest = sb("rest", [64, 2, TT])
        e2 = sb("e2", [128, 2, TT])
        e3 = sb("e3", [128, 2, TT])
        e4 = sb("e4", [128, 2, TT])
        e5 = sb("e5", [128, 2, TT])
        e6 = sb("e6", [128, 2, TT])
        dt = sb("dt", [128, 2, 6, TT])
        dtx = sb("dtx", [128, 2, 6, TT])

        p_mean = pb("p_mean", [128, TT])
        p_var = pb("p_var", [128, TT])
        p_in = [pb(f"p_in{i}", [128, TT]) for i in range(2)]
        p_dbl = pb("p_dbl", [128, TT])
        p_dt = [pb(f"p_dt{i}", [128, TT]) for i in range(2)]

        s = {k: sem("a_" + k) for k in (
            "weights", "zeroed", "const", "wg", "bias_mm", "bias", "x0", "x1", "mean", "centred",
            "squared", "var", "lnv", "rstd", "normed", "proj", "xr", "gate", "conv_step", "conv",
            "xs", "xproj", "dbl", "part_step", "parts", "dtproj", "absv", "expv", "onep", "lnw",
            "relu", "fix", "sum", "dt", "dtx", "st0", "st1", "st_bc", "st_gate0", "st_gate1",
            "sp_go", "pool_go")}

        block = ctx.enter_context(nc.Block())

        @block.sync
        def _(sp):
            sp.dma_start(w_in_sb[:, :, :], w_in.rearrange("(h p) n -> p h n", h=2)).then_inc(s["weights"], 16)
            sp.dma_start(gam[:, :], gamma.rearrange("(h p) -> p h", h=2), allow_slow_non_contiguous=True).then_inc(s["weights"], 16)
            sp.dma_start(bet[:, :], beta.rearrange("(h p) -> p h", h=2), allow_slow_non_contiguous=True).then_inc(s["weights"], 16)
            sp.dma_start(cw[:, :, :], conv_w.rearrange("(e p) k -> p e k", p=128)).then_inc(s["weights"], 16)
            sp.dma_start(cb[:, :], conv_b.rearrange("(e p) -> p e", p=128), allow_slow_non_contiguous=True).then_inc(s["weights"], 16)
            sp.dma_start(bdt[:, :], b_dt.rearrange("(e p) -> p e", p=128), allow_slow_non_contiguous=True).then_inc(s["weights"], 16)
            hold(sp, s["sp_go"], s["zeroed"], 1)
            wx_v = w_xproj.rearrange("(e p) n -> p e n", p=128)
            for d in range(2):
                sp.dma_start(wx[:, d, :, 32 * d:32 * d + 2 * NST], wx_v[:, :, RANK:]).then_inc(s["weights"], 16)
                sp.dma_start(wx[:, d, :, 64 + 32 * d:64 + 32 * d + RANK], wx_v[:, :, :RANK]).then_inc(s["weights"], 16)
                sp.dma_start(wdt[64 + 32 * d:64 + 32 * d + RANK, :], w_dt).then_inc(s["weights"], 16)
            x_v = x.rearrange("b (h p) t -> b p h t", h=2)
            with sp.Fori(0, B) as b:
                for t in range(NT + 2):
                    if t < NT:
                        src = x_v[bass.ds(b, 1), :, :, t * TT:(t + 1) * TT].rearrange("a p h t -> (a p) h t")
                        hold(sp, s["sp_go"], s["centred"], freed(b, t, 2, 1, NT))
                        sp.dma_start(xt[:, t % 2, :, :], src).then_inc(s[f"x{t % 2}"], 16)
                    if t >= 2:
                        j = t - 2
                        st = s[f"st{j % 2}"]
                        hold(sp, s["sp_go"], s["gate"], b * (NT * EB) + (j + 1) * EB)
                        sp.dma_start(gate_d[bass.ds(b, 1), j, :, :, :].rearrange("a p e t -> (a p) e t"),
                                     gate[:, j % 2, :, :]).then_inc(s[f"st_gate{j % 2}"], 16)
                        hold(sp, s["sp_go"], s["dtx"], b * (NT * 6) + (j + 1) * 6)
                        hold(sp, s["sp_go"], s["dt"], b * (NT * 6) + (j + 1) * 6)
                        hold(sp, s["sp_go"], s["parts"], b * NT + j + 1)
                        for d in range(2):
                            jj = j if d == 0 else NT - 1 - j
                            c, h = jj // 2, jj % 2
                            for dram, tile in ((dt_d, dt), (dtx_d, dtx), (xs_d, xs)):
                                sp.dma_start(
                                    dram[bass.ds(b + B * d, 1), c, :, :, h * TT:(h + 1) * TT].rearrange(
                                        "a p e t -> (a p) e t"),
                                    tile[:, j % 2, 3 * d:3 * d + 3, :]).then_inc(st, 16)
                            for k in range(3):
                                sp.dma_start(
                                    bc_d[bass.ds(b + B * d, 1), c, 32 * k:32 * k + 32, h * TT:(h + 1) * TT].rearrange(
                                        "a p t -> (a p) t"),
                                    part[32 * d:32 * d + 32, j % 2, k, :]).then_inc(st, 16)
            hold(sp, s["sp_go"], s["st0"], B * NT // 2 * 192)
            hold(sp, s["sp_go"], s["st1"], B * NT // 2 * 192)
            hold(sp, s["sp_go"], s["st_gate0"], B * NT // 2 * 16)
            hold(sp, s["sp_go"], s["st_gate1"], B * NT // 2 * 16)

        def stored(eng, b, j, name="st", per=192):
            v = b * (NT // 2 * per) + (j // 2) * per
            eng.wait_ge(s[f"{name}{j % 2}"], v)

        @block.gpsimd
        def _(pool):
            pool.memset(wx[:, :, :, :], 0.0).then_inc(s["zeroed"], 1)
            pool.memset(ones[:, :], 1.0 / C).then_inc(s["const"], 1)
            pool.memset(eps[:, :], 1e-5).then_inc(s["const"], 1)
            for e in range(EB):
                pool.memset(xr[:, e, 0:PAD], 0.0).then_inc(s["const"], 1)
                pool.memset(xr[:, e, L + PAD:], 0.0).then_inc(s["const"], 1)

            def dt_sums(b, j):
                for k in range(6):
                    g = b * (NT * 6) + j * 6 + k
                    i = k % 2
                    pool.wait_ge(s["expv"], g + 1)
                    pool.wait_ge(s["fix"], freed(b, j * 6 + k, 2, 1, NT * 6))
                    pool.wait_ge(s["lnw"], freed(b, j * 6 + k, 2, 1, NT * 6))
                    pool.sem_inc(s["pool_go"], 1)
                    pool.tensor_scalar(e3[:, i, :], e2[:, i, :], 1.0, 1.0, ALU.mult, ALU.add).then_inc(s["onep"], 1)
                    pool.wait_ge(s["fix"], g + 1)
                    pool.wait_ge(s["lnw"], g + 1)
                    pool.tensor_tensor(e4[:, i, :], e4[:, i, :], e5[:, i, :], ALU.subtract).then_inc(s["sum"], 1)
                    pool.wait_ge(s["sum"], g + 1)
                    pool.wait_ge(s["relu"], g + 1)
                    if k == 0:
                        stored(pool, b, j)
                    pool.tensor_tensor(dt[:, j % 2, k, :], e4[:, i, :], e6[:, i, :], ALU.add).then_inc(s["dt"], 1)

            def split_bc(b, j):
                pool.wait_ge(s["dbl"], b * NT + j + 1)
                stored(pool, b, j)
                n0 = b * (NT * 4) + j * 4
                bc = dbl[0:64, j % 2, :]
                hi, mid, lo = (part[:, j % 2, k, :] for k in range(3))
                r1, r2 = rest[:, 0, :], rest[:, 1, :]
                pool.sem_inc(s["pool_go"], 1)
                pool.tensor_scalar(hi, bc, 1.0, 0.0, ALU.mult, ALU.add).then_inc(s["part_step"], 1)
                pool.wait_ge(s["part_step"], n0 + 1)
                pool.tensor_tensor(r1, bc, hi, ALU.subtract).then_inc(s["part_step"], 1)
                pool.wait_ge(s["part_step"], n0 + 2)
                pool.sem_inc(s["pool_go"], 1)
                pool.tensor_scalar(mid, r1, 1.0, 0.0, ALU.mult, ALU.add).then_inc(s["part_step"], 1)
                pool.wait_ge(s["part_step"], n0 + 3)
                pool.tensor_tensor(r2, r1, mid, ALU.subtract).then_inc(s["part_step"], 1)
                pool.wait_ge(s["part_step"], n0 + 4)
                pool.sem_inc(s["pool_go"], 1)
                pool.tensor_scalar(lo, r2, 1.0, 0.0, ALU.mult, ALU.add).then_inc(s["parts"], 1)

            with pool.Fori(0, B) as b:
                for t in range(NT + 2):
                    if t >= 2:
                        dt_sums(b, t - 2)
                    if 1 <= t <= NT:
                        split_bc(b, t - 1)

        @block.scalar
        def _(act):
            act.wait_ge(s["bias_mm"], 1)
            act.wait_ge(s["const"], 2 + 2 * EB)
            act.activation(bias_in[:, :], p_dbl[:, 0:6], ACT.Identity).then_inc(s["bias"], 1)
            act.wait_ge(s["bias"], 1)

            def rstd_of(b, t):
                act.wait_ge(s["centred"], b * NT + t + 1)
                act.wait_ge(s["var"], freed(b, t, 1, 1, NT))
                act.activation(sq[:, :, :], xc[:, t % 2, :, :], ACT.Square).then_inc(s["squared"], 1)
                act.wait_ge(s["var"], b * NT + t + 1)
                act.activation(lnv[:, :], p_var[0:CH, :], ACT.Ln, bias=eps[:, 0:1]).then_inc(s["lnv"], 1)
                act.wait_ge(s["lnv"], b * NT + t + 1)
                act.wait_ge(s["normed"], freed(b, t, 1, 1, NT))
                act.activation(rstd[:, :], lnv[:, :], ACT.Exp, scale=-0.5).then_inc(s["rstd"], 1)

            def projected(b, t, blocks):
                for m in blocks:
                    act.wait_ge(s["proj"], b * (NT * 6) + t * 6 + m + 1)
                    if m < 3:
                        if t == 0 and m == 0:
                            act.wait_ge(s["conv"], b * (NT * 6))
                        act.activation(xr[:, m, PAD + t * TT:PAD + (t + 1) * TT], p_in[m % 2][:, :],
                                       ACT.Identity, bias=bias_in[:, m:m + 1]).then_inc(s["xr"], 1)
                    else:
                        if m == 3:
                            stored(act, b, t, "st_gate", 16)
                        act.activation(gate[:, t % 2, m - 3, :], p_in[m % 2][:, :], ACT.Silu,
                                       bias=bias_in[:, m:m + 1]).then_inc(s["gate"], 1)

            def softplus(b, j):
                for k in range(7):
                    g = b * (NT * 6) + j * 6 + k
                    i = k % 2
                    if k < 6:
                        act.wait_ge(s["dtproj"], g + 1)
                        act.wait_ge(s["dt"], freed(b, j * 6 + k, 2, 1, NT * 6))
                        act.activation(e2[:, i, :], p_dt[i][:, :], ACT.Abs,
                                       bias=bdt[:, k % 3:k % 3 + 1]).then_inc(s["absv"], 1)
                        act.activation(e6[:, i, :], p_dt[i][:, :], ACT.Relu,
                                       bias=bdt[:, k % 3:k % 3 + 1]).then_inc(s["relu"], 1)
                        act.wait_ge(s["absv"], g + 1)
                        act.activation(e2[:, i, :], e2[:, i, :], ACT.Exp, scale=-1.0).then_inc(s["expv"], 1)
                    if k >= 1:
                        i = (k - 1) % 2
                        act.wait_ge(s["onep"], g)
                        act.activation(e4[:, i, :], e3[:, i, :], ACT.Ln).then_inc(s["lnw"], 1)

            with act.Fori(0, B) as b:
                for t in range(NT + 2):
                    if t < NT:
                        rstd_of(b, t)
                        projected(b, t, (0, 1, 2))
                    if t >= 2:
                        softplus(b, t - 2)
                    if t < NT:
                        projected(b, t, (3, 4, 5))
                    if 1 <= t <= NT:
                        j = t - 1
                        for k in range(6):
                            act.wait_ge(s["conv"], b * (NT * 6) + j * 6 + k + 1)
                            act.activation(xs[:, j % 2, k, :], xs[:, j % 2, k, :], ACT.Silu,
                                           bias=cb[:, k % 3:k % 3 + 1]).then_inc(s["xs"], 1)
                        act.wait_ge(s["xproj"], b * NT + j + 1)
                        act.wait_ge(s["parts"], freed(b, j, 2, 1, NT))
                        act.wait_ge(s["dtproj"], freed(b, j, 2, 6, NT))
                        act.activation(dbl[:, j % 2, :], p_dbl[:, :], ACT.Identity).then_inc(s["dbl"], 1)

        @block.vector
        def _(dve):
            dve.wait_ge(s["weights"], 12 * 16)
            dve.wait_ge(s["bias_mm"], 1)
            for h in range(2):
                dve.tensor_scalar(w_in_sb[:, h, :], w_in_sb[:, h, :], gam[:, h:h + 1], None, ALU.mult).then_inc(s["wg"], 1)
            dve.wait_ge(s["const"], 2 + 2 * EB)

            def normalise(b, t):
                dve.wait_ge(s["mean"], b * NT + t + 1)
                dve.wait_ge(s["proj"], freed(b, t, 2, 6, NT))
                dve.tensor_tensor(xc[:, t % 2, :, :], xt[:, t % 2, :, :],
                                  p_mean[0:CH, None, :].broadcast_to([CH, 2, TT]),
                                  ALU.subtract).then_inc(s["centred"], 1)
                dve.wait_ge(s["rstd"], b * NT + t + 1)
                dve.tensor_tensor(xc[:, t % 2, :, :], xc[:, t % 2, :, :],
                                  rstd[:, None, :].broadcast_to([CH, 2, TT]),
                                  ALU.mult).then_inc(s["normed"], 1)

            def tap(b, j, w, k):
                e = k % 3
                if k < 3:
                    lo = PAD + j * TT - 3 + w
                    src = xr[:, e, lo:lo + TT]
                else:
                    lo = PAD + j * TT + 3 - w
                    src = xr[:, e, lo:lo + TT][:, ::-1]
                out = xs[:, j % 2, k, :]
                wt = cw[:, e, w:w + 1]
                if w == 0:
                    if k == 0:
                        stored(dve, b, j)
                        dve.wait_ge(s["xproj"], freed(b, j, 2, 1, NT))
                        dve.wait_ge(s["dtx"], freed(b, j, 2, 6, NT))
                    dve.tensor_scalar(out, src, wt, None, ALU.mult).then_inc(s["conv_step"], 1)
                else:
                    dve.wait_ge(s["conv_step"], b * (NT * 18) + j * 18 + (w - 1) * 6 + k + 1)
                    ins = dve.scalar_tensor_tensor(out, src, wt, out, ALU.mult, ALU.add)
                    ins.then_inc(s["conv"] if w == 3 else s["conv_step"], 1)

            def rounding(b, j, k):
                g = b * (NT * 6) + j * 6 + k
                dve.wait_ge(s["onep"], g + 1)
                dve.wait_ge(s["sum"], freed(b, j * 6 + k, 2, 1, NT * 6))
                dve.scalar_tensor_tensor(e5[:, k % 2, :], e3[:, k % 2, :], 1.0, e2[:, k % 2, :],
                                         ALU.subtract, ALU.subtract).then_inc(s["fix"], 1)

            def times_x(b, j, k):
                g = b * (NT * 6) + j * 6 + k
                dve.wait_ge(s["dt"], g + 1)
                if k == 0:
                    stored(dve, b, j)
                dve.tensor_tensor(dtx[:, j % 2, k, :], dt[:, j % 2, k, :], xs[:, j % 2, k, :],
                                  ALU.mult).then_inc(s["dtx"], 1)

            with dve.Fori(0, B) as b:
                for t in range(NT + 2):
                    if t < NT:
                        normalise(b, t)
                        dve.wait_ge(s["xr"], b * (NT * 3) + (t + 1) * 3)
                    for k in range(8):
                        if t >= 2 and k < 6:
                            rounding(b, t - 2, k)
                        if 1 <= t <= NT:
                            for n in range(3 * k, 3 * k + 3):
                                tap(b, t - 1, n // 6, n % 6)
                        if t >= 2 and k >= 2:
                            times_x(b, t - 2, k - 2)

        @block.tensor
        def _(pe):
            pe.wait_ge(s["weights"], 12 * 16)
            pe.wait_ge(s["const"], 2 + 2 * EB)
            for m in range(6):
                for h in range(2):
                    mm = pe.matmul(p_dbl[:, m:m + 1], w_in_sb[:, h, m * 128:(m + 1) * 128], bet[:, h:h + 1],
                                   start=(h == 0), stop=(h == 1))
            mm.then_inc(s["bias_mm"], 1)
            pe.wait_ge(s["bias"], 1)
            pe.wait_ge(s["wg"], 2)
            n_x = NT // 2 * 16

            def statistics(b, t):
                pe.wait_ge(s[f"x{t % 2}"], b * n_x + (t // 2 + 1) * 16)
                pe.wait_ge(s["centred"], freed(b, t, 1, 1, NT))
                for h in range(2):
                    mm = pe.matmul(p_mean[0:CH, :], ones[:, :], xt[:, t % 2, h, :], start=(h == 0), stop=(h == 1))
                mm.then_inc(s["mean"], 1)
                pe.wait_ge(s["squared"], b * NT + t + 1)
                pe.wait_ge(s["lnv"], freed(b, t, 1, 1, NT))
                for h in range(2):
                    mm = pe.matmul(p_var[0:CH, :], ones[:, :], sq[:, h, :], start=(h == 0), stop=(h == 1))
                mm.then_inc(s["var"], 1)

            def project(b, t, blocks):
                for m in blocks:
                    if t == 0 and m < 2:
                        pe.wait_ge(s["gate"], b * (NT * 3))
                    elif m < 2:
                        pe.wait_ge(s["gate"], b * (NT * 3) + (t - 1) * 3 + m + 2)
                    elif m < 5:
                        pe.wait_ge(s["xr"], b * (NT * 3) + t * 3 + m - 1)
                    else:
                        pe.wait_ge(s["gate"], b * (NT * 3) + t * 3 + 1)
                    for h in range(2):
                        mm = pe.matmul(p_in[m % 2][:, :], w_in_sb[:, h, m * 128:(m + 1) * 128],
                                       xc[:, t % 2, h, :], start=(h == 0), stop=(h == 1))
                    mm.then_inc(s["proj"], 1)

            def dt_projection(b, j):
                for k in range(6):
                    lo = 64 + 32 * (k // 3)
                    pe.wait_ge(s["relu"], freed(b, j * 6 + k, 2, 1, NT * 6))
                    pe.matmul(p_dt[k % 2][:, :], wdt[lo:lo + RANK, (k % 3) * 128:(k % 3 + 1) * 128],
                              dbl[lo:lo + RANK, j % 2, :], start=True, stop=True,
                              tile_position=(lo, 0)).then_inc(s["dtproj"], 1)

            def x_projection(b, j):
                pe.wait_ge(s["dbl"], freed(b, j, 1, 1, NT))
                for k in range(6):
                    pe.wait_ge(s["xs"], b * (NT * 6) + j * 6 + k + 1)
                    mm = pe.matmul(p_dbl[:, :], wx[:, k // 3, k % 3, :], xs[:, j % 2, k, :],
                                   start=(k == 0), stop=(k == 5))
                mm.then_inc(s["xproj"], 1)

            with pe.Fori(0, B) as b:
                for t in range(NT + 2):
                    if t < NT:
                        statistics(b, t)
                        pe.wait_ge(s["normed"], b * NT + t + 1)
                        project(b, t, (0, 1, 2))
                    if t >= 2:
                        pe.wait_ge(s["dbl"], b * NT + t - 1)
                        dt_projection(b, t - 2)
                    if t < NT:
                        project(b, t, (3, 4, 5))
                    if 1 <= t <= NT:
                        x_projection(b, t - 1)

    nc.clear_and_free_semaphores(list(s.values()))
    nc.all_engine_barrier()


def selective_scan(nc, sem, a_log, d_skip, dt_d, dtx_d, xs_d, bc_d, y_d):
    with ExitStack() as ctx:
        def sb(name, shape, dt=FP32):
            return ctx.enter_context(nc.sbuf_tensor("b_" + name, shape, dt))

        TPC = NST * EB
        TPS = NC * TPC
        NPS = NC * NST
        ND, NU, NH, NY = 4, 4, 4, 4

        ident = sb("ident", [128, 128])
        diag_d = sb("diag_d", [128, EB, 128])
        sel = sb("sel", [96, 2 * NST, 128], BF16)
        a_neg = sb("a_neg", [128, EB, NST])
        dsk = sb("dsk", [128, EB])
        dt = sb("dt", [128, 2, EB, CK])
        dtx = sb("dtx", [128, 2, EB, CK])
        xs = sb("xs", [128, EB, CK])
        bc = sb("bc", [96, 2, CK], BF16)
        decay = sb("decay", [128, ND, CK])
        inp = sb("inp", [128, NU, CK])
        hid = sb("hid", [128, NH, CK])
        hc = sb("hc", [128, NY, CK])
        b_row = sb("b_row", [128, 4, CK])
        c_row = sb("c_row", [128, 4, CK])
        carry = sb("carry", [128, TPC])
        y_sb = sb("y_sb", [128, EB, CK])
        p_row = ctx.enter_context(nc.psum_tensor("b_p_row", [128, CK], FP32))
        p_y = ctx.enter_context(nc.psum_tensor("b_p_y", [128, EB, CK], FP32))

        s = {k: sem("b_" + k) for k in (
            "a_loaded", "a_exp", "a_neg", "made", "ident", "sel", "diag", "dt0", "dt1", "dtx0", "dtx1", "xs",
            "bc0", "bc1", "spread", "taken", "decay", "input", "scan", "product", "summed", "skip",
            "carried", "y_out", "stored", "sp_go")}

        block = ctx.enter_context(nc.Block())

        def used(q, k, depth, per):
            return freed(q, k, depth, 1, per)

        def one(dram, q, c):
            return dram[bass.ds(q, 1), c, :, :, :].rearrange("a p e t -> (a p) e t")

        def load(sp, q, c):
            sp.dma_start(bc[:, c % 2, :], bc_d[bass.ds(q, 1), c, :, :].rearrange("a p t -> (a p) t")
                         ).then_inc(s[f"bc{c % 2}"], 16)
            sp.dma_start(dt[:, c % 2, :, :], one(dt_d, q, c)).then_inc(s[f"dt{c % 2}"], 16)
            sp.dma_start(dtx[:, c % 2, :, :], one(dtx_d, q, c)).then_inc(s[f"dtx{c % 2}"], 16)

        def load_x(sp, q, c):
            sp.dma_start(xs[:, :, :], one(xs_d, q, c)).then_inc(s["xs"], 16)

        def turn(sp, q, c, last):
            hold(sp, s["sp_go"], s["skip"], q * NC + c + 1)
            if c + 1 < NC:
                load_x(sp, q, c + 1)
            elif not last:
                load_x(sp, q + 1, 0)
            if c + 2 < NC or not last:
                hold(sp, s["sp_go"], s["decay"], q * TPS + (c + 1) * TPC)
                hold(sp, s["sp_go"], s["input"], q * TPS + (c + 1) * TPC)
                hold(sp, s["sp_go"], s["spread"], q * (2 * NPS) + (c + 1) * 2 * NST)
                load(sp, q + (c + 2) // NC, (c + 2) % NC)
            hold(sp, s["sp_go"], s["y_out"], q * (NC * EB) + (c + 1) * EB)
            sp.dma_start(one(y_d, q, c), y_sb[:, :, :]).then_inc(s["stored"], 16)

        @block.sync
        def _(sp):
            sp.dma_start(a_neg[:, :, :], a_log.rearrange("(e p) n -> p e n", p=128)).then_inc(s["a_loaded"], 16)
            sp.dma_start(dsk[:, :], d_skip.rearrange("(e p) -> p e", p=128),
                         allow_slow_non_contiguous=True).then_inc(s["a_loaded"], 16)
            load(sp, 0, 0)
            load_x(sp, 0, 0)
            load(sp, 0, 1)
            with sp.Fori(0, SEQ - 1) as q:
                for c in range(NC):
                    turn(sp, q, c, False)
            for c in range(NC):
                turn(sp, SEQ - 1, c, True)
            hold(sp, s["sp_go"], s["stored"], SEQ * NC * 16)

        @block.gpsimd
        def _(pool):
            pool.memset(ident[:, :], 0.0).then_inc(s["made"], 1)
            pool.memset(sel[:, :, :], 0.0).then_inc(s["made"], 1)
            pool.wait_ge(s["made"], 2)
            pool.affine_select(out=ident[:, :], in_=ident[:, :], compare_op=ALU.not_equal, fill=1.0, base=0,
                               pattern=[[-1, 128]], channel_multiplier=1).then_inc(s["ident"], 1)
            for k in range(3):
                pool.affine_select(out=sel[:, :, :], in_=sel[:, :, :], compare_op=ALU.not_equal, fill=1.0,
                                   base=-32 * k, pattern=[[-1, 2 * NST], [0, 128]],
                                   channel_multiplier=1).then_inc(s["sel"], 1)
                pool.wait_ge(s["sel"], k + 1)
            with pool.Fori(0, SEQ) as q:
                for c in range(NC):
                    for n in range(NST):
                        m = c * NST + n
                        for e in range(EB):
                            k = c * TPC + n * EB + e
                            if k % TPC == 0:
                                pool.wait_ge(s[f"dtx{c % 2}"], q * (NC // 2 * 16) + (c // 2 + 1) * 16)
                            if e == 0:
                                pool.wait_ge(s["taken"], q * (2 * NPS) + 2 * m + 1)
                            pool.wait_ge(s["scan"], used(q, k, NU, TPS))
                            pool.tensor_tensor(inp[:, k % NU, :], dtx[:, c % 2, e, :], b_row[:, m % 4, :],
                                               ALU.mult).then_inc(s["input"], 1)

        @block.scalar
        def _(act):
            act.wait_ge(s["a_loaded"], 32)
            act.activation(a_neg[:, :, :], a_neg[:, :, :], ACT.Exp).then_inc(s["a_exp"], 1)
            act.wait_ge(s["a_exp"], 1)
            act.activation(a_neg[:, :, :], a_neg[:, :, :], ACT.Copy, scale=-1.0).then_inc(s["a_neg"], 1)
            act.wait_ge(s["a_neg"], 1)

            def take(q, m, row):
                act.wait_ge(s["spread"], q * (2 * NPS) + 2 * m + row + 1)
                if row == 0:
                    act.wait_ge(s["input"], freed(q, m, 4, EB, NPS))
                    out = b_row[:, m % 4, :]
                else:
                    act.wait_ge(s["product"], freed(q, m, 4, EB, NPS))
                    out = c_row[:, m % 4, :]
                act.activation(out, p_row[:, :], ACT.Copy).then_inc(s["taken"], 1)

            def keep_state(q, k):
                act.wait_ge(s["scan"], q * TPS + k + 1)
                act.activation(carry[:, k % TPC:k % TPC + 1], hid[:, k % NH, CK - 1:CK],
                               ACT.Copy).then_inc(s["carried"], 1)

            def y_out(q, c):
                act.wait_ge(s["summed"], q * TPS + (c + 1) * TPC)
                act.wait_ge(s["stored"], q * (NC * 16) + c * 16)
                for e in range(EB):
                    act.activation(y_sb[:, e, :], p_y[:, e, :], ACT.Copy).then_inc(s["y_out"], 1)

            with act.Fori(0, SEQ) as q:
                take(q, 0, 0)
                take(q, 0, 1)
                for m in range(NPS):
                    c = m // NST
                    for e in range(EB):
                        k = 3 * m + e
                        if k % TPC == 0:
                            act.wait_ge(s[f"dt{c % 2}"], q * (NC // 2 * 16) + (c // 2 + 1) * 16)
                        act.wait_ge(s["scan"], used(q, k, ND, TPS))
                        n = m % NST
                        act.activation(decay[:, k % ND, :], dt[:, c % 2, e, :], ACT.Exp,
                                       scale=a_neg[:, e, n:n + 1]).then_inc(s["decay"], 1)
                        if k >= 2:
                            keep_state(q, k - 2)
                        if e >= 1 and m + 1 < NPS:
                            take(q, m + 1, e - 1)
                    if m % NST == 0 and m:
                        y_out(q, c - 1)
                keep_state(q, TPS - 2)
                keep_state(q, TPS - 1)
                y_out(q, NC - 1)

        @block.vector
        def _(dve):
            dve.wait_ge(s["a_loaded"], 32)
            dve.wait_ge(s["ident"], 1)
            for e in range(EB):
                dve.tensor_scalar(diag_d[:, e, :], ident[:, :], dsk[:, e:e + 1], None, ALU.mult).then_inc(s["diag"], 1)

            def product(q, k):
                m = k // EB
                dve.wait_ge(s["scan"], q * TPS + k + 1)
                dve.wait_ge(s["taken"], q * (2 * NPS) + 2 * m + 2)
                dve.wait_ge(s["summed"], used(q, k, NY, TPS))
                dve.tensor_tensor(hc[:, k % NY, :], hid[:, k % NH, :], c_row[:, m % 4, :],
                                  ALU.mult).then_inc(s["product"], 1)

            with dve.Fori(0, SEQ) as q:
                for k in range(TPS):
                    c = k // TPC
                    dve.wait_ge(s["decay"], q * TPS + k + 1)
                    dve.wait_ge(s["input"], q * TPS + k + 1)
                    dve.wait_ge(s["carried"], used(q, k, NH, TPS))
                    if k >= NH:
                        dve.wait_ge(s["product"], q * TPS + k - NH + 1)
                    start = 0.0 if c == 0 else carry[:, k % TPC:k % TPC + 1]
                    dve.tensor_tensor_scan(hid[:, k % NH, :], decay[:, k % ND, :], inp[:, k % NU, :], start,
                                           ALU.mult, ALU.add).then_inc(s["scan"], 1)
                    if k >= 1:
                        product(q, k - 1)
                product(q, TPS - 1)

        @block.tensor
        def _(pe):
            pe.wait_ge(s["sel"], 3)
            pe.wait_ge(s["diag"], EB)

            def spread(q, m, row):
                c, n = m // NST, m % NST
                if row == 0 and n == 0:
                    pe.wait_ge(s[f"bc{c % 2}"], q * (NC // 2 * 16) + (c // 2 + 1) * 16)
                pe.wait_ge(s["taken"], q * (2 * NPS) + 2 * m + row)
                for h in range(2):
                    mm = pe.matmul(p_row[:, h * 512:(h + 1) * 512], sel[:, n + NST * row, :],
                                   bc[:, c % 2, h * 512:(h + 1) * 512], start=True, stop=True)
                mm.then_inc(s["spread"], 1)

            def skip(q, c):
                pe.wait_ge(s["xs"], q * (NC * 16) + (c + 1) * 16)
                pe.wait_ge(s["y_out"], q * (NC * EB) + c * EB)
                for e in range(EB):
                    for h in range(2):
                        mm = pe.matmul(p_y[:, e, h * 512:(h + 1) * 512], diag_d[:, e, :],
                                       xs[:, e, h * 512:(h + 1) * 512], start=True, stop=False)
                mm.then_inc(s["skip"], 1)

            def add_state(q, k):
                e, last = k % EB, k % TPC >= TPC - EB
                pe.wait_ge(s["product"], q * TPS + k + 1)
                for h in range(2):
                    mm = pe.matmul(p_y[:, e, h * 512:(h + 1) * 512], ident[:, :],
                                   hc[:, k % NY, h * 512:(h + 1) * 512], start=False, stop=last)
                mm.then_inc(s["summed"], 1)

            with pe.Fori(0, SEQ) as q:
                spread(q, 0, 0)
                spread(q, 0, 1)
                for m in range(NPS + 1):
                    if m + 1 < NPS:
                        spread(q, m + 1, 0)
                    if m >= 1:
                        if (m - 1) % NST == 0:
                            skip(q, (m - 1) // NST)
                        add_state(q, 3 * m - 3)
                    if m + 1 < NPS:
                        spread(q, m + 1, 1)
                    if m >= 1:
                        add_state(q, 3 * m - 2)
                        add_state(q, 3 * m - 1)

    nc.clear_and_free_semaphores(list(s.values()))
    nc.all_engine_barrier()


def mamba_output(nc, sem, x, w_out, y_d, gate_d, x1_d):
    with ExitStack() as ctx:
        def sb(name, shape, dt=FP32):
            return ctx.enter_context(nc.sbuf_tensor("c_" + name, shape, dt))

        W = 2 * TT
        w_sb = sb("w", [128, EB, C])
        yf = sb("yf", [128, 2, EB, W])
        yr = sb("yr", [128, 2, EB, W])
        gt = sb("gt", [128, 2, 2, EB, TT])
        xt = sb("xt", [CH, 2, 2, W])
        out = sb("out", [CH, 2, 2, W])
        p_o = ctx.enter_context(nc.psum_tensor("c_p_o", [128, 2, 2, TT], FP32))
        s = {k: sem("c_" + k) for k in ("weights", "in0", "in1", "both", "gated", "mm", "out", "st0", "st1", "sp_go")}
        block = ctx.enter_context(nc.Block())
        x_v = x.rearrange("b (h p) t -> b p h t", h=2)
        o_v = x1_d.rearrange("b (h p) t -> b p h t", h=2)
        NL = 5

        def store(sp, b, c):
            hold(sp, s["sp_go"], s["out"], b * (NC * 4) + (c + 1) * 4)
            sp.dma_start(o_v[bass.ds(b, 1), :, :, c * W:(c + 1) * W].rearrange("a p h t -> (a p) h t"),
                         out[:, c % 2, :, :]).then_inc(s[f"st{c % 2}"], 16)

        @block.sync
        def _(sp):
            sp.dma_start(w_sb[:, :, :], w_out.rearrange("(e p) n -> p e n", p=128)).then_inc(s["weights"], 16)
            with sp.Fori(0, B) as b:
                for c in range(NC):
                    i = c % 2
                    ld = s[f"in{i}"]
                    hold(sp, s["sp_go"], s["out"], freed(b, c, 2, 4, NC))
                    sp.dma_start(yf[:, i, :, :], y_d[bass.ds(b, 1), c, :, :, :].rearrange("a p e t -> (a p) e t")).then_inc(ld, 16)
                    sp.dma_start(yr[:, i, :, :], y_d[bass.ds(b + B, 1), NC - 1 - c, :, :, :].rearrange("a p e t -> (a p) e t")).then_inc(ld, 16)
                    for h in range(2):
                        sp.dma_start(gt[:, i, h, :, :], gate_d[bass.ds(b, 1), 2 * c + h, :, :, :].rearrange("a p e t -> (a p) e t")).then_inc(ld, 16)
                    sp.dma_start(xt[:, i, :, :], x_v[bass.ds(b, 1), :, :, c * W:(c + 1) * W].rearrange("a p h t -> (a p) h t")).then_inc(ld, 16)
                    if c >= 1:
                        store(sp, b, c - 1)
                store(sp, b, NC - 1)
            for i in range(2):
                hold(sp, s["sp_go"], s[f"st{i}"], B * NC // 2 * 16)

        @block.vector
        def _(dve):
            def gated(b, c):
                i = c % 2
                dve.wait_ge(s[f"in{i}"], b * (NC // 2 * 16 * NL) + (c // 2 + 1) * 16 * NL)
                dve.tensor_tensor(yf[:, i, :, :], yf[:, i, :, :], yr[:, i, :, ::-1], ALU.add).then_inc(s["both"], 1)
                dve.wait_ge(s["both"], b * NC + c + 1)
                for h in range(2):
                    v = yf[:, i, :, h * TT:(h + 1) * TT]
                    dve.tensor_tensor(v, v, gt[:, i, h, :, :], ALU.mult).then_inc(s["gated"], 1)

            def finish(b, c):
                i = c % 2
                dve.wait_ge(s[f"st{i}"], b * (NC // 2 * 16) + c // 2 * 16)
                for h in range(2):
                    for m in range(2):
                        dve.wait_ge(s["mm"], b * (NC * 4) + c * 4 + 2 * h + m + 1)
                        dve.scalar_tensor_tensor(out[:, i, m, h * TT:(h + 1) * TT], p_o[0:CH, h, m, :], 0.5,
                                                 xt[:, i, m, h * TT:(h + 1) * TT], ALU.mult,
                                                 ALU.add).then_inc(s["out"], 1)

            dve.wait_ge(s["weights"], 16)
            with dve.Fori(0, B) as b:
                for c in range(NC + 1):
                    if c < NC:
                        gated(b, c)
                    if c >= 1:
                        finish(b, c - 1)

        @block.tensor
        def _(pe):
            pe.wait_ge(s["weights"], 16)
            with pe.Fori(0, B) as b:
                for c in range(NC):
                    for h in range(2):
                        pe.wait_ge(s["gated"], b * (NC * 2) + c * 2 + h + 1)
                        for m in range(2):
                            g = c * 4 + 2 * h + m
                            pe.wait_ge(s["out"], freed(b, g, 4, 1, NC * 4))
                            for e in range(EB):
                                mm = pe.matmul(p_o[0:CH, h, m, :], w_sb[:, e, m * CH:(m + 1) * CH],
                                               yf[:, c % 2, e, h * TT:(h + 1) * TT], start=(e == 0), stop=(e == EB - 1))
                            mm.then_inc(s["mm"], 1)

    nc.clear_and_free_semaphores(list(s.values()))
    nc.all_engine_barrier()


CB = 64
WINDOWS = (4, 8, 12)
STEP = tuple(64 // n for n in WINDOWS)
SIDE = tuple(64 // n + 64 % n for n in WINDOWS)
AREA = tuple(k * k for k in SIDE)
NWIN = tuple(n * n for n in WINDOWS)
FLAT = tuple(AREA[j] * NWIN[j] for j in range(3))
IMG = 64


def windows_cut(nc, sem, x1_d, w1t, b1, pat_d):
    with ExitStack() as ctx:
        def sb(name, shape, dt=FP32):
            return ctx.enter_context(nc.sbuf_tensor("d_" + name, shape, dt))

        w = sb("w", [CB, 3, CB])
        bias = sb("bias", [CB, 1])
        xt = sb("xt", [CB, 2, 3, TT])
        xc = sb("xc", [CB, 2, L])
        flat = [sb(f"flat{j}", [CB, FLAT[j]]) for j in range(3)]
        p = ctx.enter_context(nc.psum_tensor("d_p", [CB, 4, TT], FP32))
        s = {k: sem("d_" + k) for k in ("weights", "x0", "x1", "mm", "conv", "cut0", "cut1", "cut2",
                                        "st0", "st1", "st2", "sp_go", "pe_go")}
        block = ctx.enter_context(nc.Block())
        x_v = x1_d.rearrange("b (g p) t -> b p g t", g=3)

        def cutting(eng, copy, b, j, par):
            n, k, st = WINDOWS[j], SIDE[j], STEP[j]
            src0 = xc[:, par, :]
            d0 = flat[j][:, :]
            for i in range(k):
                src = bass.AP(src0.tensor, src0.offset + i * IMG, [src0.ap[0], [st * IMG, n], [1, k], [st, n]])
                dst = bass.AP(d0.tensor, d0.offset + i * k * n * n, [d0.ap[0], [n, n], [n * n, k], [1, n]])
                copy(dst, src).then_inc(s[f"cut{j}"], 1)

        @block.sync
        def _(sp):
            sp.dma_start(w[:, :, :], w1t.rearrange("(g p) n -> p g n", g=3)).then_inc(s["weights"], 16)
            sp.dma_start(bias[:, :], b1.rearrange("(p a) -> p a", a=1)).then_inc(s["weights"], 16)
            with sp.Fori(0, B) as b:
                for t in range(NT):
                    hold(sp, s["sp_go"], s["mm"], freed(b, t, 2, 1, NT))
                    sp.dma_start(xt[:, t % 2, :, :], x_v[bass.ds(b, 1), :, :, t * TT:(t + 1) * TT].rearrange(
                        "a p g t -> (a p) g t")).then_inc(s[f"x{t % 2}"], 16)
                for j in range(3):
                    hold(sp, s["sp_go"], s[f"cut{j}"], (b + 1) * SIDE[j])
                    sp.dma_start(pat_d[j][bass.ds(b, 1), :].rearrange("a (c f) -> (a c) f", c=CB),
                                 flat[j][:, :]).then_inc(s[f"st{j}"], 16)
            for j in range(3):
                hold(sp, s["sp_go"], s[f"st{j}"], B * 16)

        @block.scalar
        def _(act):
            act.wait_ge(s["weights"], 32)
            with act.Fori(0, B // 2) as bb:
                for par in range(2):
                    b = bb * 2 + par
                    for t in range(NT):
                        act.wait_ge(s["mm"], b * NT + t + 1)
                        if t == 0:
                            act.wait_ge(s["cut0"], bb * (2 * SIDE[0]))
                            act.wait_ge(s["cut1"], bb * (2 * SIDE[1]))
                        act.activation(xc[:, par, t * TT:(t + 1) * TT], p[:, t % 4, :], ACT.Identity,
                                       bias=bias[:, 0:1]).then_inc(s["conv"], 1)
                    act.wait_ge(s["conv"], (b + 1) * NT)
                    act.wait_ge(s["st2"], b * 16)
                    cutting(act, lambda o, i: act.activation(o, i, ACT.Copy), b, 2, par)

        @block.vector
        def _(dve):
            with dve.Fori(0, B // 2) as bb:
                for par in range(2):
                    b = bb * 2 + par
                    dve.wait_ge(s["conv"], (b + 1) * NT)
                    for j in range(2):
                        dve.wait_ge(s[f"st{j}"], b * 16)
                        cutting(dve, dve.tensor_copy, b, j, par)

        @block.tensor
        def _(pe):
            pe.wait_ge(s["weights"], 32)
            with pe.Fori(0, B) as b:
                for t in range(NT):
                    pe.wait_ge(s[f"x{t % 2}"], b * (NT // 2 * 16) + (t // 2 + 1) * 16)
                    pe.wait_ge(s["conv"], freed(b, t, 4, 1, NT))
                    pe.sem_inc(s["pe_go"], 1)
                    for g in range(3):
                        mm = pe.matmul(p[:, t % 4, :], w[:, g, :], xt[:, t % 2, g, :], start=(g == 0), stop=(g == 2))
                    mm.then_inc(s["mm"], 1)

    nc.clear_and_free_semaphores(list(s.values()))
    nc.all_engine_barrier()


def windows_attend(nc, sem, w2t, b2, wpos, bpos, wse1t, wse2t, pat_d, att_d):
    with ExitStack() as ctx:
        def sb(name, shape, dt=FP32):
            return ctx.enter_context(nc.sbuf_tensor("e_" + name, shape, dt))

        HW = tuple(n // 2 for n in NWIN)
        GW = tuple(512 // a for a in AREA)
        NG = tuple(HW[j] // GW[j] for j in range(3))
        groups = [(j, g) for j in range(3) for g in range(NG[j])]
        NGR = len(groups)
        ident = sb("ident", [128, 128])
        w2 = sb("w2", [128, 128])
        se1 = sb("se1", [128, 8])
        se2 = sb("se2", [8, 128])
        b2s = sb("b2s", [128, 1])
        bps = sb("bps", [128, 1])
        wp = sb("wp", [128, 9])
        dw = sb("dw", [128, 9, 128])
        u = [sb(f"u{j}", [128, HW[j], AREA[j]]) for j in range(3)]
        scaled = sb("scaled", [128, 2, 512])
        total = sb("total", [128, 2, max(HW)])
        mean_y = sb("mean_y", [128, max(HW)])
        hidden = sb("hidden", [8, max(HW)])
        gain = [sb(f"gain{j}", [128, HW[j]]) for j in range(3)]
        NB = 3
        p_y = ctx.enter_context(nc.psum_tensor("e_p_y", [128, NB, 512], FP32))
        p_d = ctx.enter_context(nc.psum_tensor("e_p_d", [128, NB, 512], FP32))
        p_se = ctx.enter_context(nc.psum_tensor("e_p_se", [128, 512], FP32))
        s = {k: sem("e_" + k) for k in (
            "made", "ident", "weights", "dw", "u0", "u1", "u2", "total", "se1", "mean", "se2", "hidden", "se3",
            "gain", "mm", "scaled", "att", "st0", "st1", "st2", "sp_go")}
        block = ctx.enter_context(nc.Block())
        NW = 12

        def halves(dram, b, j, h):
            v = dram[j].rearrange("b (h w c p) -> b h c w p", h=2, w=HW[j], c=CB)
            return v[bass.ds(b, 1), h, :, :, :].rearrange("a c w p -> (a c) w p")

        @block.sync
        def _(sp):
            hold(sp, s["sp_go"], s["made"], 4)
            for h in range(2):
                r = slice(64 * h, 64 * h + 64)
                sp.dma_start(w2[r, r], w2t).then_inc(s["weights"], 16)
                sp.dma_start(se1[r, 4 * h:4 * h + 4], wse1t).then_inc(s["weights"], 16)
                sp.dma_start(se2[4 * h:4 * h + 4, r], wse2t).then_inc(s["weights"], 16)
                sp.dma_start(b2s[r, :], b2.rearrange("(p a) -> p a", a=1)).then_inc(s["weights"], 16)
                sp.dma_start(bps[r, :], bpos.rearrange("(p a) -> p a", a=1)).then_inc(s["weights"], 16)
                sp.dma_start(wp[r, :], wpos).then_inc(s["weights"], 16)
            with sp.Fori(0, B) as b:
                for j in range(3):
                    hold(sp, s["sp_go"], s[f"st{j}"], b * 32)
                    for h in range(2):
                        sp.dma_start(u[j][64 * h:64 * h + 64, :, :], halves(pat_d, b, j, h)).then_inc(s[f"u{j}"], 16)
                for j in range(3):
                    hold(sp, s["sp_go"], s["att"], b * NGR + sum(NG[:j + 1]))
                    for h in range(2):
                        sp.dma_start(halves(att_d, b, j, h), u[j][64 * h:64 * h + 64, :, :]).then_inc(s[f"st{j}"], 16)
            for j in range(3):
                hold(sp, s["sp_go"], s[f"st{j}"], B * 32)

        @block.gpsimd
        def _(pool):
            for t in (w2, se1, se2, ident):
                pool.memset(t[:, :], 0.0).then_inc(s["made"], 1)
            pool.wait_ge(s["made"], 4)
            pool.affine_select(out=ident[:, :], in_=ident[:, :], compare_op=ALU.not_equal, fill=1.0, base=0,
                               pattern=[[-1, 128]], channel_multiplier=1).then_inc(s["ident"], 1)

        @block.scalar
        def _(act):
            act.wait_ge(s["weights"], NW * 16)
            with act.Fori(0, B) as b:
                for j in range(3):
                    n = HW[j]
                    act.wait_ge(s["se1"], b * 3 + j + 1)
                    act.activation(mean_y[:, 0:n], p_se[:, 0:n], ACT.Identity, bias=b2s[:, 0:1],
                                   scale=1.0 / AREA[j]).then_inc(s["mean"], 1)
                    act.wait_ge(s["se2"], b * 3 + j + 1)
                    act.activation(hidden[:, 0:n], p_se[0:8, 128:128 + n], ACT.Relu).then_inc(s["hidden"], 1)
                    act.wait_ge(s["se3"], b * 3 + j + 1)
                    act.wait_ge(s["scaled"], b * NGR)
                    act.activation(gain[j][:, :], p_se[:, 256:256 + n], ACT.Sigmoid).then_inc(s["gain"], 1)

        @block.vector
        def _(dve):
            dve.wait_ge(s["weights"], NW * 16)
            dve.wait_ge(s["ident"], 1)
            for t in range(9):
                dve.tensor_scalar(dw[:, t, :], ident[:, :], wp[:, t:t + 1], None, ALU.mult).then_inc(s["dw"], 1)
            with dve.Fori(0, B) as b:
                for j in range(3):
                    dve.wait_ge(s[f"u{j}"], (b + 1) * 32)
                    if j >= 2:
                        dve.wait_ge(s["se1"], b * 3 + j - 1)
                    else:
                        dve.wait_ge(s["se1"], b * 3)
                    dve.tensor_reduce(total[:, j % 2, 0:HW[j]], u[j][:, :, :], AX.X, ALU.add).then_inc(s["total"], 1)
                for n, (j, g) in enumerate(groups):
                    wins = slice(g * GW[j], (g + 1) * GW[j])
                    size = GW[j] * AREA[j]
                    k = b * NGR + n + 1
                    sc = scaled[:, n % 2, 0:size].rearrange("p (w a) -> p w a", a=AREA[j])
                    py = p_y[:, n % NB, 0:size].rearrange("p (w a) -> p w a", a=AREA[j])
                    pd = p_d[:, n % NB, 0:size].rearrange("p (w a) -> p w a", a=AREA[j])
                    if g == 0:
                        dve.wait_ge(s["gain"], b * 3 + j + 1)
                    dve.wait_ge(s["mm"], k)
                    dve.wait_ge(s["att"], freed(b, n, 2, 1, NGR))
                    dve.scalar_tensor_tensor(sc, py, b2s[:, 0:1],
                                             gain[j][:, wins, None].broadcast_to([128, GW[j], AREA[j]]),
                                             ALU.add, ALU.mult).then_inc(s["scaled"], 1)
                    dve.wait_ge(s["scaled"], k)
                    dve.scalar_tensor_tensor(u[j][:, wins, :], pd, bps[:, 0:1], sc, ALU.add,
                                             ALU.add).then_inc(s["att"], 1)

        @block.tensor
        def _(pe):
            pe.wait_ge(s["weights"], NW * 16)
            pe.wait_ge(s["dw"], 9)
            taps = sorted(((dy, dx) for dy in (-1, 0, 1) for dx in (-1, 0, 1)), key=lambda t: t != (0, 0))

            def squeeze(b, j):
                n = HW[j]
                k = b * 3 + j
                pe.wait_ge(s["total"], k + 1)
                pe.wait_ge(s["gain"], k)
                pe.matmul(p_se[:, 0:n], w2[:, :], total[:, j % 2, 0:n], start=True, stop=True).then_inc(s["se1"], 1)
                pe.wait_ge(s["mean"], k + 1)
                pe.matmul(p_se[0:8, 128:128 + n], se1[:, :], mean_y[:, 0:n], start=True, stop=True).then_inc(s["se2"], 1)
                pe.wait_ge(s["hidden"], k + 1)
                pe.matmul(p_se[:, 256:256 + n], se2[:, :], hidden[:, 0:n], start=True, stop=True).then_inc(s["se3"], 1)

            with pe.Fori(0, B) as b:
                for n, (j, g) in enumerate(groups):
                    if g == 0:
                        squeeze(b, j)
                        pe.wait_ge(s[f"u{j}"], (b + 1) * 32)
                    k = SIDE[j]
                    size = GW[j] * AREA[j]
                    wins = slice(g * GW[j], (g + 1) * GW[j])
                    pe.wait_ge(s["att"], freed(b, n, NB, 1, NGR))
                    pe.matmul(p_y[:, n % NB, 0:size], w2[:, :], u[j][:, wins, :], start=True, stop=True)
                    src = u[j][:, wins, :].rearrange("p w (y x) -> p w y x", x=k)
                    dst = p_d[:, n % NB, 0:size].rearrange("p (w y x) -> p w y x", y=k, x=k)
                    for t, (dy, dx) in enumerate(taps):
                        y0, y1, x0, x1 = max(0, -dy), k - max(0, dy), max(0, -dx), k - max(0, dx)
                        mm = pe.matmul(dst[:, :, y0:y1, x0:x1], dw[:, (dy + 1) * 3 + dx + 1, :],
                                       src[:, :, y0 + dy:y1 + dy, x0 + dx:x1 + dx], start=(t == 0), stop=(t == 8))
                    mm.then_inc(s["mm"], 1)

    nc.clear_and_free_semaphores(list(s.values()))
    nc.all_engine_barrier()


def windows_fold(nc, sem, x1_d, w3t, b3, att_d, x2_d):
    with ExitStack() as ctx:
        def sb(name, shape, dt=FP32):
            return ctx.enter_context(nc.sbuf_tensor("f_" + name, shape, dt))

        w = sb("w", [CB, 3, C])
        bias = sb("bias", [CH, 2])
        xt = sb("xt", [CB, 3, L])
        flat = [sb(f"flat{j}", [CB, FLAT[j]]) for j in range(3)]
        fold = sb("fold", [CB, L])
        out = sb("out", [CH, 2, 2, TT])
        p = ctx.enter_context(nc.psum_tensor("f_p", [CH, 4, TT], FP32))
        s = {k: sem("f_" + k) for k in ("weights", "x", "in0", "in1", "in2", "clear", "add0", "add1", "add2", "half",
                                        "x_done", "mm", "out", "st0", "st1", "sp_go")}
        block = ctx.enter_context(nc.Block())
        x_v = x1_d.rearrange("b (g p) t -> b p g t", g=3)
        o_v = x2_d.rearrange("b (h p) t -> b p h t", h=2)
        n2, k2, st2 = WINDOWS[2], SIDE[2], STEP[2]
        OVER = k2 - st2
        N_ADD2 = 2 * k2

        def view(img, flat_j, j, i, c0, c1):
            n, k, st = WINDOWS[j], SIDE[j], STEP[j]
            im = bass.AP(img.tensor, img.offset + i * IMG + c0, [img.ap[0], [st * IMG, n], [1, c1 - c0], [st, n]])
            fl = bass.AP(flat_j.tensor, flat_j.offset + (i * k + c0) * n * n,
                         [flat_j.ap[0], [n, n], [n * n, c1 - c0], [1, n]])
            return im, fl

        @block.sync
        def _(sp):
            sp.dma_start(w[:, :, :], w3t.rearrange("(g p) n -> p g n", g=3)).then_inc(s["weights"], 16)
            sp.dma_start(bias[:, :], b3.rearrange("(h p) -> p h", h=2), allow_slow_non_contiguous=True).then_inc(s["weights"], 16)
            with sp.Fori(0, B) as b:
                hold(sp, s["sp_go"], s["mm"], b * (NT * 2))
                sp.dma_start(xt[:, :, :], x_v[bass.ds(b, 1), :, :, :].rearrange("a p g t -> (a p) g t")).then_inc(s["x"], 16)
                for j in (2, 0, 1):
                    hold(sp, s["sp_go"], s[f"add{j}"], b * (N_ADD2 if j == 2 else SIDE[j]))
                    sp.dma_start(flat[j][:, :], att_d[j][bass.ds(b, 1), :].rearrange("a (c f) -> (a c) f", c=CB)).then_inc(s[f"in{j}"], 16)
                for t in range(NT):
                    hold(sp, s["sp_go"], s["out"], b * (NT * 2) + (t + 1) * 2)
                    sp.dma_start(o_v[bass.ds(b, 1), :, :, t * TT:(t + 1) * TT].rearrange("a p h t -> (a p) h t"),
                                 out[:, t % 2, :, :]).then_inc(s[f"st{t % 2}"], 16)
            for i in range(2):
                hold(sp, s["sp_go"], s[f"st{i}"], B * NT // 2 * 16)

        @block.gpsimd
        def _(pool):
            with pool.Fori(0, B) as b:
                pool.wait_ge(s["x"], (b + 1) * 16)
                pool.wait_ge(s["in0"], (b + 1) * 16)
                for i in range(SIDE[0]):
                    im, fl = view(xt[:, 0, :], flat[0][:, :], 0, i, 0, SIDE[0])
                    pool.tensor_tensor(im, im, fl, ALU.add).then_inc(s["add0"], 1)

        @block.vector
        def _(dve):
            with dve.Fori(0, B) as b:
                dve.memset(fold[:, :], 0.0).then_inc(s["clear"], 1)
                dve.wait_ge(s["clear"], b + 1)
                dve.wait_ge(s["in2"], (b + 1) * 16)
                a = 0
                for c0, c1 in ((0, st2), (st2, k2)):
                    for i in range(k2):
                        im, fl = view(fold[:, :], flat[2][:, :], 2, i, c0, c1)
                        if i == st2 or (i == 0 and c0):
                            dve.wait_ge(s["add2"], b * N_ADD2 + a)
                        dve.tensor_tensor(im, im, fl, ALU.add).then_inc(s["add2"], 1)
                        a += 1
                dve.wait_ge(s["add2"], b * N_ADD2 + a)
                f0 = fold[:, :]
                for i, dims in enumerate(([[st2 * IMG, n2 - 1], [1, OVER * IMG]],
                                          [[IMG, IMG], [st2, n2 - 1], [1, OVER]])):
                    v = bass.AP(f0.tensor, f0.offset + (st2 * IMG if i == 0 else st2), [f0.ap[0]] + dims)
                    dve.tensor_scalar(v, v, 0.5, None, ALU.mult).then_inc(s["half"], 1)
                    dve.wait_ge(s["half"], 2 * b + i + 1)
                dve.wait_ge(s["x"], (b + 1) * 16)
                dve.tensor_tensor(xt[:, 2, :], xt[:, 2, :], fold[:, :], ALU.add).then_inc(s["x_done"], 1)
                dve.wait_ge(s["in1"], (b + 1) * 16)
                for i in range(SIDE[1]):
                    im, fl = view(xt[:, 1, :], flat[1][:, :], 1, i, 0, SIDE[1])
                    dve.tensor_tensor(im, im, fl, ALU.add).then_inc(s["add1"], 1)
                dve.wait_ge(s["x_done"], b + 1)

        @block.tensor
        def _(pe):
            pe.wait_ge(s["weights"], 32)
            with pe.Fori(0, B) as b:
                pe.wait_ge(s["add0"], (b + 1) * SIDE[0])
                pe.wait_ge(s["x_done"], b + 1)
                pe.wait_ge(s["add1"], (b + 1) * SIDE[1])
                for t in range(NT):
                    for m in range(2):
                        n = 2 * t + m
                        pe.wait_ge(s["out"], freed(b, n, 4, 1, NT * 2))
                        for g in range(3):
                            mm = pe.matmul(p[:, n % 4, :], w[:, g, m * CH:(m + 1) * CH], xt[:, g, t * TT:(t + 1) * TT],
                                           start=(g == 0), stop=(g == 2))
                        mm.then_inc(s["mm"], 1)

        @block.scalar
        def _(act):
            act.wait_ge(s["weights"], 32)
            with act.Fori(0, B) as b:
                for n in range(2 * NT):
                    t, m = n // 2, n % 2
                    act.wait_ge(s["mm"], b * (NT * 2) + n + 1)
                    if m == 0:
                        act.wait_ge(s[f"st{t % 2}"], b * (NT // 2 * 16) + t // 2 * 16)
                    act.activation(out[:, t % 2, m, :], p[:, n % 4, :], ACT.Identity,
                                   bias=bias[:, m:m + 1]).then_inc(s["out"], 1)

    nc.clear_and_free_semaphores(list(s.values()))
    nc.all_engine_barrier()


def attention(nc, sem, tag, x_in, w_query, w_key, w_value, w_out, biases, rowmax_d, out_d):
    gated = biases is None
    D = w_query.shape[1]
    G = 4 if gated else 1
    DP = 32 if gated else 128
    ROWS = 128 if gated else D
    VC = 32 if gated else D + 1
    VS = 32 if gated else 128
    OC = 128 if gated else D + 1
    SCALE = 1.0 if gated else float(D) ** -0.5
    KB = L // 128
    PAIR = 2 * TT
    NSLOT = 3
    UNITS = KB // 2
    NP = 4
    LAG = 2
    VB = PAIR // VS

    order = [("qk", t, 0) for t in range(NT)]
    order += [("v", i, 0) for i in range(KB // VB)]
    order += [("max", i, h) for i in range(KB) for h in range(L // PAIR)]
    for n in range(NT * UNITS + LAG + 2):
        if n < NT * UNITS:
            order.append(("s", n // UNITS, n % UNITS))
        m = n - LAG - 1
        if m >= 0 and m % UNITS == UNITS - 1:
            order.append(("o", m // UNITS, 0))
    reader = ["act" if what in ("qk", "s") else "dve" for what, _, _ in order]
    U = len(order)
    at = {key: n for n, key in enumerate(order)}
    reads = {r: reader.count(r) for r in ("act", "dve")}

    with ExitStack() as ctx:
        def sb(name, shape, dt=FP32):
            return ctx.enter_context(nc.sbuf_tensor(tag + name, shape, dt))

        ident = sb("ident", [128, 128])
        wq = sb("wq", [CH, 2, ROWS])
        wk = sb("wk", [CH, 2, ROWS])
        wv = sb("wv", [CH, 2, D])
        wo = sb("wo", [OC, C])
        den_sel = sb("den_sel", [OC, CH])
        bias_q = sb("bias_q", [ROWS, 1])
        bias_k = sb("bias_k", [ROWS, 1])
        bias_v = sb("bias_v", [D, 1])
        bias_d = sb("bias_d", [CH, 2])
        bias_o = sb("bias_o", [CH, 2])
        x = sb("x", [CH, 2, 2, L])
        qa = sb("qa", [128, L])
        ka = sb("ka", [128, L])
        va = sb("va", [128, KB, VS])
        part_max = sb("part_max", [128, KB, L // PAIR])
        neg_max = sb("neg_max", [128, KB])
        max_t = sb("max_t", [KB, 128])
        prob = sb("prob", [128, NP, PAIR])
        o_sb = sb("o_sb", [OC, 2, TT])
        recip = sb("recip", [CH, TT])
        normed = sb("normed", [CH, 2, 2, TT])
        out = sb("out", [CH, 2, 2, TT])
        p_s = ctx.enter_context(nc.psum_tensor(tag + "p_s", [128, NSLOT, PAIR], FP32))
        p_o = ctx.enter_context(nc.psum_tensor(tag + "p_o", [128, TT], FP32))
        p_m = ctx.enter_context(nc.psum_tensor(tag + "p_m", [128, TT], FP32))
        s = {k: sem(tag + k) for k in (
            "made", "ident", "weights", "bias_mm", "bias", "x0", "x1", "filled", "act", "dve", "part", "max",
            "max_mm", "max_t", "max_st", "max_row", "weighed", "o_sb", "den", "recip", "normed", "gate", "out",
            "st0", "st1", "sp_go", "pe_go")}
        block = ctx.enter_context(nc.Block())
        x_v = x_in.rearrange("b (h p) t -> b p h t", h=2)
        o_v = out_d.rearrange("b (h p) t -> b p h t", h=2)

        def rows(g, extra):
            return slice(DP * (g % G), DP * (g % G) + D + extra)

        def filled(eng, b, key):
            eng.wait_ge(s["filled"], b * U + at[key] + 1)

        def slot(key):
            return p_s[:, at[key] % NSLOT, :]

        loads = []
        for g in range(G):
            c = slice(DP * g, DP * g + D) if gated else slice(0, D)
            loads.append((wq[:, :, c], w_query.rearrange("(h p) n -> p h n", h=2)))
            loads.append((wk[:, :, c], w_key.rearrange("(h p) n -> p h n", h=2)))
            loads.append((wo[DP * g:DP * g + D, :], w_out))
        loads.append((wv[:, :, :], w_value.rearrange("(h p) n -> p h n", h=2)))
        if not gated:
            b_q, b_k, b_v, b_o = biases
            for dst, src in ((bias_q, b_q), (bias_k, b_k), (bias_v, b_v)):
                loads.append((dst[:, :], src.rearrange("(p a) -> p a", a=1)))
        NL = len(loads) + (0 if gated else 1)
        n_made = 9

        @block.sync
        def _(sp):
            hold(sp, s["sp_go"], s["made"], n_made)
            for dst, src in loads:
                sp.dma_start(dst, src).then_inc(s["weights"], 16)
            if not gated:
                sp.dma_start(bias_d[:, :], b_o.rearrange("(h p) -> p h", h=2),
                             allow_slow_non_contiguous=True).then_inc(s["weights"], 16)
            with sp.Fori(0, B // 2) as bb:
                for par in range(2):
                    b = bb * 2 + par
                    hold(sp, s["sp_go"], s["out"], bb * (2 * NT))
                    sp.dma_start(x[:, par, :, :], x_v[bass.ds(b, 1), :, :, :].rearrange("a p h t -> (a p) h t")
                                 ).then_inc(s[f"x{par}"], 16)
                for par in range(2):
                    b = bb * 2 + par
                    hold(sp, s["sp_go"], s["max_t"], b + 1)
                    sp.dma_start(rowmax_d[bass.ds(b, 1), :].rearrange("a (k p) -> (a k) p", p=128),
                                 max_t[:, :]).then_inc(s["max_st"], 16)
                    hold(sp, s["sp_go"], s["max_st"], (b + 1) * 16)
                    for g in range(G):
                        sp.dma_start(qa[DP * g + D:DP * g + D + 1, :], rowmax_d[bass.ds(b, 1), :]
                                     ).then_inc(s["max_row"], 16)
                    for t in range(NT):
                        hold(sp, s["sp_go"], s["out"], b * NT + t + 1)
                        sp.dma_start(o_v[bass.ds(b, 1), :, :, t * TT:(t + 1) * TT].rearrange("a p h t -> (a p) h t"),
                                     out[:, t % 2, :, :]).then_inc(s[f"st{t % 2}"], 16)
            for i in range(2):
                hold(sp, s["sp_go"], s[f"st{i}"], B * NT // 2 * 16)

        @block.gpsimd
        def _(pool):
            for t in (ident, den_sel, wo, bias_q, bias_k):
                pool.memset(t[:, :], 0.0).then_inc(s["made"], 1)
            for t in (wq, wk, va):
                pool.memset(t[:, :, :], 0.0).then_inc(s["made"], 1)
            pool.memset(ka[:, :], 1.0).then_inc(s["made"], 1)
            pool.wait_ge(s["made"], n_made)
            pool.affine_select(out=ident[:, :], in_=ident[:, :], compare_op=ALU.not_equal, fill=1.0, base=0,
                               pattern=[[-1, 128]], channel_multiplier=1).then_inc(s["ident"], 1)
            pool.memset(va[:, :, D:D + 1], 1.0).then_inc(s["ident"], 1)
            n = 2
            for g in range(G):
                pool.affine_select(out=den_sel[:, :], in_=den_sel[:, :], compare_op=ALU.not_equal, fill=1.0,
                                   base=-(DP * g + D), pattern=[[0, CH]], channel_multiplier=1).then_inc(s["ident"], 1)
                n += 1
                pool.wait_ge(s["ident"], n)
            if gated:
                for g in range(G):
                    pool.affine_select(out=bias_k[:, :], in_=bias_k[:, :], compare_op=ALU.not_equal, fill=1.0,
                                       base=-(DP * g + D), pattern=[[0, 1]], channel_multiplier=1
                                       ).then_inc(s["ident"], 1)
                    n += 1
                    pool.wait_ge(s["ident"], n)

        N_ID = 2 + G + (G if gated else 0)

        @block.scalar
        def _(act):
            act.wait_ge(s["ident"], N_ID)
            act.wait_ge(s["weights"], NL * 16)
            if not gated:
                act.wait_ge(s["bias_mm"], 1)
                for m in range(2):
                    act.activation(bias_o[:, m:m + 1], p_m[0:CH, m:m + 1], ACT.Identity,
                                   bias=bias_d[:, m:m + 1]).then_inc(s["bias"], 1)

            def projected(b, t):
                key = ("qk", t, 0)
                filled(act, b, key)
                cols = slice(t * TT, (t + 1) * TT)
                act.activation(qa[0:ROWS, cols], slot(key)[0:ROWS, 0:TT], ACT.Identity, bias=bias_q[:, 0:1]
                               ).then_inc(s["gate"], 1)
                act.activation(ka[0:ROWS, cols], slot(key)[0:ROWS, TT:PAIR], ACT.Identity, bias=bias_k[:, 0:1]
                               ).then_inc(s["act"], 1)

            def weights_of(b, n):
                key = ("s", n // UNITS, n % UNITS)
                filled(act, b, key)
                act.wait_ge(s["weighed"], freed(b, n, NP, 1, NT * UNITS))
                act.activation(prob[:, n % NP, :], slot(key), ACT.Exp, scale=SCALE).then_inc(s["act"], 1)

            def gate_of(b, t):
                act.wait_ge(s["normed"], b * NT + t + 1)
                act.activation(normed[:, t % 2, :, :], normed[:, t % 2, :, :], ACT.Sigmoid).then_inc(s["gate"], 1)

            n_gate = NT + (NT if gated else 0)
            with act.Fori(0, B) as b:
                act.wait_ge(s["weighed"], b * (NT * UNITS))
                for t in range(NT):
                    projected(b, t)
                act.wait_ge(s["max_mm"], b + 1)
                act.wait_ge(s["max_st"], b * 16)
                act.activation(max_t[:, :], p_m[0:KB, 0:128], ACT.Copy).then_inc(s["max_t"], 1)
                for n in range(NT * UNITS + LAG + 1):
                    if n < NT * UNITS:
                        weights_of(b, n)
                    m = n - LAG
                    if m >= 0 and m % UNITS == UNITS - 1:
                        t = m // UNITS
                        act.wait_ge(s["weighed"], b * (NT * UNITS) + m + 1)
                        act.wait_ge(s["den"], freed(b, t, 2, 1, NT))
                        act.activation(o_sb[:, t % 2, :], p_o[0:OC, :], ACT.Copy).then_inc(s["o_sb"], 1)
                    m = n - 10
                    if gated and m >= 0 and m % UNITS == UNITS - 1:
                        gate_of(b, m // UNITS)
                if gated:
                    gate_of(b, NT - 1)

        @block.vector
        def _(dve):
            dve.wait_ge(s["ident"], N_ID)
            dve.wait_ge(s["weights"], NL * 16)
            if not gated:
                dve.wait_ge(s["bias"], 2)
            n_gate = NT + (NT if gated else 0)

            def normalise(b, t):
                key = ("o", t, 0)
                dve.wait_ge(s["den"], b * NT + t + 1)
                dve.wait_ge(s["normed"], b * NT + t)
                dve.reciprocal(recip[:, :], p_m[0:CH, :]).then_inc(s["recip"], 1)
                dve.wait_ge(s["recip"], b * NT + t + 1)
                filled(dve, b, key)
                dve.wait_ge(s["out"], freed(b, t, 2, 1, NT))
                dve.tensor_tensor(normed[:, t % 2, :, :], slot(key)[0:CH, :].rearrange("p (h t) -> p h t", h=2),
                                  recip[:, None, :].broadcast_to([CH, 2, TT]), ALU.mult).then_inc(s["dve"], 1)
                dve.wait_ge(s["dve"], b * reads["dve"] + sum(r == "dve" for r in reader[:at[key] + 1]))
                dve.sem_inc(s["normed"], 1)

            def finish(b, par, t):
                cols = slice(t * TT, (t + 1) * TT)
                dve.wait_ge(s[f"st{t % 2}"], b * (NT // 2 * 16) + t // 2 * 16)
                if gated:
                    dve.wait_ge(s["gate"], b * n_gate + NT + t + 1)
                    dve.scalar_tensor_tensor(out[:, t % 2, :, :], normed[:, t % 2, :, :], 1.0, x[:, par, :, cols],
                                             ALU.add, ALU.mult).then_inc(s["out"], 1)
                else:
                    dve.wait_ge(s["normed"], b * NT + t + 1)
                    for m in range(2):
                        ins = dve.scalar_tensor_tensor(out[:, t % 2, m, :], normed[:, t % 2, m, :], bias_o[:, m:m + 1],
                                                       x[:, par, m, cols], ALU.add, ALU.add)
                        if m:
                            ins.then_inc(s["out"], 1)

            with dve.Fori(0, B // 2) as bb:
                for par in range(2):
                    b = bb * 2 + par
                    dve.wait_ge(s["weighed"], b * (NT * UNITS))
                    for i in range(KB // VB):
                        key = ("v", i, 0)
                        filled(dve, b, key)
                        dve.tensor_copy(va[:, i * VB:(i + 1) * VB, 0:D],
                                        slot(key).rearrange("p (k c) -> p k c", c=VS)[:, :, 0:D]).then_inc(s["dve"], 1)
                    for i in range(KB):
                        for h in range(L // PAIR):
                            key = ("max", i, h)
                            filled(dve, b, key)
                            if i == 0 and h == 0:
                                dve.wait_ge(s["max"], b)
                            dve.tensor_reduce(part_max[:, i, h:h + 1], slot(key), AX.X, ALU.max).then_inc(s["dve"], 1)
                    dve.wait_ge(s["dve"], b * reads["dve"] + KB // VB + KB * (L // PAIR))
                    dve.wait_ge(s["max_mm"], b)
                    dve.tensor_reduce(neg_max[:, :], part_max[:, :, :], AX.X, ALU.max, negate=True).then_inc(s["max"], 1)
                    for t in range(NT + 1):
                        if t < NT:
                            normalise(b, t)
                        if t >= 1:
                            finish(b, par, t - 1)

        @block.tensor
        def _(pe):
            pe.wait_ge(s["ident"], N_ID)
            pe.wait_ge(s["weights"], NL * 16)
            if not gated:
                for m in range(2):
                    mm = pe.matmul(p_m[0:CH, m:m + 1], wo[0:D, m * CH:(m + 1) * CH], bias_v[:, :], start=True, stop=True)
                mm.then_inc(s["bias_mm"], 1)
                pe.wait_ge(s["bias"], 2)

            def claim(b, key):
                n = at[key] - NSLOT
                if n >= 0:
                    r = reader[n]
                    pe.wait_ge(s[r], b * reads[r] + reader[:n + 1].count(r))
                else:
                    pe.wait_ge(s["act"], b * reads["act"])
                    pe.wait_ge(s["dve"], b * reads["dve"])
                pe.sem_inc(s["pe_go"], 1)

            def project(b, par, t):
                key = ("qk", t, 0)
                claim(b, key)
                for i, w in enumerate((wq, wk)):
                    for h in range(2):
                        mm = pe.matmul(slot(key)[0:ROWS, i * TT:(i + 1) * TT], w[:, h, :],
                                       x[:, par, h, t * TT:(t + 1) * TT], start=(h == 0), stop=(h == 1))
                mm.then_inc(s["filled"], 1)

            def project_values(b, par, i):
                key = ("v", i, 0)
                claim(b, key)
                for k in range(VB):
                    kb = i * VB + k
                    for h in range(2):
                        mm = pe.matmul(slot(key)[:, k * VS:k * VS + D], x[:, par, h, kb * 128:(kb + 1) * 128],
                                       wv[:, h, :], start=(h == 0), stop=(h == 1))
                mm.then_inc(s["filled"], 1)

            def scores_for_max(b, i, h):
                key = ("max", i, h)
                claim(b, key)
                for j in range(2):
                    r = rows(2 * h + j, 0)
                    mm = pe.matmul(slot(key)[:, j * TT:(j + 1) * TT], qa[r, i * 128:(i + 1) * 128],
                                   ka[r, h * PAIR + j * TT:h * PAIR + (j + 1) * TT], start=True, stop=True,
                                   tile_position=(r.start, 0))
                mm.then_inc(s["filled"], 1)

            def scores(b, n):
                t, u = n // UNITS, n % UNITS
                key = ("s", t, u)
                claim(b, key)
                for j in range(2):
                    kb = 2 * u + j
                    r = rows(kb, 1)
                    mm = pe.matmul(slot(key)[:, j * TT:(j + 1) * TT], ka[r, kb * 128:(kb + 1) * 128],
                                   qa[r, t * TT:(t + 1) * TT], start=True, stop=True, tile_position=(r.start, 0))
                mm.then_inc(s["filled"], 1)

            def weigh(b, n):
                t, u = n // UNITS, n % UNITS
                key = ("s", t, u)
                pe.wait_ge(s["act"], b * reads["act"] + reader[:at[key] + 1].count("act"))
                if u == 0:
                    pe.wait_ge(s["o_sb"], b * NT + t)
                    pe.sem_inc(s["pe_go"], 1)
                for j in range(2):
                    kb = 2 * u + j
                    o = DP * (kb % G)
                    mm = pe.matmul(p_o[o:o + VC, :], va[:, kb, 0:VC], prob[:, n % NP, j * TT:(j + 1) * TT],
                                   start=(kb < G), stop=(kb >= KB - G), tile_position=(0, o))
                mm.then_inc(s["weighed"], 1)

            def project_out(b, t):
                key = ("o", t, 0)
                pe.wait_ge(s["o_sb"], b * NT + t + 1)
                pe.wait_ge(s["recip"], b * NT + t)
                if t == 0:
                    pe.wait_ge(s["max_t"], b + 1)
                claim(b, key)
                pe.matmul(p_m[0:CH, :], den_sel[:, :], o_sb[:, t % 2, :], start=True, stop=True).then_inc(s["den"], 1)
                for m in range(2):
                    mm = pe.matmul(slot(key)[0:CH, m * TT:(m + 1) * TT], wo[:, m * CH:(m + 1) * CH], o_sb[:, t % 2, :],
                                   start=True, stop=True)
                mm.then_inc(s["filled"], 1)

            with pe.Fori(0, B // 2) as bb:
                for par in range(2):
                    b = bb * 2 + par
                    pe.wait_ge(s[f"x{par}"], (bb + 1) * 16)
                    for t in range(NT):
                        project(b, par, t)
                    for i in range(KB // VB):
                        project_values(b, par, i)
                    for i in range(KB):
                        for h in range(L // PAIR):
                            scores_for_max(b, i, h)
                    pe.wait_ge(s["max"], b + 1)
                    pe.wait_ge(s["recip"], b * NT)
                    pe.sem_inc(s["pe_go"], 1)
                    pe.transpose(p_m[0:KB, 0:128], neg_max[:, :], ident[:, :]).then_inc(s["max_mm"], 1)
                    pe.wait_ge(s["max_row"], (b + 1) * 16 * G)
                    pe.sem_inc(s["pe_go"], 1)
                    for n in range(NT * UNITS + LAG + 2):
                        if n < NT * UNITS:
                            scores(b, n)
                        if n >= LAG and n - LAG < NT * UNITS:
                            weigh(b, n - LAG)
                        m = n - LAG - 1
                        if m >= 0 and m % UNITS == UNITS - 1:
                            project_out(b, m // UNITS)

    nc.clear_and_free_semaphores(list(s.values()))
    nc.all_engine_barrier()


def four_layers(nc, x, v, out):
    def sem(name):
        return nc.alloc_semaphore(name=name)

    def scratch(name, shape, dt=FP32):
        return nc.dram_tensor(name, shape, dt, kind="Internal").ap()

    dt_d, dtx_d, xs_d, y_d = (scratch(n + "_scratch", (SEQ, NC, 128, EB, CK)) for n in ("dt", "dtx", "xs", "y"))
    bc_d = scratch("bc_scratch", (SEQ, NC, 96, CK), BF16)
    gate_d = scratch("gate_scratch", (B, NT, 128, EB, TT))
    x1_d, x2_d, x3_d = (scratch(f"x{n}_scratch", (B, C, L)) for n in (1, 2, 3))
    pat_d = [scratch(f"windows{j}_scratch", (B, CB * FLAT[j])) for j in range(3)]
    att_d = [scratch(f"attended{j}_scratch", (B, CB * FLAT[j])) for j in range(3)]
    max2_d, max3_d = (scratch(f"max{n}_scratch", (B, L)) for n in (2, 3))

    mamba_inputs(nc, sem, x, v["gamma"], v["beta"], v["w_in"], v["conv_w"], v["conv_b"], v["w_xproj"], v["w_dt"],
                 v["b_dt"], dt_d, dtx_d, xs_d, bc_d, gate_d)
    selective_scan(nc, sem, v["a_log"], v["d"], dt_d, dtx_d, xs_d, bc_d, y_d)
    mamba_output(nc, sem, x, v["w_out"], y_d, gate_d, x1_d)
    windows_cut(nc, sem, x1_d, v["w1t"], v["b1"], pat_d)
    windows_attend(nc, sem, v["w2t"], v["b2"], v["wpos"], v["bpos"], v["wse1t"], v["wse2t"], pat_d, att_d)
    windows_fold(nc, sem, x1_d, v["w3t"], v["b3"], att_d, x2_d)
    attention(nc, sem, "g_", x2_d, v["wqt"], v["wkt"], v["wvt"], v["wot"], None, max2_d, x3_d)
    n = v["wtt"].shape[1] // 3
    attention(nc, sem, "h_", x3_d, v["wtt"][:, 2 * n:], v["wtt"][:, 0:n], v["wtt"][:, n:2 * n], v["wdt"],
              (v["bt"][2 * n:], v["bt"][0:n], v["bt"][n:2 * n], v["bd"]), max3_d, out)


_PLAIN = {"gamma": "L0_conv_gamma", "beta": "L0_conv_beta", "w_in": "L0_conv_W_in", "conv_w": "L0_conv_conv_w",
          "conv_b": "L0_conv_conv_b", "w_xproj": "L0_conv_W_xproj", "w_dt": "L0_conv_W_dt", "b_dt": "L0_conv_b_dt",
          "a_log": "L0_conv_A_log", "d": "L0_conv_D", "w_out": "L0_conv_W_out", "b1": "L1_conv_b1",
          "b2": "L1_conv_b2", "b3": "L1_conv_b3", "bpos": "L1_conv_bpos", "bt": "L3_conv_bt", "bd": "L3_conv_bd"}
_TURNED = {"w1t": "L1_conv_w1", "w2t": "L1_conv_w2", "w3t": "L1_conv_w3", "wse1t": "L1_conv_wse1",
           "wse2t": "L1_conv_wse2", "wqt": "L2_conv_Wq", "wkt": "L2_conv_Wk", "wvt": "L2_conv_Wv",
           "wot": "L2_conv_Wout", "wtt": "L3_conv_Wt", "wdt": "L3_conv_Wd"}


def kernel(**inputs):
    import numpy as _np
    import concourse.bacc as _bacc
    from concourse import mybir as _mybir
    from concourse.bass_utils import run_bass_kernel_spmd as _run

    nc = _bacc.Bacc("TRN2", target_bir_lowering=False, num_devices=1)
    arrays, views = {}, {}

    def put(name, a):
        a = _np.ascontiguousarray(a)
        arrays[f"in_{name}_dram"] = a
        views[name] = nc.dram_tensor(f"in_{name}_dram", a.shape, _mybir.dt.from_np(a.dtype), kind="ExternalInput").ap()

    x = inputs["x"]
    put("x", _np.asarray(x).reshape(x.shape[0], x.shape[1], -1))
    put("wpos", _np.asarray(inputs["L1_conv_wpos"]).reshape(-1, 9))
    for name, key in _PLAIN.items():
        put(name, inputs[key])
    for name, key in _TURNED.items():
        put(name, _np.asarray(inputs[key]).T)
    shape = views["x"].shape
    out = nc.dram_tensor("out_dram", shape, _mybir.dt.float32, kind="ExternalOutput").ap()
    four_layers(nc, views["x"], views, out)
    r = _run(nc, [arrays], core_ids=[0])
    return _np.asarray(r.results[0]["out_dram"]).reshape(x.shape)
```

```python
import concourse.bass as bass
from concourse import mybir
from contextlib import ExitStack

FP32 = mybir.dt.float32
BF16 = mybir.dt.bfloat16
ALU = mybir.AluOpType
ACT = mybir.ActivationFunctionType
AX = mybir.AxisListType

B, C, L = 4, 192, 4096
CH = C // 2
E, EB = 384, 3
NST = 16
RANK = 12
TT = 512
NT = L // TT
CK = 1024
NC = L // CK
SEQ = 2 * B


def freed(b, t, depth, per_tile, tiles):
    base = b * (per_tile * tiles)
    return base + (t - depth + 1) * per_tile if t >= depth else base


def hold(engine, go, semaphore, value):
    engine.wait_ge(semaphore, value)
    engine.sem_inc(go, 1)


def reach(engine, semaphore, b, c, per_tile, n):
    value = c * per_tile + n
    if isinstance(b, int):
        value += b * NT * per_tile
        if value > 0:
            engine.wait_ge(semaphore, value)
    else:
        assert value > 0
        engine.wait_ge(semaphore, b * (NT * per_tile) + value)


def mamba_inputs(nc, sem, x, gamma, beta, w_in, conv_w, conv_b, w_xproj, w_dt, b_dt,
                 dt_d, dtx_d, xs_d, bc_d, gate_d):
    with ExitStack() as ctx:
        def sb(name, shape, dt=FP32):
            return ctx.enter_context(nc.sbuf_tensor("a_" + name, shape, dt))

        def pb(name, shape):
            return ctx.enter_context(nc.psum_tensor("a_" + name, shape, FP32))

        PAD = 3
        ones = sb("ones_mean", [CH, CH])
        eps = sb("eps", [CH, 1])
        w_in_sb = sb("w_in_sb", [CH, 2, 2 * E])
        gam = sb("gam", [CH, 2])
        bet = sb("bet", [CH, 2])
        bias_in = sb("bias_in", [128, 6])
        cw = sb("cw", [128, EB, 4])
        cb = sb("cb", [128, EB])
        bdt = sb("bdt", [128, EB])
        wx = sb("wx", [128, 2, EB, 128])
        wdt = sb("wdt", [128, 2, E])
        XD = 4
        xt = sb("xt", [CH, XD, 2, TT])
        sq = sb("sq", [CH, 2, TT])
        lnv = sb("lnv", [CH, TT])
        rstd = sb("rstd", [CH, TT])
        xr = sb("xr", [128, XD, EB, TT + 2 * PAD])
        gate = sb("gate", [128, EB, TT])
        xs = sb("xs", [128, XD, 2, EB, TT])
        dbl = sb("dbl", [128, TT])
        part = sb("part", [64, 2, 3, TT], BF16)
        rest = sb("rest", [64, 2, TT])
        ev = sb("ev", [128, 2, EB, 2, TT])
        ew = sb("ew", [128, EB, 2, TT])
        dt = sb("dt", [128, 2, 2, EB, TT])
        dtx = sb("dtx", [128, 2, EB, TT])

        p_stat = pb("p_stat", [128, TT])
        p_in = [pb(f"p_in{i}", [128, TT]) for i in range(2)]
        p_dbl = pb("p_dbl", [128, TT])
        p_dt = pb("p_dt", [128, 2, 2, TT])

        s = {k: sem("a_" + k) for k in (
            "weights", "zeroed", "const", "wg", "bias_mm", "bias", "x0", "x1", "x2", "x3", "mean", "centred",
            "squared", "var", "lnv", "rstd", "normed", "proj", "xr", "gate", "halo", "conv_step", "conv",
            "xs", "xproj", "dbl", "part_step", "parts", "dtproj", "absv", "expv", "onep", "lnw",
            "relu", "fix", "sum", "dt", "dtx", "st_xs0", "st_xs1", "st_xs2", "st_xs3", "st_bc0", "st_bc1",
            "st_gate", "st_dt0", "st_dt1", "st_dtx", "sp_go", "pool_go")}

        block = ctx.enter_context(nc.Block())

        def steps(eng, step, drain):
            for T in range(NT):
                step(0, T)
            with eng.Fori(0, B - 1) as b:
                for T in range(NT, 2 * NT):
                    step(b, T)
            for T in range(B * NT, B * NT + drain):
                step(0, T)

        def active(b, c):
            return not isinstance(b, int) or 0 <= c < B * NT

        def split_tile(b, c):
            return b + c // NT, c % NT

        @block.sync
        def _(sp):
            sp.dma_start(w_in_sb[:, :, :], w_in.rearrange("(h p) n -> p h n", h=2)).then_inc(s["weights"], 16)
            sp.dma_start(gam[:, :], gamma.rearrange("(h p) -> p h", h=2), allow_slow_non_contiguous=True).then_inc(s["weights"], 16)
            sp.dma_start(bet[:, :], beta.rearrange("(h p) -> p h", h=2), allow_slow_non_contiguous=True).then_inc(s["weights"], 16)
            sp.dma_start(cw[:, :, :], conv_w.rearrange("(e p) k -> p e k", p=128)).then_inc(s["weights"], 16)
            sp.dma_start(cb[:, :], conv_b.rearrange("(e p) -> p e", p=128), allow_slow_non_contiguous=True).then_inc(s["weights"], 16)
            sp.dma_start(bdt[:, :], b_dt.rearrange("(e p) -> p e", p=128), allow_slow_non_contiguous=True).then_inc(s["weights"], 16)
            hold(sp, s["sp_go"], s["zeroed"], 2)
            wx_v = w_xproj.rearrange("(e p) n -> p e n", p=128)
            for d in range(2):
                sp.dma_start(wx[:, d, :, 32 * d:32 * d + 2 * NST], wx_v[:, :, RANK:]).then_inc(s["weights"], 16)
                sp.dma_start(wx[:, d, :, 64 + 32 * d:64 + 32 * d + RANK], wx_v[:, :, :RANK]).then_inc(s["weights"], 16)
                sp.dma_start(wdt[64 + 32 * d:64 + 32 * d + RANK, d, :], w_dt).then_inc(s["weights"], 16)
            x_v = x.rearrange("b (h p) t -> b p h t", h=2)

            def load(b, c):
                q, j = split_tile(b, c)
                src = x_v[bass.ds(q, 1), :, :, j * TT:(j + 1) * TT].rearrange("a p h t -> (a p) h t")
                reach(sp, s["proj"], b, c - XD, 6, 6)
                sp.sem_inc(s["sp_go"], 1)
                sp.dma_start(xt[:, c % XD, :, :], src).then_inc(s[f"x{c % XD}"], 16)

            def store_pair(b, c, dram, tile, sem_st):
                q, j = split_tile(b, c)
                for d in range(2):
                    jj = j if d == 0 else NT - 1 - j
                    k, h = jj // 2, jj % 2
                    sp.dma_start(dram[bass.ds(q + B * d, 1), k, :, :, h * TT:(h + 1) * TT].rearrange(
                        "a p e t -> (a p) e t"), tile[:, d, :, :]).then_inc(sem_st, 16)

            def step(b, T):
                if active(b, T) and T < B * NT:
                    load(b, T)
                c = T - 5
                if active(b, c):
                    reach(sp, s["xs"], b, c, EB, EB)
                    sp.sem_inc(s["sp_go"], 1)
                    store_pair(b, c, xs_d, xs[:, c % XD], s[f"st_xs{c % XD}"])
                c = T - 6
                if active(b, c):
                    reach(sp, s["parts"], b, c, 1, 1)
                    sp.sem_inc(s["sp_go"], 1)
                    q, j = split_tile(b, c)
                    for d in range(2):
                        jj = j if d == 0 else NT - 1 - j
                        k, h = jj // 2, jj % 2
                        for i in range(3):
                            sp.dma_start(bc_d[bass.ds(q + B * d, 1), k, 32 * i:32 * i + 32, h * TT:(h + 1) * TT
                                              ].rearrange("a p t -> (a p) t"),
                                         part[32 * d:32 * d + 32, c % 2, i, :]).then_inc(s[f"st_bc{c % 2}"], 16)
                c = T - 2
                if active(b, c):
                    reach(sp, s["gate"], b, c, EB, EB)
                    sp.sem_inc(s["sp_go"], 1)
                    q, j = split_tile(b, c)
                    sp.dma_start(gate_d[bass.ds(q, 1), j, :, :, :].rearrange("a p e t -> (a p) e t"),
                                 gate[:, :, :]).then_inc(s["st_gate"], 16)
                c = T - 7
                if active(b, c):
                    reach(sp, s["dt"], b, c, EB, EB)
                    sp.sem_inc(s["sp_go"], 1)
                    store_pair(b, c, dt_d, dt[:, c % 2], s[f"st_dt{c % 2}"])
                    reach(sp, s["dtx"], b, c, EB, EB)
                    sp.sem_inc(s["sp_go"], 1)
                    store_pair(b, c, dtx_d, dtx, s["st_dtx"])

            steps(sp, step, 7)
            for i in range(XD):
                sp.wait_ge(s[f"st_xs{i}"], B * NT // XD * 32)
            for i in range(2):
                sp.wait_ge(s[f"st_bc{i}"], B * NT // 2 * 96)
                sp.wait_ge(s[f"st_dt{i}"], B * NT // 2 * 32)
            sp.wait_ge(s["st_gate"], B * NT * 16)
            sp.wait_ge(s["st_dtx"], B * NT * 32)

        def stored(eng, name, b, c, depth, each):
            n = c // depth * each
            if not isinstance(b, int):
                eng.wait_ge(s[name], b * (NT // depth * each) + n)
            elif n > 0:
                eng.wait_ge(s[name], n)

        @block.gpsimd
        def _(pool):
            pool.memset(wx[:, :, :, :], 0.0).then_inc(s["zeroed"], 1)
            pool.memset(wdt[:, :, :], 0.0).then_inc(s["zeroed"], 1)
            pool.memset(ones[:, :], 1.0 / C).then_inc(s["const"], 1)
            pool.memset(eps[:, :], 1e-5).then_inc(s["const"], 1)

            def edges(b, c):
                first = c % NT == 0
                if c > 0:
                    reach(pool, s["conv"], b, c - XD, 6, 0)
                    if c < B * NT:
                        reach(pool, s["xr"], b, c, EB, EB)
                    pool.sem_inc(s["pool_go"], 1)
                    behind = xr[:, (c - 1) % XD, :, PAD + TT:]
                    if first:
                        pool.memset(behind, 0.0).then_inc(s["halo"], 1)
                    else:
                        pool.tensor_scalar(behind, xr[:, c % XD, :, PAD:2 * PAD], 1.0, 0.0, ALU.mult, ALU.add
                                           ).then_inc(s["halo"], 1)
                else:
                    pool.sem_inc(s["halo"], 1)
                if c < B * NT:
                    reach(pool, s["conv"], b, c - XD + 1, 6, 0)
                    pool.sem_inc(s["pool_go"], 1)
                    before = xr[:, c % XD, :, 0:PAD]
                    if first:
                        pool.memset(before, 0.0).then_inc(s["halo"], 1)
                    else:
                        pool.tensor_scalar(before, xr[:, (c - 1) % XD, :, TT:PAD + TT], 1.0, 0.0, ALU.mult, ALU.add
                                           ).then_inc(s["halo"], 1)
                else:
                    pool.sem_inc(s["halo"], 1)

            def split_bc(b, c):
                reach(pool, s["dbl"], b, c, 1, 1)
                stored(pool, f"st_bc{c % 2}", b, c, 2, 96)
                bc = dbl[0:64, :]
                hi, mid, lo = (part[:, c % 2, k, :] for k in range(3))
                r1, r2 = rest[:, 0, :], rest[:, 1, :]
                pool.sem_inc(s["pool_go"], 1)
                pool.tensor_scalar(hi, bc, 1.0, 0.0, ALU.mult, ALU.add).then_inc(s["part_step"], 1)
                reach(pool, s["part_step"], b, c, 4, 1)
                pool.tensor_tensor(r1, bc, hi, ALU.subtract).then_inc(s["part_step"], 1)
                reach(pool, s["part_step"], b, c, 4, 2)
                pool.sem_inc(s["pool_go"], 1)
                pool.tensor_scalar(mid, r1, 1.0, 0.0, ALU.mult, ALU.add).then_inc(s["part_step"], 1)
                reach(pool, s["part_step"], b, c, 4, 3)
                reach(pool, s["parts"], b, c, 1, 0)
                pool.tensor_tensor(r2, r1, mid, ALU.subtract).then_inc(s["part_step"], 1)
                reach(pool, s["part_step"], b, c, 4, 4)
                pool.sem_inc(s["pool_go"], 1)
                pool.tensor_scalar(lo, r2, 1.0, 0.0, ALU.mult, ALU.add).then_inc(s["parts"], 1)

            def step(b, T):
                c = T - 2
                if active(b, c) or c == B * NT:
                    edges(b, c)
                c = T - 5
                if active(b, c):
                    split_bc(b, c)
                c = T - 6
                if active(b, c):
                    for e in range(EB):
                        reach(pool, s["lnw"], b, c, EB, e + 1)
                        pool.tensor_tensor(ew[:, e], ew[:, e], ev[:, c % 2, e], ALU.subtract).then_inc(s["sum"], 1)
                        reach(pool, s["sum"], b, c, EB, e + 1)
                        pool.tensor_tensor(dt[:, c % 2, :, e, :], ew[:, e], dt[:, c % 2, :, e, :], ALU.add
                                           ).then_inc(s["dt"], 1)
                c = T - 5
                if active(b, c):
                    for e in range(EB):
                        reach(pool, s["expv"], b, c, EB, e + 1)
                        reach(pool, s["dt"], b, c - 1, EB, e + 1)
                        pool.sem_inc(s["pool_go"], 1)
                        pool.tensor_scalar(ew[:, e], ev[:, c % 2, e], 1.0, 1.0, ALU.mult, ALU.add
                                           ).then_inc(s["onep"], 1)

            steps(pool, step, 6)

        @block.scalar
        def _(act):
            act.wait_ge(s["bias_mm"], 1)
            act.wait_ge(s["const"], 2)
            act.activation(bias_in[:, :], p_dbl[:, 0:6], ACT.Identity).then_inc(s["bias"], 1)
            act.wait_ge(s["bias"], 1)

            def project(b, c, m):
                reach(act, s["proj"], b, c, 6, m + 1)
                if m < EB:
                    reach(act, s["conv"], b, c - XD + 1, 6, 0)
                    act.activation(xr[:, c % XD, m, PAD:PAD + TT], p_in[m % 2][:, :], ACT.Identity,
                                   bias=bias_in[:, m:m + 1]).then_inc(s["xr"], 1)
                else:
                    if m == EB:
                        stored(act, "st_gate", b, c, 1, 16)
                    act.activation(gate[:, m - EB, :], p_in[m % 2][:, :], ACT.Silu,
                                   bias=bias_in[:, m:m + 1]).then_inc(s["gate"], 1)

            def step(b, T):
                c = T - 1
                if active(b, c):
                    reach(act, s["var"], b, c, 1, 1)
                    reach(act, s["rstd"], b, c, 1, 0)
                    act.activation(lnv[:, :], p_stat[0:CH, :], ACT.Ln, bias=eps[:, 0:1]).then_inc(s["lnv"], 1)
                c = T - 6
                if active(b, c):
                    for e in range(EB):
                        reach(act, s["fix"], b, c, EB, e + 1)
                        act.activation(ew[:, e], ew[:, e], ACT.Ln).then_inc(s["lnw"], 1)
                c = T - 1
                if active(b, c):
                    reach(act, s["lnv"], b, c, 1, 1)
                    reach(act, s["normed"], b, c, 1, 0)
                    act.activation(rstd[:, :], lnv[:, :], ACT.Exp, scale=-0.5).then_inc(s["rstd"], 1)
                c = T - 5
                if active(b, c):
                    for e in range(EB):
                        i = (EB * c + e) % 2
                        reach(act, s["dtproj"], b, c, EB, e + 1)
                        reach(act, s["sum"], b, c - 2, EB, e + 1)
                        act.activation(ev[:, c % 2, e], p_dt[:, i], ACT.Abs, bias=bdt[:, e:e + 1]).then_inc(s["absv"], 1)
                        if e == 0:
                            stored(act, f"st_dt{c % 2}", b, c, 2, 32)
                        act.activation(dt[:, c % 2, :, e, :], p_dt[:, i], ACT.Relu, bias=bdt[:, e:e + 1]
                                       ).then_inc(s["relu"], 1)
                    for e in range(EB):
                        reach(act, s["absv"], b, c, EB, e + 1)
                        act.activation(ev[:, c % 2, e], ev[:, c % 2, e], ACT.Exp, scale=-1.0).then_inc(s["expv"], 1)
                c = T
                if active(b, c):
                    reach(act, s["centred"], b, c, 1, 1)
                    reach(act, s["var"], b, c, 1, 0)
                    act.activation(sq[:, :, :], xt[:, c % XD], ACT.Square).then_inc(s["squared"], 1)
                c = T - 4
                if active(b, c):
                    for e in range(EB):
                        reach(act, s["conv"], b, c, 6, 2 * e + 2)
                        act.activation(xs[:, c % XD, :, e, :], xs[:, c % XD, :, e, :], ACT.Silu, bias=cb[:, e:e + 1]
                                       ).then_inc(s["xs"], 1)
                c = T - 1
                if active(b, c):
                    for m in range(4):
                        project(b, c, m)
                c = T - 4
                if active(b, c):
                    reach(act, s["xproj"], b, c, 1, 1)
                    reach(act, s["dtproj"], b, c, EB, 0)
                    reach(act, s["part_step"], b, c - 1, 4, 2)
                    act.activation(dbl[:, :], p_dbl[:, :], ACT.Identity).then_inc(s["dbl"], 1)
                c = T - 1
                if active(b, c):
                    for m in range(4, 6):
                        project(b, c, m)

            steps(act, step, 6)

        @block.vector
        def _(dve):
            dve.wait_ge(s["weights"], 12 * 16)
            dve.wait_ge(s["bias_mm"], 1)
            for h in range(2):
                dve.tensor_scalar(w_in_sb[:, h, :], w_in_sb[:, h, :], gam[:, h:h + 1], None, ALU.mult).then_inc(s["wg"], 1)
            dve.wait_ge(s["const"], 2)

            def tap(b, c, w, k):
                e, d = k // 2, k % 2
                if d == 0:
                    src = xr[:, c % XD, e, w:w + TT]
                else:
                    src = xr[:, c % XD, e, 2 * PAD - w:2 * PAD - w + TT][:, ::-1]
                out = xs[:, c % XD, d, e, :]
                wt = cw[:, e, w:w + 1]
                if w == 0:
                    if k == 0:
                        reach(dve, s["halo"], b, c + 1, 2, 2 if c + 1 == B * NT else 1)
                        reach(dve, s["halo"], b, c, 2, 2)
                        stored(dve, f"st_xs{c % XD}", b, c, XD, 32)
                        reach(dve, s["xproj"], b, c - XD, 1, 1)
                        reach(dve, s["dtx"], b, c - XD, EB, EB)
                    dve.tensor_scalar(out, src, wt, None, ALU.mult).then_inc(s["conv_step"], 1)
                else:
                    reach(dve, s["conv_step"], b, c, 18, (w - 1) * 6 + k + 1)
                    ins = dve.scalar_tensor_tensor(out, src, wt, out, ALU.mult, ALU.add)
                    ins.then_inc(s["conv"] if w == 3 else s["conv_step"], 1)

            def step(b, T):
                c = T
                if active(b, c):
                    reach(dve, s["mean"], b, c, 1, 1)
                    dve.tensor_tensor(xt[:, c % XD], xt[:, c % XD], p_stat[0:CH, None, :].broadcast_to([CH, 2, TT]),
                                      ALU.subtract).then_inc(s["centred"], 1)
                for n in range(24):
                    if n == 8 and active(b, T - 1):
                        c = T - 1
                        reach(dve, s["rstd"], b, c, 1, 1)
                        dve.tensor_tensor(xt[:, c % XD], xt[:, c % XD], rstd[:, None, :].broadcast_to([CH, 2, TT]),
                                          ALU.mult).then_inc(s["normed"], 1)
                    if active(b, T - 3):
                        tap(b, T - 3, n // 6, n % 6)
                c = T - 6
                if active(b, c):
                    for e in range(EB):
                        reach(dve, s["dt"], b, c, EB, e + 1)
                        if e == 0:
                            stored(dve, "st_dtx", b, c, 1, 32)
                        dve.tensor_tensor(dtx[:, :, e, :], dt[:, c % 2, :, e, :], xs[:, c % XD, :, e, :], ALU.mult
                                          ).then_inc(s["dtx"], 1)
                c = T - 5
                if active(b, c):
                    for e in range(EB):
                        reach(dve, s["onep"], b, c, EB, e + 1)
                        dve.scalar_tensor_tensor(ev[:, c % 2, e], ew[:, e], 1.0, ev[:, c % 2, e],
                                                 ALU.subtract, ALU.subtract).then_inc(s["fix"], 1)

            steps(dve, step, 6)

        @block.tensor
        def _(pe):
            pe.wait_ge(s["weights"], 12 * 16)
            pe.wait_ge(s["const"], 2)
            for m in range(6):
                for h in range(2):
                    mm = pe.matmul(p_dbl[:, m:m + 1], w_in_sb[:, h, m * 128:(m + 1) * 128], bet[:, h:h + 1],
                                   start=(h == 0), stop=(h == 1))
            mm.then_inc(s["bias_mm"], 1)
            pe.wait_ge(s["bias"], 1)
            pe.wait_ge(s["wg"], 2)

            def statistics(rhs, done):
                for h in range(2):
                    mm = pe.matmul(p_stat[0:CH, :], ones[:, :], rhs[:, h, :], start=(h == 0), stop=(h == 1))
                mm.then_inc(done, 1)

            def project(b, c, blocks):
                for m in blocks:
                    name, cc, n = (("gate", c - 1, 2), ("gate", c - 1, 3), ("xr", c, 1), ("xr", c, 2),
                                   ("xr", c, 3), ("gate", c, 1))[m]
                    reach(pe, s[name], b, cc, EB, n)
                    for h in range(2):
                        mm = pe.matmul(p_in[m % 2][:, :], w_in_sb[:, h, m * 128:(m + 1) * 128],
                                       xt[:, c % XD, h, :], start=(h == 0), stop=(h == 1))
                    mm.then_inc(s["proj"], 1)

            def dt_projection(b, c, blocks):
                for e in blocks:
                    reach(pe, s["relu"], b, c, EB, e - 1)
                    for d in range(2):
                        mm = pe.matmul(p_dt[:, (EB * c + e) % 2, d, :], wdt[:, d, e * 128:(e + 1) * 128], dbl[:, :],
                                       start=True, stop=True)
                    mm.then_inc(s["dtproj"], 1)

            def x_projection(b, c):
                reach(pe, s["dbl"], b, c, 1, 0)
                for e in range(EB):
                    reach(pe, s["xs"], b, c, EB, e + 1)
                    for d in range(2):
                        mm = pe.matmul(p_dbl[:, :], wx[:, d, e, :], xs[:, c % XD, d, e, :],
                                       start=(e == 0 and d == 0), stop=(e == EB - 1 and d == 1))
                mm.then_inc(s["xproj"], 1)

            def step(b, T):
                if active(b, T - 5):
                    reach(pe, s["dbl"], b, T - 5, 1, 1)
                    dt_projection(b, T - 5, (0, 1))
                if active(b, T):
                    pe_x = T // XD * 16 + 16
                    pe.wait_ge(s[f"x{T % XD}"], pe_x if isinstance(b, int) else b * (NT // XD * 16) + pe_x)
                    reach(pe, s["lnv"], b, T, 1, 0)
                    statistics(xt[:, T % XD], s["mean"])
                if active(b, T - 5):
                    dt_projection(b, T - 5, (2,))
                if active(b, T - 1):
                    reach(pe, s["normed"], b, T - 1, 1, 1)
                    project(b, T - 1, (0, 1))
                if active(b, T):
                    reach(pe, s["squared"], b, T, 1, 1)
                    statistics(sq, s["var"])
                if active(b, T - 4):
                    x_projection(b, T - 4)
                if active(b, T - 1):
                    project(b, T - 1, (2, 3, 4, 5))

            steps(pe, step, 6)

    nc.clear_and_free_semaphores(list(s.values()))
    nc.all_engine_barrier()


def selective_scan(nc, sem, a_log, d_skip, dt_d, dtx_d, xs_d, bc_d, y_d):
    with ExitStack() as ctx:
        def sb(name, shape, dt=FP32):
            return ctx.enter_context(nc.sbuf_tensor("b_" + name, shape, dt))

        TPC = NST * EB
        TPS = NC * TPC
        NPS = NC * NST
        ND, NU, NH, NY = 4, 4, 4, 4

        ident = sb("ident", [128, 128])
        diag_d = sb("diag_d", [128, EB, 128])
        sel = sb("sel", [96, 2 * NST, 128], BF16)
        a_neg = sb("a_neg", [128, EB, NST])
        dsk = sb("dsk", [128, EB])
        dt = sb("dt", [128, 2, EB, CK])
        dtx = sb("dtx", [128, 2, EB, CK])
        xs = sb("xs", [128, EB, CK])
        bc = sb("bc", [96, 2, CK], BF16)
        decay = sb("decay", [128, ND, CK])
        inp = sb("inp", [128, NU, CK])
        hid = sb("hid", [128, NH, CK])
        hc = sb("hc", [128, NY, CK])
        b_row = sb("b_row", [128, 4, CK])
        c_row = sb("c_row", [128, 4, CK])
        carry = sb("carry", [128, TPC])
        y_sb = sb("y_sb", [128, EB, CK])
        p_row = ctx.enter_context(nc.psum_tensor("b_p_row", [128, CK], FP32))
        p_y = ctx.enter_context(nc.psum_tensor("b_p_y", [128, EB, CK], FP32))

        s = {k: sem("b_" + k) for k in (
            "a_loaded", "a_exp", "a_neg", "made", "ident", "sel", "diag", "dt0", "dt1", "dtx0", "dtx1", "xs",
            "bc0", "bc1", "spread", "taken", "decay", "input", "scan", "product", "summed", "skip",
            "carried", "y_out", "stored", "sp_go")}

        block = ctx.enter_context(nc.Block())

        def used(q, k, depth, per):
            return freed(q, k, depth, 1, per)

        def one(dram, q, c):
            return dram[bass.ds(q, 1), c, :, :, :].rearrange("a p e t -> (a p) e t")

        def load(sp, q, c):
            sp.dma_start(bc[:, c % 2, :], bc_d[bass.ds(q, 1), c, :, :].rearrange("a p t -> (a p) t")
                         ).then_inc(s[f"bc{c % 2}"], 16)
            sp.dma_start(dt[:, c % 2, :, :], one(dt_d, q, c)).then_inc(s[f"dt{c % 2}"], 16)
            sp.dma_start(dtx[:, c % 2, :, :], one(dtx_d, q, c)).then_inc(s[f"dtx{c % 2}"], 16)

        def load_x(sp, q, c):
            sp.dma_start(xs[:, :, :], one(xs_d, q, c)).then_inc(s["xs"], 16)

        def turn(sp, q, c, last):
            hold(sp, s["sp_go"], s["skip"], q * NC + c + 1)
            if c + 1 < NC:
                load_x(sp, q, c + 1)
            elif not last:
                load_x(sp, q + 1, 0)
            if c + 2 < NC or not last:
                hold(sp, s["sp_go"], s["decay"], q * TPS + (c + 1) * TPC)
                hold(sp, s["sp_go"], s["input"], q * TPS + (c + 1) * TPC)
                hold(sp, s["sp_go"], s["spread"], q * (2 * NPS) + (c + 1) * 2 * NST)
                load(sp, q + (c + 2) // NC, (c + 2) % NC)
            hold(sp, s["sp_go"], s["y_out"], q * (NC * EB) + (c + 1) * EB)
            sp.dma_start(one(y_d, q, c), y_sb[:, :, :]).then_inc(s["stored"], 16)

        @block.sync
        def _(sp):
            sp.dma_start(a_neg[:, :, :], a_log.rearrange("(e p) n -> p e n", p=128)).then_inc(s["a_loaded"], 16)
            sp.dma_start(dsk[:, :], d_skip.rearrange("(e p) -> p e", p=128),
                         allow_slow_non_contiguous=True).then_inc(s["a_loaded"], 16)
            load(sp, 0, 0)
            load_x(sp, 0, 0)
            load(sp, 0, 1)
            with sp.Fori(0, SEQ - 1) as q:
                for c in range(NC):
                    turn(sp, q, c, False)
            for c in range(NC):
                turn(sp, SEQ - 1, c, True)
            hold(sp, s["sp_go"], s["stored"], SEQ * NC * 16)

        @block.gpsimd
        def _(pool):
            pool.memset(ident[:, :], 0.0).then_inc(s["made"], 1)
            pool.memset(sel[:, :, :], 0.0).then_inc(s["made"], 1)
            pool.wait_ge(s["made"], 2)
            pool.affine_select(out=ident[:, :], in_=ident[:, :], compare_op=ALU.not_equal, fill=1.0, base=0,
                               pattern=[[-1, 128]], channel_multiplier=1).then_inc(s["ident"], 1)
            for k in range(3):
                pool.affine_select(out=sel[:, :, :], in_=sel[:, :, :], compare_op=ALU.not_equal, fill=1.0,
                                   base=-32 * k, pattern=[[-1, 2 * NST], [0, 128]],
                                   channel_multiplier=1).then_inc(s["sel"], 1)
                pool.wait_ge(s["sel"], k + 1)
            with pool.Fori(0, SEQ) as q:
                for c in range(NC):
                    for n in range(NST):
                        m = c * NST + n
                        for e in range(EB):
                            k = c * TPC + n * EB + e
                            if k % TPC == 0:
                                pool.wait_ge(s[f"dtx{c % 2}"], q * (NC // 2 * 16) + (c // 2 + 1) * 16)
                            if e == 0:
                                pool.wait_ge(s["taken"], q * (2 * NPS) + 2 * m + 1)
                            pool.wait_ge(s["scan"], used(q, k, NU, TPS))
                            pool.tensor_tensor(inp[:, k % NU, :], dtx[:, c % 2, e, :], b_row[:, m % 4, :],
                                               ALU.mult).then_inc(s["input"], 1)

        @block.scalar
        def _(act):
            act.wait_ge(s["a_loaded"], 32)
            act.activation(a_neg[:, :, :], a_neg[:, :, :], ACT.Exp).then_inc(s["a_exp"], 1)
            act.wait_ge(s["a_exp"], 1)
            act.activation(a_neg[:, :, :], a_neg[:, :, :], ACT.Copy, scale=-1.0).then_inc(s["a_neg"], 1)
            act.wait_ge(s["a_neg"], 1)

            def take(q, m, row):
                act.wait_ge(s["spread"], q * (2 * NPS) + 2 * m + row + 1)
                if row == 0:
                    act.wait_ge(s["input"], freed(q, m, 4, EB, NPS))
                    out = b_row[:, m % 4, :]
                else:
                    act.wait_ge(s["product"], freed(q, m, 4, EB, NPS))
                    out = c_row[:, m % 4, :]
                act.activation(out, p_row[:, :], ACT.Copy).then_inc(s["taken"], 1)

            def keep_state(q, k):
                act.wait_ge(s["scan"], q * TPS + k + 1)
                act.activation(carry[:, k % TPC:k % TPC + 1], hid[:, k % NH, CK - 1:CK],
                               ACT.Copy).then_inc(s["carried"], 1)

            def y_out(q, c):
                act.wait_ge(s["summed"], q * TPS + (c + 1) * TPC)
                act.wait_ge(s["stored"], q * (NC * 16) + c * 16)
                for e in range(EB):
                    act.activation(y_sb[:, e, :], p_y[:, e, :], ACT.Copy).then_inc(s["y_out"], 1)

            with act.Fori(0, SEQ) as q:
                take(q, 0, 0)
                take(q, 0, 1)
                for m in range(NPS):
                    c = m // NST
                    for e in range(EB):
                        k = 3 * m + e
                        if k % TPC == 0:
                            act.wait_ge(s[f"dt{c % 2}"], q * (NC // 2 * 16) + (c // 2 + 1) * 16)
                        act.wait_ge(s["scan"], used(q, k, ND, TPS))
                        n = m % NST
                        act.activation(decay[:, k % ND, :], dt[:, c % 2, e, :], ACT.Exp,
                                       scale=a_neg[:, e, n:n + 1]).then_inc(s["decay"], 1)
                        if k >= 2:
                            keep_state(q, k - 2)
                        if e >= 1 and m + 1 < NPS:
                            take(q, m + 1, e - 1)
                    if m % NST == 0 and m:
                        y_out(q, c - 1)
                keep_state(q, TPS - 2)
                keep_state(q, TPS - 1)
                y_out(q, NC - 1)

        @block.vector
        def _(dve):
            dve.wait_ge(s["a_loaded"], 32)
            dve.wait_ge(s["ident"], 1)
            for e in range(EB):
                dve.tensor_scalar(diag_d[:, e, :], ident[:, :], dsk[:, e:e + 1], None, ALU.mult).then_inc(s["diag"], 1)

            def product(q, k):
                m = k // EB
                dve.wait_ge(s["scan"], q * TPS + k + 1)
                dve.wait_ge(s["taken"], q * (2 * NPS) + 2 * m + 2)
                dve.wait_ge(s["summed"], used(q, k, NY, TPS))
                dve.tensor_tensor(hc[:, k % NY, :], hid[:, k % NH, :], c_row[:, m % 4, :],
                                  ALU.mult).then_inc(s["product"], 1)

            with dve.Fori(0, SEQ) as q:
                for k in range(TPS):
                    c = k // TPC
                    dve.wait_ge(s["decay"], q * TPS + k + 1)
                    dve.wait_ge(s["input"], q * TPS + k + 1)
                    dve.wait_ge(s["carried"], used(q, k, NH, TPS))
                    if k >= NH:
                        dve.wait_ge(s["product"], q * TPS + k - NH + 1)
                    start = 0.0 if c == 0 else carry[:, k % TPC:k % TPC + 1]
                    dve.tensor_tensor_scan(hid[:, k % NH, :], decay[:, k % ND, :], inp[:, k % NU, :], start,
                                           ALU.mult, ALU.add).then_inc(s["scan"], 1)
                    if k >= 1:
                        product(q, k - 1)
                product(q, TPS - 1)

        @block.tensor
        def _(pe):
            pe.wait_ge(s["sel"], 3)
            pe.wait_ge(s["diag"], EB)

            def spread(q, m, row):
                c, n = m // NST, m % NST
                if row == 0 and n == 0:
                    pe.wait_ge(s[f"bc{c % 2}"], q * (NC // 2 * 16) + (c // 2 + 1) * 16)
                pe.wait_ge(s["taken"], q * (2 * NPS) + 2 * m + row)
                for h in range(2):
                    mm = pe.matmul(p_row[:, h * 512:(h + 1) * 512], sel[:, n + NST * row, :],
                                   bc[:, c % 2, h * 512:(h + 1) * 512], start=True, stop=True)
                mm.then_inc(s["spread"], 1)

            def skip(q, c):
                pe.wait_ge(s["xs"], q * (NC * 16) + (c + 1) * 16)
                pe.wait_ge(s["y_out"], q * (NC * EB) + c * EB)
                for e in range(EB):
                    for h in range(2):
                        mm = pe.matmul(p_y[:, e, h * 512:(h + 1) * 512], diag_d[:, e, :],
                                       xs[:, e, h * 512:(h + 1) * 512], start=True, stop=False)
                mm.then_inc(s["skip"], 1)

            def add_state(q, k):
                e, last = k % EB, k % TPC >= TPC - EB
                pe.wait_ge(s["product"], q * TPS + k + 1)
                for h in range(2):
                    mm = pe.matmul(p_y[:, e, h * 512:(h + 1) * 512], ident[:, :],
                                   hc[:, k % NY, h * 512:(h + 1) * 512], start=False, stop=last)
                mm.then_inc(s["summed"], 1)

            with pe.Fori(0, SEQ) as q:
                spread(q, 0, 0)
                spread(q, 0, 1)
                for m in range(NPS + 1):
                    if m + 1 < NPS:
                        spread(q, m + 1, 0)
                    if m >= 1:
                        if (m - 1) % NST == 0:
                            skip(q, (m - 1) // NST)
                        add_state(q, 3 * m - 3)
                    if m + 1 < NPS:
                        spread(q, m + 1, 1)
                    if m >= 1:
                        add_state(q, 3 * m - 2)
                        add_state(q, 3 * m - 1)

    nc.clear_and_free_semaphores(list(s.values()))
    nc.all_engine_barrier()


def mamba_output(nc, sem, x, w_out, y_d, gate_d, x1_d):
    with ExitStack() as ctx:
        def sb(name, shape, dt=FP32):
            return ctx.enter_context(nc.sbuf_tensor("c_" + name, shape, dt))

        W = 2 * TT
        w_sb = sb("w", [128, EB, C])
        yf = sb("yf", [128, 2, EB, W])
        yr = sb("yr", [128, 2, EB, W])
        gt = sb("gt", [128, 2, 2, EB, TT])
        xt = sb("xt", [CH, 2, 2, W])
        out = sb("out", [CH, 2, 2, W])
        p_o = ctx.enter_context(nc.psum_tensor("c_p_o", [128, 2, 2, TT], FP32))
        s = {k: sem("c_" + k) for k in ("weights", "in0", "in1", "both", "gated", "mm", "out", "st0", "st1", "sp_go")}
        block = ctx.enter_context(nc.Block())
        x_v = x.rearrange("b (h p) t -> b p h t", h=2)
        o_v = x1_d.rearrange("b (h p) t -> b p h t", h=2)
        NL = 5

        def store(sp, b, c):
            hold(sp, s["sp_go"], s["out"], b * (NC * 4) + (c + 1) * 4)
            sp.dma_start(o_v[bass.ds(b, 1), :, :, c * W:(c + 1) * W].rearrange("a p h t -> (a p) h t"),
                         out[:, c % 2, :, :]).then_inc(s[f"st{c % 2}"], 16)

        @block.sync
        def _(sp):
            sp.dma_start(w_sb[:, :, :], w_out.rearrange("(e p) n -> p e n", p=128)).then_inc(s["weights"], 16)
            with sp.Fori(0, B) as b:
                for c in range(NC):
                    i = c % 2
                    ld = s[f"in{i}"]
                    hold(sp, s["sp_go"], s["out"], freed(b, c, 2, 4, NC))
                    sp.dma_start(yf[:, i, :, :], y_d[bass.ds(b, 1), c, :, :, :].rearrange("a p e t -> (a p) e t")).then_inc(ld, 16)
                    sp.dma_start(yr[:, i, :, :], y_d[bass.ds(b + B, 1), NC - 1 - c, :, :, :].rearrange("a p e t -> (a p) e t")).then_inc(ld, 16)
                    for h in range(2):
                        sp.dma_start(gt[:, i, h, :, :], gate_d[bass.ds(b, 1), 2 * c + h, :, :, :].rearrange("a p e t -> (a p) e t")).then_inc(ld, 16)
                    sp.dma_start(xt[:, i, :, :], x_v[bass.ds(b, 1), :, :, c * W:(c + 1) * W].rearrange("a p h t -> (a p) h t")).then_inc(ld, 16)
                    if c >= 1:
                        store(sp, b, c - 1)
                store(sp, b, NC - 1)
            for i in range(2):
                hold(sp, s["sp_go"], s[f"st{i}"], B * NC // 2 * 16)

        @block.vector
        def _(dve):
            def gated(b, c):
                i = c % 2
                dve.wait_ge(s[f"in{i}"], b * (NC // 2 * 16 * NL) + (c // 2 + 1) * 16 * NL)
                dve.tensor_tensor(yf[:, i, :, :], yf[:, i, :, :], yr[:, i, :, ::-1], ALU.add).then_inc(s["both"], 1)
                dve.wait_ge(s["both"], b * NC + c + 1)
                for h in range(2):
                    v = yf[:, i, :, h * TT:(h + 1) * TT]
                    dve.tensor_tensor(v, v, gt[:, i, h, :, :], ALU.mult).then_inc(s["gated"], 1)

            def finish(b, c):
                i = c % 2
                dve.wait_ge(s[f"st{i}"], b * (NC // 2 * 16) + c // 2 * 16)
                for h in range(2):
                    for m in range(2):
                        dve.wait_ge(s["mm"], b * (NC * 4) + c * 4 + 2 * h + m + 1)
                        dve.scalar_tensor_tensor(out[:, i, m, h * TT:(h + 1) * TT], p_o[0:CH, h, m, :], 0.5,
                                                 xt[:, i, m, h * TT:(h + 1) * TT], ALU.mult,
                                                 ALU.add).then_inc(s["out"], 1)

            dve.wait_ge(s["weights"], 16)
            with dve.Fori(0, B) as b:
                for c in range(NC + 1):
                    if c < NC:
                        gated(b, c)
                    if c >= 1:
                        finish(b, c - 1)

        @block.tensor
        def _(pe):
            pe.wait_ge(s["weights"], 16)
            with pe.Fori(0, B) as b:
                for c in range(NC):
                    for h in range(2):
                        pe.wait_ge(s["gated"], b * (NC * 2) + c * 2 + h + 1)
                        for m in range(2):
                            g = c * 4 + 2 * h + m
                            pe.wait_ge(s["out"], freed(b, g, 4, 1, NC * 4))
                            for e in range(EB):
                                mm = pe.matmul(p_o[0:CH, h, m, :], w_sb[:, e, m * CH:(m + 1) * CH],
                                               yf[:, c % 2, e, h * TT:(h + 1) * TT], start=(e == 0), stop=(e == EB - 1))
                            mm.then_inc(s["mm"], 1)

    nc.clear_and_free_semaphores(list(s.values()))
    nc.all_engine_barrier()


CB = 64
WINDOWS = (4, 8, 12)
STEP = tuple(64 // n for n in WINDOWS)
SIDE = tuple(64 // n + 64 % n for n in WINDOWS)
AREA = tuple(k * k for k in SIDE)
NWIN = tuple(n * n for n in WINDOWS)
FLAT = tuple(AREA[j] * NWIN[j] for j in range(3))
IMG = 64


def windows_cut(nc, sem, x1_d, w1t, b1, pat_d):
    with ExitStack() as ctx:
        def sb(name, shape, dt=FP32):
            return ctx.enter_context(nc.sbuf_tensor("d_" + name, shape, dt))

        w = sb("w", [CB, 3, CB])
        bias = sb("bias", [CB, 1])
        xt = sb("xt", [CB, 2, 3, TT])
        xc = sb("xc", [CB, 2, L])
        flat = [sb(f"flat{j}", [CB, FLAT[j]]) for j in range(3)]
        p = ctx.enter_context(nc.psum_tensor("d_p", [CB, 4, TT], FP32))
        s = {k: sem("d_" + k) for k in ("weights", "x0", "x1", "mm", "conv", "cut0", "cut1", "cut2",
                                        "st0", "st1", "st2", "sp_go", "pe_go")}
        block = ctx.enter_context(nc.Block())
        x_v = x1_d.rearrange("b (g p) t -> b p g t", g=3)

        def cutting(eng, copy, b, j, par):
            n, k, st = WINDOWS[j], SIDE[j], STEP[j]
            src0 = xc[:, par, :]
            d0 = flat[j][:, :]
            for i in range(k):
                src = bass.AP(src0.tensor, src0.offset + i * IMG, [src0.ap[0], [st * IMG, n], [1, k], [st, n]])
                dst = bass.AP(d0.tensor, d0.offset + i * k * n * n, [d0.ap[0], [n, n], [n * n, k], [1, n]])
                copy(dst, src).then_inc(s[f"cut{j}"], 1)

        @block.sync
        def _(sp):
            sp.dma_start(w[:, :, :], w1t.rearrange("(g p) n -> p g n", g=3)).then_inc(s["weights"], 16)
            sp.dma_start(bias[:, :], b1.rearrange("(p a) -> p a", a=1)).then_inc(s["weights"], 16)
            with sp.Fori(0, B) as b:
                for t in range(NT):
                    hold(sp, s["sp_go"], s["mm"], freed(b, t, 2, 1, NT))
                    sp.dma_start(xt[:, t % 2, :, :], x_v[bass.ds(b, 1), :, :, t * TT:(t + 1) * TT].rearrange(
                        "a p g t -> (a p) g t")).then_inc(s[f"x{t % 2}"], 16)
                for j in range(3):
                    hold(sp, s["sp_go"], s[f"cut{j}"], (b + 1) * SIDE[j])
                    sp.dma_start(pat_d[j][bass.ds(b, 1), :].rearrange("a (c f) -> (a c) f", c=CB),
                                 flat[j][:, :]).then_inc(s[f"st{j}"], 16)
            for j in range(3):
                hold(sp, s["sp_go"], s[f"st{j}"], B * 16)

        @block.scalar
        def _(act):
            act.wait_ge(s["weights"], 32)
            with act.Fori(0, B // 2) as bb:
                for par in range(2):
                    b = bb * 2 + par
                    for t in range(NT):
                        act.wait_ge(s["mm"], b * NT + t + 1)
                        if t == 0:
                            act.wait_ge(s["cut0"], bb * (2 * SIDE[0]))
                            act.wait_ge(s["cut1"], bb * (2 * SIDE[1]))
                        act.activation(xc[:, par, t * TT:(t + 1) * TT], p[:, t % 4, :], ACT.Identity,
                                       bias=bias[:, 0:1]).then_inc(s["conv"], 1)
                    act.wait_ge(s["conv"], (b + 1) * NT)
                    act.wait_ge(s["st2"], b * 16)
                    cutting(act, lambda o, i: act.activation(o, i, ACT.Copy), b, 2, par)

        @block.vector
        def _(dve):
            with dve.Fori(0, B // 2) as bb:
                for par in range(2):
                    b = bb * 2 + par
                    dve.wait_ge(s["conv"], (b + 1) * NT)
                    for j in range(2):
                        dve.wait_ge(s[f"st{j}"], b * 16)
                        cutting(dve, dve.tensor_copy, b, j, par)

        @block.tensor
        def _(pe):
            pe.wait_ge(s["weights"], 32)
            with pe.Fori(0, B) as b:
                for t in range(NT):
                    pe.wait_ge(s[f"x{t % 2}"], b * (NT // 2 * 16) + (t // 2 + 1) * 16)
                    pe.wait_ge(s["conv"], freed(b, t, 4, 1, NT))
                    pe.sem_inc(s["pe_go"], 1)
                    for g in range(3):
                        mm = pe.matmul(p[:, t % 4, :], w[:, g, :], xt[:, t % 2, g, :], start=(g == 0), stop=(g == 2))
                    mm.then_inc(s["mm"], 1)

    nc.clear_and_free_semaphores(list(s.values()))
    nc.all_engine_barrier()


def windows_attend(nc, sem, w2t, b2, wpos, bpos, wse1t, wse2t, pat_d, att_d):
    with ExitStack() as ctx:
        def sb(name, shape, dt=FP32):
            return ctx.enter_context(nc.sbuf_tensor("e_" + name, shape, dt))

        HW = tuple(n // 2 for n in NWIN)
        GW = tuple(512 // a for a in AREA)
        NG = tuple(HW[j] // GW[j] for j in range(3))
        groups = [(j, g) for j in range(3) for g in range(NG[j])]
        NGR = len(groups)
        ident = sb("ident", [128, 128])
        w2 = sb("w2", [128, 128])
        se1 = sb("se1", [128, 8])
        se2 = sb("se2", [8, 128])
        b2s = sb("b2s", [128, 1])
        bps = sb("bps", [128, 1])
        wp = sb("wp", [128, 9])
        dw = sb("dw", [128, 9, 128])
        u = [sb(f"u{j}", [128, HW[j], AREA[j]]) for j in range(3)]
        scaled = sb("scaled", [128, 2, 512])
        total = sb("total", [128, 2, max(HW)])
        mean_y = sb("mean_y", [128, max(HW)])
        hidden = sb("hidden", [8, max(HW)])
        gain = [sb(f"gain{j}", [128, HW[j]]) for j in range(3)]
        NB = 3
        p_y = ctx.enter_context(nc.psum_tensor("e_p_y", [128, NB, 512], FP32))
        p_d = ctx.enter_context(nc.psum_tensor("e_p_d", [128, NB, 512], FP32))
        p_se = ctx.enter_context(nc.psum_tensor("e_p_se", [128, 512], FP32))
        s = {k: sem("e_" + k) for k in (
            "made", "ident", "weights", "dw", "u0", "u1", "u2", "total", "se1", "mean", "se2", "hidden", "se3",
            "gain", "mm", "scaled", "att", "st0", "st1", "st2", "sp_go")}
        block = ctx.enter_context(nc.Block())
        NW = 12

        def halves(dram, b, j, h):
            v = dram[j].rearrange("b (h w c p) -> b h c w p", h=2, w=HW[j], c=CB)
            return v[bass.ds(b, 1), h, :, :, :].rearrange("a c w p -> (a c) w p")

        @block.sync
        def _(sp):
            hold(sp, s["sp_go"], s["made"], 4)
            for h in range(2):
                r = slice(64 * h, 64 * h + 64)
                sp.dma_start(w2[r, r], w2t).then_inc(s["weights"], 16)
                sp.dma_start(se1[r, 4 * h:4 * h + 4], wse1t).then_inc(s["weights"], 16)
                sp.dma_start(se2[4 * h:4 * h + 4, r], wse2t).then_inc(s["weights"], 16)
                sp.dma_start(b2s[r, :], b2.rearrange("(p a) -> p a", a=1)).then_inc(s["weights"], 16)
                sp.dma_start(bps[r, :], bpos.rearrange("(p a) -> p a", a=1)).then_inc(s["weights"], 16)
                sp.dma_start(wp[r, :], wpos).then_inc(s["weights"], 16)
            with sp.Fori(0, B) as b:
                for j in range(3):
                    hold(sp, s["sp_go"], s[f"st{j}"], b * 32)
                    for h in range(2):
                        sp.dma_start(u[j][64 * h:64 * h + 64, :, :], halves(pat_d, b, j, h)).then_inc(s[f"u{j}"], 16)
                for j in range(3):
                    hold(sp, s["sp_go"], s["att"], b * NGR + sum(NG[:j + 1]))
                    for h in range(2):
                        sp.dma_start(halves(att_d, b, j, h), u[j][64 * h:64 * h + 64, :, :]).then_inc(s[f"st{j}"], 16)
            for j in range(3):
                hold(sp, s["sp_go"], s[f"st{j}"], B * 32)

        @block.gpsimd
        def _(pool):
            for t in (w2, se1, se2, ident):
                pool.memset(t[:, :], 0.0).then_inc(s["made"], 1)
            pool.wait_ge(s["made"], 4)
            pool.affine_select(out=ident[:, :], in_=ident[:, :], compare_op=ALU.not_equal, fill=1.0, base=0,
                               pattern=[[-1, 128]], channel_multiplier=1).then_inc(s["ident"], 1)

        @block.scalar
        def _(act):
            act.wait_ge(s["weights"], NW * 16)
            with act.Fori(0, B) as b:
                for j in range(3):
                    n = HW[j]
                    act.wait_ge(s["se1"], b * 3 + j + 1)
                    act.activation(mean_y[:, 0:n], p_se[:, 0:n], ACT.Identity, bias=b2s[:, 0:1],
                                   scale=1.0 / AREA[j]).then_inc(s["mean"], 1)
                    act.wait_ge(s["se2"], b * 3 + j + 1)
                    act.activation(hidden[:, 0:n], p_se[0:8, 128:128 + n], ACT.Relu).then_inc(s["hidden"], 1)
                    act.wait_ge(s["se3"], b * 3 + j + 1)
                    act.wait_ge(s["scaled"], b * NGR)
                    act.activation(gain[j][:, :], p_se[:, 256:256 + n], ACT.Sigmoid).then_inc(s["gain"], 1)

        @block.vector
        def _(dve):
            dve.wait_ge(s["weights"], NW * 16)
            dve.wait_ge(s["ident"], 1)
            for t in range(9):
                dve.tensor_scalar(dw[:, t, :], ident[:, :], wp[:, t:t + 1], None, ALU.mult).then_inc(s["dw"], 1)
            with dve.Fori(0, B) as b:
                for j in range(3):
                    dve.wait_ge(s[f"u{j}"], (b + 1) * 32)
                    if j >= 2:
                        dve.wait_ge(s["se1"], b * 3 + j - 1)
                    else:
                        dve.wait_ge(s["se1"], b * 3)
                    dve.tensor_reduce(total[:, j % 2, 0:HW[j]], u[j][:, :, :], AX.X, ALU.add).then_inc(s["total"], 1)
                for n, (j, g) in enumerate(groups):
                    wins = slice(g * GW[j], (g + 1) * GW[j])
                    size = GW[j] * AREA[j]
                    k = b * NGR + n + 1
                    sc = scaled[:, n % 2, 0:size].rearrange("p (w a) -> p w a", a=AREA[j])
                    py = p_y[:, n % NB, 0:size].rearrange("p (w a) -> p w a", a=AREA[j])
                    pd = p_d[:, n % NB, 0:size].rearrange("p (w a) -> p w a", a=AREA[j])
                    if g == 0:
                        dve.wait_ge(s["gain"], b * 3 + j + 1)
                    dve.wait_ge(s["mm"], k)
                    dve.wait_ge(s["att"], freed(b, n, 2, 1, NGR))
                    dve.scalar_tensor_tensor(sc, py, b2s[:, 0:1],
                                             gain[j][:, wins, None].broadcast_to([128, GW[j], AREA[j]]),
                                             ALU.add, ALU.mult).then_inc(s["scaled"], 1)
                    dve.wait_ge(s["scaled"], k)
                    dve.scalar_tensor_tensor(u[j][:, wins, :], pd, bps[:, 0:1], sc, ALU.add,
                                             ALU.add).then_inc(s["att"], 1)

        @block.tensor
        def _(pe):
            pe.wait_ge(s["weights"], NW * 16)
            pe.wait_ge(s["dw"], 9)
            taps = sorted(((dy, dx) for dy in (-1, 0, 1) for dx in (-1, 0, 1)), key=lambda t: t != (0, 0))

            def squeeze(b, j):
                n = HW[j]
                k = b * 3 + j
                pe.wait_ge(s["total"], k + 1)
                pe.wait_ge(s["gain"], k)
                pe.matmul(p_se[:, 0:n], w2[:, :], total[:, j % 2, 0:n], start=True, stop=True).then_inc(s["se1"], 1)
                pe.wait_ge(s["mean"], k + 1)
                pe.matmul(p_se[0:8, 128:128 + n], se1[:, :], mean_y[:, 0:n], start=True, stop=True).then_inc(s["se2"], 1)
                pe.wait_ge(s["hidden"], k + 1)
                pe.matmul(p_se[:, 256:256 + n], se2[:, :], hidden[:, 0:n], start=True, stop=True).then_inc(s["se3"], 1)

            with pe.Fori(0, B) as b:
                for n, (j, g) in enumerate(groups):
                    if g == 0:
                        squeeze(b, j)
                        pe.wait_ge(s[f"u{j}"], (b + 1) * 32)
                    k = SIDE[j]
                    size = GW[j] * AREA[j]
                    wins = slice(g * GW[j], (g + 1) * GW[j])
                    pe.wait_ge(s["att"], freed(b, n, NB, 1, NGR))
                    pe.matmul(p_y[:, n % NB, 0:size], w2[:, :], u[j][:, wins, :], start=True, stop=True)
                    src = u[j][:, wins, :].rearrange("p w (y x) -> p w y x", x=k)
                    dst = p_d[:, n % NB, 0:size].rearrange("p (w y x) -> p w y x", y=k, x=k)
                    for t, (dy, dx) in enumerate(taps):
                        y0, y1, x0, x1 = max(0, -dy), k - max(0, dy), max(0, -dx), k - max(0, dx)
                        mm = pe.matmul(dst[:, :, y0:y1, x0:x1], dw[:, (dy + 1) * 3 + dx + 1, :],
                                       src[:, :, y0 + dy:y1 + dy, x0 + dx:x1 + dx], start=(t == 0), stop=(t == 8))
                    mm.then_inc(s["mm"], 1)

    nc.clear_and_free_semaphores(list(s.values()))
    nc.all_engine_barrier()


def windows_fold(nc, sem, x1_d, w3t, b3, att_d, x2_d):
    with ExitStack() as ctx:
        def sb(name, shape, dt=FP32):
            return ctx.enter_context(nc.sbuf_tensor("f_" + name, shape, dt))

        w = sb("w", [CB, 3, C])
        bias = sb("bias", [CH, 2])
        xt = sb("xt", [CB, 3, L])
        flat = [sb(f"flat{j}", [CB, FLAT[j]]) for j in range(3)]
        fold = sb("fold", [CB, L])
        out = sb("out", [CH, 2, 2, TT])
        p = ctx.enter_context(nc.psum_tensor("f_p", [CH, 4, TT], FP32))
        s = {k: sem("f_" + k) for k in ("weights", "x", "in0", "in1", "in2", "clear", "add0", "add1", "add2", "half",
                                        "x_done", "mm", "out", "st0", "st1", "sp_go")}
        block = ctx.enter_context(nc.Block())
        x_v = x1_d.rearrange("b (g p) t -> b p g t", g=3)
        o_v = x2_d.rearrange("b (h p) t -> b p h t", h=2)
        n2, k2, st2 = WINDOWS[2], SIDE[2], STEP[2]
        OVER = k2 - st2
        N_ADD2 = 2 * k2

        def view(img, flat_j, j, i, c0, c1):
            n, k, st = WINDOWS[j], SIDE[j], STEP[j]
            im = bass.AP(img.tensor, img.offset + i * IMG + c0, [img.ap[0], [st * IMG, n], [1, c1 - c0], [st, n]])
            fl = bass.AP(flat_j.tensor, flat_j.offset + (i * k + c0) * n * n,
                         [flat_j.ap[0], [n, n], [n * n, c1 - c0], [1, n]])
            return im, fl

        @block.sync
        def _(sp):
            sp.dma_start(w[:, :, :], w3t.rearrange("(g p) n -> p g n", g=3)).then_inc(s["weights"], 16)
            sp.dma_start(bias[:, :], b3.rearrange("(h p) -> p h", h=2), allow_slow_non_contiguous=True).then_inc(s["weights"], 16)
            with sp.Fori(0, B) as b:
                hold(sp, s["sp_go"], s["mm"], b * (NT * 2))
                sp.dma_start(xt[:, :, :], x_v[bass.ds(b, 1), :, :, :].rearrange("a p g t -> (a p) g t")).then_inc(s["x"], 16)
                for j in (2, 0, 1):
                    hold(sp, s["sp_go"], s[f"add{j}"], b * (N_ADD2 if j == 2 else SIDE[j]))
                    sp.dma_start(flat[j][:, :], att_d[j][bass.ds(b, 1), :].rearrange("a (c f) -> (a c) f", c=CB)).then_inc(s[f"in{j}"], 16)
                for t in range(NT):
                    hold(sp, s["sp_go"], s["out"], b * (NT * 2) + (t + 1) * 2)
                    sp.dma_start(o_v[bass.ds(b, 1), :, :, t * TT:(t + 1) * TT].rearrange("a p h t -> (a p) h t"),
                                 out[:, t % 2, :, :]).then_inc(s[f"st{t % 2}"], 16)
            for i in range(2):
                hold(sp, s["sp_go"], s[f"st{i}"], B * NT // 2 * 16)

        @block.gpsimd
        def _(pool):
            with pool.Fori(0, B) as b:
                pool.wait_ge(s["x"], (b + 1) * 16)
                pool.wait_ge(s["in0"], (b + 1) * 16)
                for i in range(SIDE[0]):
                    im, fl = view(xt[:, 0, :], flat[0][:, :], 0, i, 0, SIDE[0])
                    pool.tensor_tensor(im, im, fl, ALU.add).then_inc(s["add0"], 1)

        @block.vector
        def _(dve):
            with dve.Fori(0, B) as b:
                dve.memset(fold[:, :], 0.0).then_inc(s["clear"], 1)
                dve.wait_ge(s["clear"], b + 1)
                dve.wait_ge(s["in2"], (b + 1) * 16)
                a = 0
                for c0, c1 in ((0, st2), (st2, k2)):
                    for i in range(k2):
                        im, fl = view(fold[:, :], flat[2][:, :], 2, i, c0, c1)
                        if i == st2 or (i == 0 and c0):
                            dve.wait_ge(s["add2"], b * N_ADD2 + a)
                        dve.tensor_tensor(im, im, fl, ALU.add).then_inc(s["add2"], 1)
                        a += 1
                dve.wait_ge(s["add2"], b * N_ADD2 + a)
                f0 = fold[:, :]
                for i, dims in enumerate(([[st2 * IMG, n2 - 1], [1, OVER * IMG]],
                                          [[IMG, IMG], [st2, n2 - 1], [1, OVER]])):
                    v = bass.AP(f0.tensor, f0.offset + (st2 * IMG if i == 0 else st2), [f0.ap[0]] + dims)
                    dve.tensor_scalar(v, v, 0.5, None, ALU.mult).then_inc(s["half"], 1)
                    dve.wait_ge(s["half"], 2 * b + i + 1)
                dve.wait_ge(s["x"], (b + 1) * 16)
                dve.tensor_tensor(xt[:, 2, :], xt[:, 2, :], fold[:, :], ALU.add).then_inc(s["x_done"], 1)
                dve.wait_ge(s["in1"], (b + 1) * 16)
                for i in range(SIDE[1]):
                    im, fl = view(xt[:, 1, :], flat[1][:, :], 1, i, 0, SIDE[1])
                    dve.tensor_tensor(im, im, fl, ALU.add).then_inc(s["add1"], 1)
                dve.wait_ge(s["x_done"], b + 1)

        @block.tensor
        def _(pe):
            pe.wait_ge(s["weights"], 32)
            with pe.Fori(0, B) as b:
                pe.wait_ge(s["add0"], (b + 1) * SIDE[0])
                pe.wait_ge(s["x_done"], b + 1)
                pe.wait_ge(s["add1"], (b + 1) * SIDE[1])
                for t in range(NT):
                    for m in range(2):
                        n = 2 * t + m
                        pe.wait_ge(s["out"], freed(b, n, 4, 1, NT * 2))
                        for g in range(3):
                            mm = pe.matmul(p[:, n % 4, :], w[:, g, m * CH:(m + 1) * CH], xt[:, g, t * TT:(t + 1) * TT],
                                           start=(g == 0), stop=(g == 2))
                        mm.then_inc(s["mm"], 1)

        @block.scalar
        def _(act):
            act.wait_ge(s["weights"], 32)
            with act.Fori(0, B) as b:
                for n in range(2 * NT):
                    t, m = n // 2, n % 2
                    act.wait_ge(s["mm"], b * (NT * 2) + n + 1)
                    if m == 0:
                        act.wait_ge(s[f"st{t % 2}"], b * (NT // 2 * 16) + t // 2 * 16)
                    act.activation(out[:, t % 2, m, :], p[:, n % 4, :], ACT.Identity,
                                   bias=bias[:, m:m + 1]).then_inc(s["out"], 1)

    nc.clear_and_free_semaphores(list(s.values()))
    nc.all_engine_barrier()


def gated_attention(nc, sem, x_in, w_query, w_key, w_value, w_out, rowmax_d, out_d):
    D = w_query.shape[1]
    G = 4
    DP = 32
    R3 = 3 * DP
    VC = DP
    KB = L // 128
    PAIR = 2 * TT
    NSLOT = 3
    UNITS = KB // 2
    QUADS = NT * UNITS // 2
    NP = 6
    LAG = 2

    order = [("qk", t, 0) for t in range(NT)]
    order += [("max", i, h) for i in range(KB) for h in range(L // PAIR)]
    order += [("v", 0, 0)]
    for n in range(NT * UNITS + LAG + 2):
        if n < NT * UNITS:
            order.append(("s", n // UNITS, n % UNITS))
        m = n - LAG - 1
        if m >= 0 and m % UNITS == UNITS - 1:
            order.append(("o", m // UNITS, 0))
    reader = ["act" if what in ("qk", "s") else "dve" for what, _, _ in order]
    U = len(order)
    at = {key: n for n, key in enumerate(order)}
    reads = {r: reader.count(r) for r in ("act", "dve")}

    with ExitStack() as ctx:
        def sb(name, shape, dt=FP32):
            return ctx.enter_context(nc.sbuf_tensor("g_" + name, shape, dt))

        ident = sb("ident", [128, 128])
        wq = sb("wq", [CH, 2, R3])
        wk = sb("wk", [CH, 2, R3])
        wv = sb("wv", [CH, 2, D])
        wo = sb("wo", [128, C])
        den_sel = sb("den_sel", [128, CH])
        less = sb("less", [128, 3])
        x = sb("x", [CH, 2, 2, L])
        first = sb("first", [128, 2, L], BF16)
        second = sb("second", [128, 2, L], BF16)
        q_hmh = sb("q_hmh", [R3, L], BF16)
        raw = sb("raw", [R3, 2, 2, TT])
        rest = sb("rest", [R3, 2, 2, TT])
        mid = sb("mid", [R3, 2, 2, TT], BF16)
        va = sb("va", [128, KB, DP])
        part_max = sb("part_max", [128, KB, L // PAIR])
        neg_max = sb("neg_max", [128, KB])
        max_t = sb("max_t", [KB, 3, 128], BF16)
        max_rest = sb("max_rest", [KB, 128])
        prob = sb("prob", [128, NP, PAIR])
        o_sb = sb("o_sb", [128, 2, TT])
        recip = sb("recip", [CH, TT])
        normed = sb("normed", [CH, 2, 2, TT])
        out = sb("out", [CH, 2, 2, TT])
        p_s = ctx.enter_context(nc.psum_tensor("g_p_s", [128, NSLOT, PAIR], FP32))
        p_o = ctx.enter_context(nc.psum_tensor("g_p_o", [128, TT], FP32))
        p_m = ctx.enter_context(nc.psum_tensor("g_p_m", [128, TT], FP32))
        s = {k: sem("g_" + k) for k in (
            "made", "ident", "weights", "x0", "x1", "filled", "act", "dve", "high", "rest", "mid", "split", "max",
            "max_mm", "max_step", "max_t", "max_st", "max_row", "weighed", "o_sb", "den", "recip", "normed", "gate",
            "out", "st0", "st1", "sp_go", "pe_go", "pool_go")}
        block = ctx.enter_context(nc.Block())
        x_v = x_in.rearrange("b (h p) t -> b p h t", h=2)
        o_v = out_d.rearrange("b (h p) t -> b p h t", h=2)

        def filled(eng, b, key):
            eng.wait_ge(s["filled"], b * U + at[key] + 1)

        def slot(key):
            return p_s[:, at[key] % NSLOT, :]

        loads = [(wv[:, :, :], w_value.rearrange("(h p) n -> p h n", h=2))]
        for g in range(3):
            c = slice(DP * g, DP * g + D)
            loads.append((wq[:, :, c], w_query.rearrange("(h p) n -> p h n", h=2)))
            loads.append((wk[:, :, c], w_key.rearrange("(h p) n -> p h n", h=2)))
        for g in range(G):
            loads.append((wo[DP * g:DP * g + D, :], w_out))
        NL = len(loads)
        n_made = 8

        @block.sync
        def _(sp):
            hold(sp, s["sp_go"], s["made"], n_made)
            for dst, src in loads:
                sp.dma_start(dst, src).then_inc(s["weights"], 16)
            with sp.Fori(0, B // 2) as bb:
                for par in range(2):
                    b = bb * 2 + par
                    hold(sp, s["sp_go"], s["out"], bb * (2 * NT))
                    sp.dma_start(x[:, par, :, :], x_v[bass.ds(b, 1), :, :, :].rearrange("a p h t -> (a p) h t")
                                 ).then_inc(s[f"x{par}"], 16)
                for par in range(2):
                    b = bb * 2 + par
                    hold(sp, s["sp_go"], s["max_t"], b + 1)
                    sp.dma_start(rowmax_d[bass.ds(b, 1), :, :].rearrange("a r (k p) -> (a k) r p", p=128),
                                 max_t[:, :, :]).then_inc(s["max_st"], 16)
                    hold(sp, s["sp_go"], s["max_st"], (b + 1) * 16)
                    sp.dma_start(second[R3:R3 + 3, 0, :], rowmax_d[bass.ds(b, 1), :, :].rearrange("a r t -> (a r) t")
                                 ).then_inc(s["max_row"], 16)
                    for t in range(NT):
                        hold(sp, s["sp_go"], s["out"], b * NT + t + 1)
                        sp.dma_start(o_v[bass.ds(b, 1), :, :, t * TT:(t + 1) * TT].rearrange("a p h t -> (a p) h t"),
                                     out[:, t % 2, :, :]).then_inc(s[f"st{t % 2}"], 16)
            for i in range(2):
                hold(sp, s["sp_go"], s[f"st{i}"], B * NT // 2 * 16)

        @block.gpsimd
        def _(pool):
            for t in (ident, den_sel, wo, less):
                pool.memset(t[:, :], 0.0).then_inc(s["made"], 1)
            for t in (wq, wk, va):
                pool.memset(t[:, :, :], 0.0).then_inc(s["made"], 1)
            pool.wait_ge(s["made"], n_made - 1)
            pool.memset(first[R3:128, 1, :], 1.0).then_inc(s["made"], 1)
            pool.wait_ge(s["made"], n_made)
            pool.affine_select(out=ident[:, :], in_=ident[:, :], compare_op=ALU.not_equal, fill=1.0, base=0,
                               pattern=[[-1, 128]], channel_multiplier=1).then_inc(s["ident"], 1)
            pool.memset(va[:, :, D:D + 1], 1.0).then_inc(s["ident"], 1)
            for n, (c, g) in enumerate(((0, 1), (0, 2), (1, 2), (2, 1))):
                pool.wait_ge(s["ident"], n + 2)
                pool.memset(less[DP * g:DP * g + DP, c:c + 1], -1.0).then_inc(s["ident"], 1)
            pool.wait_ge(s["ident"], 6)
            for g in range(G):
                pool.affine_select(out=den_sel[:, :], in_=den_sel[:, :], compare_op=ALU.not_equal, fill=1.0,
                                   base=-(DP * g + D), pattern=[[0, CH]], channel_multiplier=1).then_inc(s["ident"], 1)
                pool.wait_ge(s["ident"], 7 + g)
            with pool.Fori(0, B) as b:
                for t in range(NT):
                    pool.wait_ge(s["rest"], b * NT + t + 1)
                    pool.wait_ge(s["split"], freed(b, t, 2, 1, NT))
                    pool.sem_inc(s["pool_go"], 1)
                    pool.tensor_scalar(mid[:, t % 2, :, :], rest[:, t % 2, :, :], 1.0, 0.0, ALU.mult, ALU.add
                                       ).then_inc(s["mid"], 1)

        N_ID = 6 + G

        @block.scalar
        def _(act):
            act.wait_ge(s["ident"], N_ID)
            act.wait_ge(s["weights"], NL * 16)

            def projected(b, t):
                key = ("qk", t, 0)
                filled(act, b, key)
                cols = slice(t * TT, (t + 1) * TT)
                both = slot(key)[0:R3, :].rearrange("p (i t) -> p i t", i=2)
                act.activation(first[0:R3, :, cols], both, ACT.Copy).then_inc(s["high"], 1)
                act.wait_ge(s["rest"], freed(b, t, 2, 1, NT))
                act.wait_ge(s["split"], freed(b, t, 2, 1, NT))
                act.activation(raw[:, t % 2, :, :], both, ACT.Copy).then_inc(s["act"], 1)

            def weights_of(b, n):
                key = ("s", n // UNITS, n % UNITS)
                filled(act, b, key)
                act.wait_ge(s["weighed"], b * QUADS + ((n - NP) // 2 + 1 if n >= NP else 0))
                act.activation(prob[:, n % NP, :], slot(key), ACT.Exp).then_inc(s["act"], 1)

            def gate_of(b, t):
                act.wait_ge(s["normed"], b * NT + t + 1)
                act.activation(normed[:, t % 2, :, :], normed[:, t % 2, :, :], ACT.Sigmoid).then_inc(s["gate"], 1)

            with act.Fori(0, B) as b:
                act.wait_ge(s["weighed"], b * QUADS)
                for t in range(NT):
                    projected(b, t)
                for n in range(NT * UNITS + LAG + 1):
                    if n < NT * UNITS:
                        weights_of(b, n)
                    m = n - LAG
                    if m >= 0 and m % UNITS == UNITS - 1:
                        t = m // UNITS
                        act.wait_ge(s["weighed"], b * QUADS + (m + 1) // 2)
                        act.wait_ge(s["den"], freed(b, t, 2, 1, NT))
                        act.activation(o_sb[:, t % 2, :], p_o[:, :], ACT.Copy).then_inc(s["o_sb"], 1)
                    m = n - 10
                    if m >= 0 and m % UNITS == UNITS - 1:
                        gate_of(b, m // UNITS)
                gate_of(b, NT - 1)

        @block.vector
        def _(dve):
            dve.wait_ge(s["ident"], N_ID)
            dve.wait_ge(s["weights"], NL * 16)

            def split(b, t):
                if t < NT:
                    cols = slice(t * TT, (t + 1) * TT)
                    dve.wait_ge(s["act"], b * reads["act"] + t + 1)
                    dve.wait_ge(s["high"], b * NT + t + 1)
                    dve.wait_ge(s["mid"], freed(b, t, 2, 1, NT))
                    q, high = raw[:, t % 2, 0, :], first[0:R3, 0, cols]
                    dve.scalar_tensor_tensor(rest[:, t % 2, 0, :], high, less[0:R3, 0:1], q, ALU.mult, ALU.add)
                    dve.tensor_tensor(rest[:, t % 2, 1, :], raw[:, t % 2, 1, :], first[0:R3, 1, cols], ALU.subtract
                                      ).then_inc(s["rest"], 1)
                    dve.scalar_tensor_tensor(q_hmh[:, cols], high, less[0:R3, 2:3], q, ALU.mult, ALU.add)
                if t >= 1:
                    cols = slice((t - 1) * TT, t * TT)
                    dve.wait_ge(s["mid"], b * NT + t)
                    dve.scalar_tensor_tensor(second[0:R3, :, cols], mid[:, (t - 1) % 2, :, :], less[0:R3, 1:2],
                                             rest[:, (t - 1) % 2, :, :], ALU.mult, ALU.add).then_inc(s["split"], 1)

            def normalise(b, t):
                key = ("o", t, 0)
                dve.wait_ge(s["den"], b * NT + t + 1)
                dve.wait_ge(s["normed"], b * NT + t)
                dve.reciprocal(recip[:, :], p_m[0:CH, :]).then_inc(s["recip"], 1)
                dve.wait_ge(s["recip"], b * NT + t + 1)
                filled(dve, b, key)
                dve.wait_ge(s["out"], freed(b, t, 2, 1, NT))
                dve.tensor_tensor(normed[:, t % 2, :, :], slot(key)[0:CH, :].rearrange("p (h t) -> p h t", h=2),
                                  recip[:, None, :].broadcast_to([CH, 2, TT]), ALU.mult).then_inc(s["dve"], 1)
                dve.wait_ge(s["dve"], b * reads["dve"] + sum(r == "dve" for r in reader[:at[key] + 1]))
                dve.sem_inc(s["normed"], 1)

            def finish(b, par, t):
                cols = slice(t * TT, (t + 1) * TT)
                dve.wait_ge(s[f"st{t % 2}"], b * (NT // 2 * 16) + t // 2 * 16)
                dve.wait_ge(s["gate"], b * NT + t + 1)
                dve.scalar_tensor_tensor(out[:, t % 2, :, :], normed[:, t % 2, :, :], 1.0, x[:, par, :, cols],
                                         ALU.add, ALU.mult).then_inc(s["out"], 1)

            with dve.Fori(0, B // 2) as bb:
                for par in range(2):
                    b = bb * 2 + par
                    for t in range(NT + 1):
                        split(b, t)
                    for i in range(KB):
                        for h in range(L // PAIR):
                            key = ("max", i, h)
                            filled(dve, b, key)
                            if i == 0 and h == 0:
                                dve.wait_ge(s["max"], b)
                            dve.tensor_reduce(part_max[:, i, h:h + 1], slot(key), AX.X, ALU.max).then_inc(s["dve"], 1)
                    dve.wait_ge(s["dve"], b * reads["dve"] + KB * (L // PAIR))
                    dve.wait_ge(s["max_mm"], b)
                    dve.tensor_reduce(neg_max[:, :], part_max[:, :, :], AX.X, ALU.max, negate=True).then_inc(s["max"], 1)
                    dve.wait_ge(s["max_mm"], b + 1)
                    dve.wait_ge(s["max_st"], b * 16)
                    high, middle, low = (max_t[:, i, :] for i in range(3))
                    dve.tensor_copy(high, p_m[0:KB, 0:128]).then_inc(s["max_step"], 1)
                    dve.wait_ge(s["max_step"], b * 3 + 1)
                    dve.tensor_tensor(max_rest[:, :], p_m[0:KB, 0:128], high, ALU.subtract).then_inc(s["max_step"], 1)
                    dve.wait_ge(s["max_step"], b * 3 + 2)
                    dve.tensor_copy(middle, max_rest[:, :]).then_inc(s["max_step"], 1)
                    dve.wait_ge(s["max_step"], b * 3 + 3)
                    dve.tensor_tensor(low, max_rest[:, :], middle, ALU.subtract).then_inc(s["max_t"], 1)
                    key = ("v", 0, 0)
                    filled(dve, b, key)
                    dve.tensor_copy(va[:, :, 0:D], slot(key).rearrange("p (k c) -> p k c", c=DP)[:, :, 0:D]
                                    ).then_inc(s["dve"], 1)
                    for t in range(NT + 1):
                        if t < NT:
                            normalise(b, t)
                        if t >= 1:
                            finish(b, par, t - 1)

        @block.tensor
        def _(pe):
            pe.wait_ge(s["ident"], N_ID)
            pe.wait_ge(s["weights"], NL * 16)

            def claim(b, key):
                n = at[key] - NSLOT
                if n >= 0:
                    r = reader[n]
                    pe.wait_ge(s[r], b * reads[r] + reader[:n + 1].count(r))
                else:
                    pe.wait_ge(s["act"], b * reads["act"])
                    pe.wait_ge(s["dve"], b * reads["dve"])
                pe.sem_inc(s["pe_go"], 1)

            def project(b, par, t):
                key = ("qk", t, 0)
                claim(b, key)
                for i, w in enumerate((wq, wk)):
                    for h in range(2):
                        mm = pe.matmul(slot(key)[0:R3, i * TT:(i + 1) * TT], w[:, h, :],
                                       x[:, par, h, t * TT:(t + 1) * TT], start=(h == 0), stop=(h == 1))
                mm.then_inc(s["filled"], 1)

            def project_values(b, par):
                key = ("v", 0, 0)
                claim(b, key)
                for kb in range(KB):
                    for h in range(2):
                        mm = pe.matmul(slot(key)[:, kb * DP:kb * DP + D], x[:, par, h, kb * 128:(kb + 1) * 128],
                                       wv[:, h, :], start=(h == 0), stop=(h == 1))
                mm.then_inc(s["filled"], 1)

            def scores_for_max(b, i, h):
                key = ("max", i, h)
                claim(b, key)
                if i == 0:
                    pe.wait_ge(s["split"], b * NT + 2 * h + 2)
                    pe.sem_inc(s["pe_go"], 1)
                q = slice(i * 128, (i + 1) * 128)
                for j in range(2):
                    k = slice(h * PAIR + j * TT, h * PAIR + (j + 1) * TT)
                    pe.matmul(slot(key)[:, j * TT:(j + 1) * TT], second[0:R3, 0, q], first[0:R3, 1, k],
                              start=True, stop=False)
                    mm = pe.matmul(slot(key)[:, j * TT:(j + 1) * TT], q_hmh[:, q], second[0:R3, 1, k],
                                   start=False, stop=True)
                mm.then_inc(s["filled"], 1)

            def scores(b, n):
                t, u = n // UNITS, n % UNITS
                key = ("s", t, u)
                claim(b, key)
                q = slice(t * TT, (t + 1) * TT)
                for j in range(2):
                    k = slice((2 * u + j) * 128, (2 * u + j + 1) * 128)
                    pe.matmul(slot(key)[:, j * TT:(j + 1) * TT], first[0:R3 + 3, 1, k], second[0:R3 + 3, 0, q],
                              start=True, stop=False)
                    mm = pe.matmul(slot(key)[:, j * TT:(j + 1) * TT], second[0:R3, 1, k], q_hmh[:, q],
                                   start=False, stop=True)
                mm.then_inc(s["filled"], 1)

            def weigh(b, n):
                t, u = n // UNITS, n % UNITS
                key = ("s", t, u)
                pe.wait_ge(s["act"], b * reads["act"] + reader[:at[key] + 1].count("act"))
                if u == 1:
                    pe.wait_ge(s["o_sb"], b * NT + t)
                pe.sem_inc(s["pe_go"], 1)
                for g in range(G):
                    kb = 2 * (u - 1) + g
                    mm = pe.matmul(p_o[DP * g:DP * g + VC, :], va[:, kb, 0:VC],
                                   prob[:, (n - 1 + g // 2) % NP, g % 2 * TT:(g % 2 + 1) * TT],
                                   start=(kb < G), stop=(kb >= KB - G), tile_position=(0, DP * g))
                mm.then_inc(s["weighed"], 1)

            def project_out(b, t):
                key = ("o", t, 0)
                pe.wait_ge(s["o_sb"], b * NT + t + 1)
                pe.wait_ge(s["recip"], b * NT + t)
                if t == 0:
                    pe.wait_ge(s["max_t"], b + 1)
                pe.sem_inc(s["pe_go"], 1)
                claim(b, key)
                pe.matmul(p_m[0:CH, :], den_sel[:, :], o_sb[:, t % 2, :], start=True, stop=True).then_inc(s["den"], 1)
                for m in range(2):
                    mm = pe.matmul(slot(key)[0:CH, m * TT:(m + 1) * TT], wo[:, m * CH:(m + 1) * CH], o_sb[:, t % 2, :],
                                   start=True, stop=True)
                mm.then_inc(s["filled"], 1)

            with pe.Fori(0, B // 2) as bb:
                for par in range(2):
                    b = bb * 2 + par
                    pe.wait_ge(s[f"x{par}"], (bb + 1) * 16)
                    for t in range(NT):
                        project(b, par, t)
                    for i in range(KB):
                        for h in range(L // PAIR):
                            scores_for_max(b, i, h)
                    pe.wait_ge(s["max"], b + 1)
                    pe.wait_ge(s["recip"], b * NT)
                    pe.sem_inc(s["pe_go"], 1)
                    pe.transpose(p_m[0:KB, 0:128], neg_max[:, :], ident[:, :]).then_inc(s["max_mm"], 1)
                    project_values(b, par)
                    pe.wait_ge(s["dve"], b * reads["dve"] + KB * (L // PAIR) + 1)
                    pe.wait_ge(s["max_row"], (b + 1) * 16)
                    pe.sem_inc(s["pe_go"], 1)
                    for n in range(NT * UNITS + LAG + 2):
                        if n < NT * UNITS:
                            scores(b, n)
                        if n >= LAG and n - LAG < NT * UNITS and (n - LAG) % 2:
                            weigh(b, n - LAG)
                        m = n - LAG - 1
                        if m >= 0 and m % UNITS == UNITS - 1:
                            project_out(b, m // UNITS)

    nc.clear_and_free_semaphores(list(s.values()))
    nc.all_engine_barrier()


def attention(nc, sem, x_in, w_query, w_key, w_value, w_out, biases, rowmax_d, out_d):
    D = w_query.shape[1]
    OC = D + 1
    VS = 128
    SCALE = float(D) ** -0.5
    KB = L // 128
    PAIR = 2 * TT
    NSLOT = 3
    UNITS = KB // 2
    NP = 4
    LAG = 2
    VB = PAIR // VS

    order = [("qk", t, 0) for t in range(NT)]
    order += [("v", i, 0) for i in range(KB // VB)]
    order += [("max", i, h) for i in range(KB) for h in range(L // PAIR)]
    for n in range(NT * UNITS + LAG + 2):
        if n < NT * UNITS:
            order.append(("s", n // UNITS, n % UNITS))
        m = n - LAG - 1
        if m >= 0 and m % UNITS == UNITS - 1:
            order.append(("o", m // UNITS, 0))
    reader = ["act" if what in ("qk", "s") else "dve" for what, _, _ in order]
    U = len(order)
    at = {key: n for n, key in enumerate(order)}
    reads = {r: reader.count(r) for r in ("act", "dve")}

    with ExitStack() as ctx:
        def sb(name, shape, dt=FP32):
            return ctx.enter_context(nc.sbuf_tensor("h_" + name, shape, dt))

        ident = sb("ident", [128, 128])
        wq = sb("wq", [CH, 2, D])
        wk = sb("wk", [CH, 2, D])
        wv = sb("wv", [CH, 2, D])
        wo = sb("wo", [OC, C])
        den_sel = sb("den_sel", [OC, CH])
        bias_q = sb("bias_q", [D, 1])
        bias_k = sb("bias_k", [D, 1])
        bias_v = sb("bias_v", [D, 1])
        bias_d = sb("bias_d", [CH, 2])
        bias_o = sb("bias_o", [CH, 2])
        x = sb("x", [CH, 2, 2, L])
        qa = sb("qa", [128, L])
        ka = sb("ka", [128, L])
        va = sb("va", [128, KB, VS])
        part_max = sb("part_max", [128, KB, L // PAIR])
        neg_max = sb("neg_max", [128, KB])
        max_t = sb("max_t", [KB, 128])
        prob = sb("prob", [128, NP, PAIR])
        o_sb = sb("o_sb", [OC, 2, TT])
        recip = sb("recip", [CH, TT])
        normed = sb("normed", [CH, 2, 2, TT])
        out = sb("out", [CH, 2, 2, TT])
        p_s = ctx.enter_context(nc.psum_tensor("h_" + "p_s", [128, NSLOT, PAIR], FP32))
        p_o = ctx.enter_context(nc.psum_tensor("h_" + "p_o", [128, TT], FP32))
        p_m = ctx.enter_context(nc.psum_tensor("h_" + "p_m", [128, TT], FP32))
        s = {k: sem("h_" + k) for k in (
            "made", "ident", "weights", "bias_mm", "bias", "x0", "x1", "filled", "act", "dve", "part", "max",
            "max_mm", "max_t", "max_st", "max_row", "weighed", "o_sb", "den", "recip", "normed", "out",
            "st0", "st1", "sp_go", "pe_go")}
        block = ctx.enter_context(nc.Block())
        x_v = x_in.rearrange("b (h p) t -> b p h t", h=2)
        o_v = out_d.rearrange("b (h p) t -> b p h t", h=2)

        def filled(eng, b, key):
            eng.wait_ge(s["filled"], b * U + at[key] + 1)

        def slot(key):
            return p_s[:, at[key] % NSLOT, :]

        loads = [(dst[:, :, 0:D], src.rearrange("(h p) n -> p h n", h=2))
                 for dst, src in ((wq, w_query), (wk, w_key), (wv, w_value))]
        loads.append((wo[0:D, :], w_out))
        b_q, b_k, b_v, b_o = biases
        for dst, src in ((bias_q, b_q), (bias_k, b_k), (bias_v, b_v)):
            loads.append((dst[:, :], src.rearrange("(p a) -> p a", a=1)))
        NL = len(loads) + 1
        n_made = 9

        @block.sync
        def _(sp):
            hold(sp, s["sp_go"], s["made"], n_made)
            for dst, src in loads:
                sp.dma_start(dst, src).then_inc(s["weights"], 16)
            sp.dma_start(bias_d[:, :], b_o.rearrange("(h p) -> p h", h=2),
                         allow_slow_non_contiguous=True).then_inc(s["weights"], 16)
            with sp.Fori(0, B // 2) as bb:
                for par in range(2):
                    b = bb * 2 + par
                    hold(sp, s["sp_go"], s["out"], bb * (2 * NT))
                    sp.dma_start(x[:, par, :, :], x_v[bass.ds(b, 1), :, :, :].rearrange("a p h t -> (a p) h t")
                                 ).then_inc(s[f"x{par}"], 16)
                for par in range(2):
                    b = bb * 2 + par
                    hold(sp, s["sp_go"], s["max_t"], b + 1)
                    sp.dma_start(rowmax_d[bass.ds(b, 1), :].rearrange("a (k p) -> (a k) p", p=128),
                                 max_t[:, :]).then_inc(s["max_st"], 16)
                    hold(sp, s["sp_go"], s["max_st"], (b + 1) * 16)
                    sp.dma_start(qa[D:D + 1, :], rowmax_d[bass.ds(b, 1), :]).then_inc(s["max_row"], 16)
                    for t in range(NT):
                        hold(sp, s["sp_go"], s["out"], b * NT + t + 1)
                        sp.dma_start(o_v[bass.ds(b, 1), :, :, t * TT:(t + 1) * TT].rearrange("a p h t -> (a p) h t"),
                                     out[:, t % 2, :, :]).then_inc(s[f"st{t % 2}"], 16)
            for i in range(2):
                hold(sp, s["sp_go"], s[f"st{i}"], B * NT // 2 * 16)

        @block.gpsimd
        def _(pool):
            for t in (ident, den_sel, wo, bias_q, bias_k):
                pool.memset(t[:, :], 0.0).then_inc(s["made"], 1)
            for t in (wq, wk, va):
                pool.memset(t[:, :, :], 0.0).then_inc(s["made"], 1)
            pool.memset(ka[:, :], 1.0).then_inc(s["made"], 1)
            pool.wait_ge(s["made"], n_made)
            pool.affine_select(out=ident[:, :], in_=ident[:, :], compare_op=ALU.not_equal, fill=1.0, base=0,
                               pattern=[[-1, 128]], channel_multiplier=1).then_inc(s["ident"], 1)
            pool.memset(va[:, :, D:D + 1], 1.0).then_inc(s["ident"], 1)
            pool.affine_select(out=den_sel[:, :], in_=den_sel[:, :], compare_op=ALU.not_equal, fill=1.0,
                               base=-D, pattern=[[0, CH]], channel_multiplier=1).then_inc(s["ident"], 1)

        N_ID = 3

        @block.scalar
        def _(act):
            act.wait_ge(s["ident"], N_ID)
            act.wait_ge(s["weights"], NL * 16)
            act.wait_ge(s["bias_mm"], 1)
            for m in range(2):
                act.activation(bias_o[:, m:m + 1], p_m[0:CH, m:m + 1], ACT.Identity,
                               bias=bias_d[:, m:m + 1]).then_inc(s["bias"], 1)

            def projected(b, t):
                key = ("qk", t, 0)
                filled(act, b, key)
                cols = slice(t * TT, (t + 1) * TT)
                act.activation(qa[0:D, cols], slot(key)[0:D, 0:TT], ACT.Identity, bias=bias_q[:, 0:1])
                act.activation(ka[0:D, cols], slot(key)[0:D, TT:PAIR], ACT.Identity, bias=bias_k[:, 0:1]
                               ).then_inc(s["act"], 1)

            def weights_of(b, n):
                key = ("s", n // UNITS, n % UNITS)
                filled(act, b, key)
                act.wait_ge(s["weighed"], freed(b, n, NP, 1, NT * UNITS))
                act.activation(prob[:, n % NP, :], slot(key), ACT.Exp, scale=SCALE).then_inc(s["act"], 1)

            with act.Fori(0, B) as b:
                act.wait_ge(s["weighed"], b * (NT * UNITS))
                for t in range(NT):
                    projected(b, t)
                act.wait_ge(s["max_mm"], b + 1)
                act.wait_ge(s["max_st"], b * 16)
                act.activation(max_t[:, :], p_m[0:KB, 0:128], ACT.Copy).then_inc(s["max_t"], 1)
                for n in range(NT * UNITS + LAG + 1):
                    if n < NT * UNITS:
                        weights_of(b, n)
                    m = n - LAG
                    if m >= 0 and m % UNITS == UNITS - 1:
                        t = m // UNITS
                        act.wait_ge(s["weighed"], b * (NT * UNITS) + m + 1)
                        act.wait_ge(s["den"], freed(b, t, 2, 1, NT))
                        act.activation(o_sb[:, t % 2, :], p_o[0:OC, :], ACT.Copy).then_inc(s["o_sb"], 1)

        @block.vector
        def _(dve):
            dve.wait_ge(s["ident"], N_ID)
            dve.wait_ge(s["weights"], NL * 16)
            dve.wait_ge(s["bias"], 2)

            def normalise(b, t):
                key = ("o", t, 0)
                dve.wait_ge(s["den"], b * NT + t + 1)
                dve.wait_ge(s["normed"], b * NT + t)
                dve.reciprocal(recip[:, :], p_m[0:CH, :]).then_inc(s["recip"], 1)
                dve.wait_ge(s["recip"], b * NT + t + 1)
                filled(dve, b, key)
                dve.wait_ge(s["out"], freed(b, t, 2, 1, NT))
                dve.tensor_tensor(normed[:, t % 2, :, :], slot(key)[0:CH, :].rearrange("p (h t) -> p h t", h=2),
                                  recip[:, None, :].broadcast_to([CH, 2, TT]), ALU.mult).then_inc(s["dve"], 1)
                dve.wait_ge(s["dve"], b * reads["dve"] + sum(r == "dve" for r in reader[:at[key] + 1]))
                dve.sem_inc(s["normed"], 1)

            def finish(b, par, t):
                cols = slice(t * TT, (t + 1) * TT)
                dve.wait_ge(s[f"st{t % 2}"], b * (NT // 2 * 16) + t // 2 * 16)
                dve.wait_ge(s["normed"], b * NT + t + 1)
                for m in range(2):
                    ins = dve.scalar_tensor_tensor(out[:, t % 2, m, :], normed[:, t % 2, m, :], bias_o[:, m:m + 1],
                                                   x[:, par, m, cols], ALU.add, ALU.add)
                ins.then_inc(s["out"], 1)

            with dve.Fori(0, B // 2) as bb:
                for par in range(2):
                    b = bb * 2 + par
                    dve.wait_ge(s["weighed"], b * (NT * UNITS))
                    for i in range(KB // VB):
                        key = ("v", i, 0)
                        filled(dve, b, key)
                        dve.tensor_copy(va[:, i * VB:(i + 1) * VB, 0:D],
                                        slot(key).rearrange("p (k c) -> p k c", c=VS)[:, :, 0:D]).then_inc(s["dve"], 1)
                    for i in range(KB):
                        for h in range(L // PAIR):
                            key = ("max", i, h)
                            filled(dve, b, key)
                            if i == 0 and h == 0:
                                dve.wait_ge(s["max"], b)
                            dve.tensor_reduce(part_max[:, i, h:h + 1], slot(key), AX.X, ALU.max).then_inc(s["dve"], 1)
                    dve.wait_ge(s["dve"], b * reads["dve"] + KB // VB + KB * (L // PAIR))
                    dve.wait_ge(s["max_mm"], b)
                    dve.tensor_reduce(neg_max[:, :], part_max[:, :, :], AX.X, ALU.max, negate=True).then_inc(s["max"], 1)
                    for t in range(NT + 1):
                        if t < NT:
                            normalise(b, t)
                        if t >= 1:
                            finish(b, par, t - 1)

        @block.tensor
        def _(pe):
            pe.wait_ge(s["ident"], N_ID)
            pe.wait_ge(s["weights"], NL * 16)
            for m in range(2):
                mm = pe.matmul(p_m[0:CH, m:m + 1], wo[0:D, m * CH:(m + 1) * CH], bias_v[:, :], start=True, stop=True)
            mm.then_inc(s["bias_mm"], 1)
            pe.wait_ge(s["bias"], 2)

            def claim(b, key):
                n = at[key] - NSLOT
                if n >= 0:
                    r = reader[n]
                    pe.wait_ge(s[r], b * reads[r] + reader[:n + 1].count(r))
                else:
                    pe.wait_ge(s["act"], b * reads["act"])
                    pe.wait_ge(s["dve"], b * reads["dve"])
                pe.sem_inc(s["pe_go"], 1)

            def project(b, par, t):
                key = ("qk", t, 0)
                claim(b, key)
                for i, w in enumerate((wq, wk)):
                    for h in range(2):
                        mm = pe.matmul(slot(key)[0:D, i * TT:(i + 1) * TT], w[:, h, :],
                                       x[:, par, h, t * TT:(t + 1) * TT], start=(h == 0), stop=(h == 1))
                mm.then_inc(s["filled"], 1)

            def project_values(b, par, i):
                key = ("v", i, 0)
                claim(b, key)
                for k in range(VB):
                    kb = i * VB + k
                    for h in range(2):
                        mm = pe.matmul(slot(key)[:, k * VS:k * VS + D], x[:, par, h, kb * 128:(kb + 1) * 128],
                                       wv[:, h, :], start=(h == 0), stop=(h == 1))
                mm.then_inc(s["filled"], 1)

            def scores_for_max(b, i, h):
                key = ("max", i, h)
                claim(b, key)
                for j in range(2):
                    mm = pe.matmul(slot(key)[:, j * TT:(j + 1) * TT], qa[0:D, i * 128:(i + 1) * 128],
                                   ka[0:D, h * PAIR + j * TT:h * PAIR + (j + 1) * TT], start=True, stop=True)
                mm.then_inc(s["filled"], 1)

            def scores(b, n):
                t, u = n // UNITS, n % UNITS
                key = ("s", t, u)
                claim(b, key)
                for j in range(2):
                    kb = 2 * u + j
                    mm = pe.matmul(slot(key)[:, j * TT:(j + 1) * TT], ka[0:D + 1, kb * 128:(kb + 1) * 128],
                                   qa[0:D + 1, t * TT:(t + 1) * TT], start=True, stop=True)
                mm.then_inc(s["filled"], 1)

            def weigh(b, n):
                t, u = n // UNITS, n % UNITS
                key = ("s", t, u)
                pe.wait_ge(s["act"], b * reads["act"] + reader[:at[key] + 1].count("act"))
                if u == 0:
                    pe.wait_ge(s["o_sb"], b * NT + t)
                    pe.sem_inc(s["pe_go"], 1)
                for j in range(2):
                    kb = 2 * u + j
                    mm = pe.matmul(p_o[0:OC, :], va[:, kb, 0:OC], prob[:, n % NP, j * TT:(j + 1) * TT],
                                   start=(kb == 0), stop=(kb == KB - 1))
                mm.then_inc(s["weighed"], 1)

            def project_out(b, t):
                key = ("o", t, 0)
                pe.wait_ge(s["o_sb"], b * NT + t + 1)
                pe.wait_ge(s["recip"], b * NT + t)
                if t == 0:
                    pe.wait_ge(s["max_t"], b + 1)
                claim(b, key)
                pe.matmul(p_m[0:CH, :], den_sel[:, :], o_sb[:, t % 2, :], start=True, stop=True).then_inc(s["den"], 1)
                for m in range(2):
                    mm = pe.matmul(slot(key)[0:CH, m * TT:(m + 1) * TT], wo[:, m * CH:(m + 1) * CH], o_sb[:, t % 2, :],
                                   start=True, stop=True)
                mm.then_inc(s["filled"], 1)

            with pe.Fori(0, B // 2) as bb:
                for par in range(2):
                    b = bb * 2 + par
                    pe.wait_ge(s[f"x{par}"], (bb + 1) * 16)
                    for t in range(NT):
                        project(b, par, t)
                    for i in range(KB // VB):
                        project_values(b, par, i)
                    for i in range(KB):
                        for h in range(L // PAIR):
                            scores_for_max(b, i, h)
                    pe.wait_ge(s["max"], b + 1)
                    pe.wait_ge(s["recip"], b * NT)
                    pe.sem_inc(s["pe_go"], 1)
                    pe.transpose(p_m[0:KB, 0:128], neg_max[:, :], ident[:, :]).then_inc(s["max_mm"], 1)
                    pe.wait_ge(s["max_row"], (b + 1) * 16)
                    pe.sem_inc(s["pe_go"], 1)
                    for n in range(NT * UNITS + LAG + 2):
                        if n < NT * UNITS:
                            scores(b, n)
                        if n >= LAG and n - LAG < NT * UNITS:
                            weigh(b, n - LAG)
                        m = n - LAG - 1
                        if m >= 0 and m % UNITS == UNITS - 1:
                            project_out(b, m // UNITS)

    nc.clear_and_free_semaphores(list(s.values()))
    nc.all_engine_barrier()


def four_layers(nc, x, v, out):
    def sem(name):
        return nc.alloc_semaphore(name=name)

    def scratch(name, shape, dt=FP32):
        return nc.dram_tensor(name, shape, dt, kind="Internal").ap()

    dt_d, dtx_d, xs_d, y_d = (scratch(n + "_scratch", (SEQ, NC, 128, EB, CK)) for n in ("dt", "dtx", "xs", "y"))
    bc_d = scratch("bc_scratch", (SEQ, NC, 96, CK), BF16)
    gate_d = scratch("gate_scratch", (B, NT, 128, EB, TT))
    x1_d, x2_d, x3_d = (scratch(f"x{n}_scratch", (B, C, L)) for n in (1, 2, 3))
    pat_d = [scratch(f"windows{j}_scratch", (B, CB * FLAT[j])) for j in range(3)]
    att_d = [scratch(f"attended{j}_scratch", (B, CB * FLAT[j])) for j in range(3)]
    max2_d = scratch("max2_scratch", (B, 3, L), BF16)
    max3_d = scratch("max3_scratch", (B, L))

    mamba_inputs(nc, sem, x, v["gamma"], v["beta"], v["w_in"], v["conv_w"], v["conv_b"], v["w_xproj"], v["w_dt"],
                 v["b_dt"], dt_d, dtx_d, xs_d, bc_d, gate_d)
    selective_scan(nc, sem, v["a_log"], v["d"], dt_d, dtx_d, xs_d, bc_d, y_d)
    mamba_output(nc, sem, x, v["w_out"], y_d, gate_d, x1_d)
    windows_cut(nc, sem, x1_d, v["w1t"], v["b1"], pat_d)
    windows_attend(nc, sem, v["w2t"], v["b2"], v["wpos"], v["bpos"], v["wse1t"], v["wse2t"], pat_d, att_d)
    windows_fold(nc, sem, x1_d, v["w3t"], v["b3"], att_d, x2_d)
    gated_attention(nc, sem, x2_d, v["wqt"], v["wkt"], v["wvt"], v["wot"], max2_d, x3_d)
    n = v["wtt"].shape[1] // 3
    attention(nc, sem, x3_d, v["wtt"][:, 2 * n:], v["wtt"][:, 0:n], v["wtt"][:, n:2 * n], v["wdt"],
              (v["bt"][2 * n:], v["bt"][0:n], v["bt"][n:2 * n], v["bd"]), max3_d, out)


_PLAIN = {"gamma": "L0_conv_gamma", "beta": "L0_conv_beta", "w_in": "L0_conv_W_in", "conv_w": "L0_conv_conv_w",
          "conv_b": "L0_conv_conv_b", "w_xproj": "L0_conv_W_xproj", "w_dt": "L0_conv_W_dt", "b_dt": "L0_conv_b_dt",
          "a_log": "L0_conv_A_log", "d": "L0_conv_D", "w_out": "L0_conv_W_out", "b1": "L1_conv_b1",
          "b2": "L1_conv_b2", "b3": "L1_conv_b3", "bpos": "L1_conv_bpos", "bt": "L3_conv_bt", "bd": "L3_conv_bd"}
_TURNED = {"w1t": "L1_conv_w1", "w2t": "L1_conv_w2", "w3t": "L1_conv_w3", "wse1t": "L1_conv_wse1",
           "wse2t": "L1_conv_wse2", "wqt": "L2_conv_Wq", "wkt": "L2_conv_Wk", "wvt": "L2_conv_Wv",
           "wot": "L2_conv_Wout", "wtt": "L3_conv_Wt", "wdt": "L3_conv_Wd"}


def kernel(**inputs):
    import numpy as _np
    import concourse.bacc as _bacc
    from concourse import mybir as _mybir
    from concourse.bass_utils import run_bass_kernel_spmd as _run

    nc = _bacc.Bacc("TRN2", target_bir_lowering=False, num_devices=1)
    arrays, views = {}, {}

    def put(name, a):
        a = _np.ascontiguousarray(a)
        arrays[f"in_{name}_dram"] = a
        views[name] = nc.dram_tensor(f"in_{name}_dram", a.shape, _mybir.dt.from_np(a.dtype), kind="ExternalInput").ap()

    x = inputs["x"]
    put("x", _np.asarray(x).reshape(x.shape[0], x.shape[1], -1))
    put("wpos", _np.asarray(inputs["L1_conv_wpos"]).reshape(-1, 9))
    for name, key in _PLAIN.items():
        put(name, inputs[key])
    for name, key in _TURNED.items():
        put(name, _np.asarray(inputs[key]).T)
    shape = views["x"].shape
    out = nc.dram_tensor("out_dram", shape, _mybir.dt.float32, kind="ExternalOutput").ap()
    four_layers(nc, views["x"], views, out)
    r = _run(nc, [arrays], core_ids=[0])
    return _np.asarray(r.results[0]["out_dram"]).reshape(x.shape)
```

```python
import concourse.bass as bass
from concourse import mybir
from contextlib import ExitStack

FP32 = mybir.dt.float32
BF16 = mybir.dt.bfloat16
ALU = mybir.AluOpType
ACT = mybir.ActivationFunctionType
AX = mybir.AxisListType

B, C, L = 4, 192, 4096
CH = C // 2
E, EB = 384, 3
NST = 16
RANK = 12
TT = 512
NT = L // TT
CK = 1024
NC = L // CK
SEQ = 2 * B


def freed(b, t, depth, per_tile, tiles):
    base = b * (per_tile * tiles)
    return base + (t - depth + 1) * per_tile if t >= depth else base


def hold(engine, go, semaphore, value):
    engine.wait_ge(semaphore, value)
    engine.sem_inc(go, 1)


def reach(engine, semaphore, b, c, per_tile, n):
    value = c * per_tile + n
    if isinstance(b, int):
        value += b * NT * per_tile
        if value > 0:
            engine.wait_ge(semaphore, value)
    else:
        assert value > 0
        engine.wait_ge(semaphore, b * (NT * per_tile) + value)


def steps(engine, step, drain):
    for T in range(NT):
        step(0, T)
    with engine.Fori(0, B - 1) as b:
        for T in range(NT, 2 * NT):
            step(b, T)
    for T in range(B * NT, B * NT + drain):
        step(0, T)


def active(b, c):
    return not isinstance(b, int) or 0 <= c < B * NT


def split_tile(b, c):
    return b + c // NT, c % NT


def stored(engine, semaphore, b, c, depth, each):
    n = c // depth * each
    if not isinstance(b, int):
        engine.wait_ge(semaphore, b * (NT // depth * each) + n)
    elif n > 0:
        engine.wait_ge(semaphore, n)


def mamba_inputs(nc, sem, x, gamma, beta, w_in, conv_w, conv_b, w_xproj, w_dt, b_dt,
                 dt_d, dtx_d, xs_d, bc_d, gate_d):
    with ExitStack() as ctx:
        def sb(name, shape, dt=FP32):
            return ctx.enter_context(nc.sbuf_tensor("a_" + name, shape, dt))

        def pb(name, shape):
            return ctx.enter_context(nc.psum_tensor("a_" + name, shape, FP32))

        PAD = 3
        ones = sb("ones_mean", [CH, CH])
        eps = sb("eps", [CH, 1])
        w_in_sb = sb("w_in_sb", [CH, 2, 2 * E])
        gam = sb("gam", [CH, 2])
        bet = sb("bet", [CH, 2])
        bias_in = sb("bias_in", [128, 6])
        cw = sb("cw", [128, EB, 4])
        cb = sb("cb", [128, EB])
        bdt = sb("bdt", [128, EB])
        wx = sb("wx", [128, 2, EB, 128])
        wdt = sb("wdt", [128, 2, E])
        XD = 4
        xt = sb("xt", [CH, XD, 2, TT])
        sq = sb("sq", [CH, 2, TT])
        lnv = sb("lnv", [CH, TT])
        rstd = sb("rstd", [CH, TT])
        xr = sb("xr", [128, XD, EB, TT + 2 * PAD])
        gate = sb("gate", [128, EB, TT])
        xs = sb("xs", [128, XD, 2, EB, TT])
        dbl = sb("dbl", [128, TT])
        part = sb("part", [64, 2, 3, TT], BF16)
        rest = sb("rest", [64, 2, TT])
        ev = sb("ev", [128, 2, EB, 2, TT])
        ew = sb("ew", [128, EB, 2, TT])
        dt = sb("dt", [128, 2, 2, EB, TT])
        dtx = sb("dtx", [128, 2, EB, TT])

        p_stat = pb("p_stat", [128, TT])
        p_in = [pb(f"p_in{i}", [128, TT]) for i in range(2)]
        p_dbl = pb("p_dbl", [128, TT])
        p_dt = pb("p_dt", [128, 2, 2, TT])

        s = {k: sem("a_" + k) for k in (
            "weights", "zeroed", "const", "wg", "bias_mm", "bias", "x0", "x1", "x2", "x3", "mean", "centred",
            "squared", "var", "lnv", "rstd", "normed", "proj", "xr", "gate", "halo", "conv_step", "conv",
            "xs", "xproj", "dbl", "part_step", "parts", "dtproj", "absv", "expv", "onep", "lnw",
            "relu", "fix", "sum", "dt", "dtx", "st_xs0", "st_xs1", "st_xs2", "st_xs3", "st_bc0", "st_bc1",
            "st_gate", "st_dt0", "st_dt1", "st_dtx", "sp_go", "pool_go")}

        block = ctx.enter_context(nc.Block())


        @block.sync
        def _(sp):
            sp.dma_start(w_in_sb[:, :, :], w_in.rearrange("(h p) n -> p h n", h=2)).then_inc(s["weights"], 16)
            sp.dma_start(gam[:, :], gamma.rearrange("(h p) -> p h", h=2), allow_slow_non_contiguous=True).then_inc(s["weights"], 16)
            sp.dma_start(bet[:, :], beta.rearrange("(h p) -> p h", h=2), allow_slow_non_contiguous=True).then_inc(s["weights"], 16)
            sp.dma_start(cw[:, :, :], conv_w.rearrange("(e p) k -> p e k", p=128)).then_inc(s["weights"], 16)
            sp.dma_start(cb[:, :], conv_b.rearrange("(e p) -> p e", p=128), allow_slow_non_contiguous=True).then_inc(s["weights"], 16)
            sp.dma_start(bdt[:, :], b_dt.rearrange("(e p) -> p e", p=128), allow_slow_non_contiguous=True).then_inc(s["weights"], 16)
            hold(sp, s["sp_go"], s["zeroed"], 2)
            wx_v = w_xproj.rearrange("(e p) n -> p e n", p=128)
            for d in range(2):
                sp.dma_start(wx[:, d, :, 32 * d:32 * d + 2 * NST], wx_v[:, :, RANK:]).then_inc(s["weights"], 16)
                sp.dma_start(wx[:, d, :, 64 + 32 * d:64 + 32 * d + RANK], wx_v[:, :, :RANK]).then_inc(s["weights"], 16)
                sp.dma_start(wdt[64 + 32 * d:64 + 32 * d + RANK, d, :], w_dt).then_inc(s["weights"], 16)
            x_v = x.rearrange("b (h p) t -> b p h t", h=2)

            def load(b, c):
                q, j = split_tile(b, c)
                src = x_v[bass.ds(q, 1), :, :, j * TT:(j + 1) * TT].rearrange("a p h t -> (a p) h t")
                reach(sp, s["proj"], b, c - XD, 6, 6)
                sp.sem_inc(s["sp_go"], 1)
                sp.dma_start(xt[:, c % XD, :, :], src).then_inc(s[f"x{c % XD}"], 16)

            def store_pair(b, c, dram, tile, sem_st):
                q, j = split_tile(b, c)
                for d in range(2):
                    jj = j if d == 0 else NT - 1 - j
                    k, h = jj // 2, jj % 2
                    sp.dma_start(dram[bass.ds(q + B * d, 1), k, :, :, h * TT:(h + 1) * TT].rearrange(
                        "a p e t -> (a p) e t"), tile[:, d, :, :]).then_inc(sem_st, 16)

            def step(b, T):
                if active(b, T) and T < B * NT:
                    load(b, T)
                c = T - 5
                if active(b, c):
                    reach(sp, s["xs"], b, c, EB, EB)
                    sp.sem_inc(s["sp_go"], 1)
                    store_pair(b, c, xs_d, xs[:, c % XD], s[f"st_xs{c % XD}"])
                c = T - 6
                if active(b, c):
                    reach(sp, s["parts"], b, c, 1, 1)
                    sp.sem_inc(s["sp_go"], 1)
                    q, j = split_tile(b, c)
                    for d in range(2):
                        jj = j if d == 0 else NT - 1 - j
                        k, h = jj // 2, jj % 2
                        for i in range(3):
                            sp.dma_start(bc_d[bass.ds(q + B * d, 1), k, 32 * i:32 * i + 32, h * TT:(h + 1) * TT
                                              ].rearrange("a p t -> (a p) t"),
                                         part[32 * d:32 * d + 32, c % 2, i, :]).then_inc(s[f"st_bc{c % 2}"], 16)
                c = T - 2
                if active(b, c):
                    reach(sp, s["gate"], b, c, EB, EB)
                    sp.sem_inc(s["sp_go"], 1)
                    q, j = split_tile(b, c)
                    sp.dma_start(gate_d[bass.ds(q, 1), j, :, :, :].rearrange("a p e t -> (a p) e t"),
                                 gate[:, :, :]).then_inc(s["st_gate"], 16)
                c = T - 7
                if active(b, c):
                    reach(sp, s["dt"], b, c, EB, EB)
                    sp.sem_inc(s["sp_go"], 1)
                    store_pair(b, c, dt_d, dt[:, c % 2], s[f"st_dt{c % 2}"])
                    reach(sp, s["dtx"], b, c, EB, EB)
                    sp.sem_inc(s["sp_go"], 1)
                    store_pair(b, c, dtx_d, dtx, s["st_dtx"])

            steps(sp, step, 7)
            for i in range(XD):
                sp.wait_ge(s[f"st_xs{i}"], B * NT // XD * 32)
            for i in range(2):
                sp.wait_ge(s[f"st_bc{i}"], B * NT // 2 * 96)
                sp.wait_ge(s[f"st_dt{i}"], B * NT // 2 * 32)
            sp.wait_ge(s["st_gate"], B * NT * 16)
            sp.wait_ge(s["st_dtx"], B * NT * 32)

        @block.gpsimd
        def _(pool):
            pool.memset(wx[:, :, :, :], 0.0).then_inc(s["zeroed"], 1)
            pool.memset(wdt[:, :, :], 0.0).then_inc(s["zeroed"], 1)
            pool.memset(ones[:, :], 1.0 / C).then_inc(s["const"], 1)
            pool.memset(eps[:, :], 1e-5).then_inc(s["const"], 1)

            def edges(b, c):
                first = c % NT == 0
                if c > 0:
                    reach(pool, s["conv"], b, c - XD, 6, 0)
                    if c < B * NT:
                        reach(pool, s["xr"], b, c, EB, EB)
                    pool.sem_inc(s["pool_go"], 1)
                    behind = xr[:, (c - 1) % XD, :, PAD + TT:]
                    if first:
                        pool.memset(behind, 0.0).then_inc(s["halo"], 1)
                    else:
                        pool.tensor_scalar(behind, xr[:, c % XD, :, PAD:2 * PAD], 1.0, 0.0, ALU.mult, ALU.add
                                           ).then_inc(s["halo"], 1)
                else:
                    pool.sem_inc(s["halo"], 1)
                if c < B * NT:
                    reach(pool, s["conv"], b, c - XD + 1, 6, 0)
                    pool.sem_inc(s["pool_go"], 1)
                    before = xr[:, c % XD, :, 0:PAD]
                    if first:
                        pool.memset(before, 0.0).then_inc(s["halo"], 1)
                    else:
                        pool.tensor_scalar(before, xr[:, (c - 1) % XD, :, TT:PAD + TT], 1.0, 0.0, ALU.mult, ALU.add
                                           ).then_inc(s["halo"], 1)
                else:
                    pool.sem_inc(s["halo"], 1)

            def split_bc(b, c):
                reach(pool, s["dbl"], b, c, 1, 1)
                stored(pool, s[f"st_bc{c % 2}"], b, c, 2, 96)
                bc = dbl[0:64, :]
                hi, mid, lo = (part[:, c % 2, k, :] for k in range(3))
                r1, r2 = rest[:, 0, :], rest[:, 1, :]
                pool.sem_inc(s["pool_go"], 1)
                pool.tensor_scalar(hi, bc, 1.0, 0.0, ALU.mult, ALU.add).then_inc(s["part_step"], 1)
                reach(pool, s["part_step"], b, c, 4, 1)
                pool.tensor_tensor(r1, bc, hi, ALU.subtract).then_inc(s["part_step"], 1)
                reach(pool, s["part_step"], b, c, 4, 2)
                pool.sem_inc(s["pool_go"], 1)
                pool.tensor_scalar(mid, r1, 1.0, 0.0, ALU.mult, ALU.add).then_inc(s["part_step"], 1)
                reach(pool, s["part_step"], b, c, 4, 3)
                reach(pool, s["parts"], b, c, 1, 0)
                pool.tensor_tensor(r2, r1, mid, ALU.subtract).then_inc(s["part_step"], 1)
                reach(pool, s["part_step"], b, c, 4, 4)
                pool.sem_inc(s["pool_go"], 1)
                pool.tensor_scalar(lo, r2, 1.0, 0.0, ALU.mult, ALU.add).then_inc(s["parts"], 1)

            def step(b, T):
                c = T - 2
                if active(b, c) or c == B * NT:
                    edges(b, c)
                c = T - 5
                if active(b, c):
                    split_bc(b, c)
                c = T - 6
                if active(b, c):
                    for e in range(EB):
                        reach(pool, s["lnw"], b, c, EB, e + 1)
                        pool.tensor_tensor(ew[:, e], ew[:, e], ev[:, c % 2, e], ALU.subtract).then_inc(s["sum"], 1)
                        reach(pool, s["sum"], b, c, EB, e + 1)
                        pool.tensor_tensor(dt[:, c % 2, :, e, :], ew[:, e], dt[:, c % 2, :, e, :], ALU.add
                                           ).then_inc(s["dt"], 1)
                c = T - 5
                if active(b, c):
                    for e in range(EB):
                        reach(pool, s["expv"], b, c, EB, e + 1)
                        reach(pool, s["dt"], b, c - 1, EB, e + 1)
                        pool.sem_inc(s["pool_go"], 1)
                        pool.tensor_scalar(ew[:, e], ev[:, c % 2, e], 1.0, 1.0, ALU.mult, ALU.add
                                           ).then_inc(s["onep"], 1)

            steps(pool, step, 6)

        @block.scalar
        def _(act):
            act.wait_ge(s["bias_mm"], 1)
            act.wait_ge(s["const"], 2)
            act.activation(bias_in[:, :], p_dbl[:, 0:6], ACT.Identity).then_inc(s["bias"], 1)
            act.wait_ge(s["bias"], 1)

            def project(b, c, m):
                reach(act, s["proj"], b, c, 6, m + 1)
                if m < EB:
                    reach(act, s["conv"], b, c - XD + 1, 6, 0)
                    act.activation(xr[:, c % XD, m, PAD:PAD + TT], p_in[m % 2][:, :], ACT.Identity,
                                   bias=bias_in[:, m:m + 1]).then_inc(s["xr"], 1)
                else:
                    if m == EB:
                        stored(act, s["st_gate"], b, c, 1, 16)
                    act.activation(gate[:, m - EB, :], p_in[m % 2][:, :], ACT.Silu,
                                   bias=bias_in[:, m:m + 1]).then_inc(s["gate"], 1)

            def step(b, T):
                c = T - 5
                if active(b, c):
                    reach(act, s["xproj"], b, c, 1, 1)
                    reach(act, s["dtproj"], b, c, EB, 0)
                    reach(act, s["part_step"], b, c - 1, 4, 2)
                    act.activation(dbl[:, :], p_dbl[:, :], ACT.Identity).then_inc(s["dbl"], 1)
                c = T - 1
                if active(b, c):
                    reach(act, s["var"], b, c, 1, 1)
                    reach(act, s["rstd"], b, c, 1, 0)
                    act.activation(lnv[:, :], p_stat[0:CH, :], ACT.Ln, bias=eps[:, 0:1]).then_inc(s["lnv"], 1)
                c = T - 6
                if active(b, c):
                    for e in range(EB):
                        reach(act, s["fix"], b, c, EB, e + 1)
                        act.activation(ew[:, e], ew[:, e], ACT.Ln).then_inc(s["lnw"], 1)
                c = T - 1
                if active(b, c):
                    reach(act, s["lnv"], b, c, 1, 1)
                    reach(act, s["normed"], b, c, 1, 0)
                    act.activation(rstd[:, :], lnv[:, :], ACT.Exp, scale=-0.5).then_inc(s["rstd"], 1)
                for e in range(EB):
                    c = T - 5
                    if active(b, c):
                        i = (EB * c + e) % 2
                        reach(act, s["dtproj"], b, c, EB, e + 1)
                        reach(act, s["sum"], b, c - 2, EB, e + 1)
                        act.activation(ev[:, c % 2, e], p_dt[:, i], ACT.Abs, bias=bdt[:, e:e + 1]).then_inc(s["absv"], 1)
                        if e == 0:
                            stored(act, s[f"st_dt{c % 2}"], b, c, 2, 32)
                        act.activation(dt[:, c % 2, :, e, :], p_dt[:, i], ACT.Relu, bias=bdt[:, e:e + 1]
                                       ).then_inc(s["relu"], 1)
                    if active(b, T - 1) and e >= 1:
                        for m in ((0, 1), (2,))[e - 1]:
                            project(b, T - 1, m)
                c = T - 5
                if active(b, c):
                    for e in range(EB):
                        reach(act, s["absv"], b, c, EB, e + 1)
                        act.activation(ev[:, c % 2, e], ev[:, c % 2, e], ACT.Exp, scale=-1.0).then_inc(s["expv"], 1)
                c = T
                if active(b, c):
                    reach(act, s["centred"], b, c, 1, 1)
                    reach(act, s["var"], b, c, 1, 0)
                    act.activation(sq[:, :, :], xt[:, c % XD], ACT.Square).then_inc(s["squared"], 1)
                c = T - 4
                if active(b, c):
                    for e in range(EB):
                        reach(act, s["conv"], b, c, 6, 2 * e + 2)
                        act.activation(xs[:, c % XD, :, e, :], xs[:, c % XD, :, e, :], ACT.Silu, bias=cb[:, e:e + 1]
                                       ).then_inc(s["xs"], 1)
                c = T - 1
                if active(b, c):
                    for m in range(3, 6):
                        project(b, c, m)

            steps(act, step, 6)

        @block.vector
        def _(dve):
            dve.wait_ge(s["weights"], 12 * 16)
            dve.wait_ge(s["bias_mm"], 1)
            for h in range(2):
                dve.tensor_scalar(w_in_sb[:, h, :], w_in_sb[:, h, :], gam[:, h:h + 1], None, ALU.mult).then_inc(s["wg"], 1)
            dve.wait_ge(s["const"], 2)

            def tap(b, c, w, k):
                e, d = k // 2, k % 2
                if d == 0:
                    src = xr[:, c % XD, e, w:w + TT]
                else:
                    src = xr[:, c % XD, e, 2 * PAD - w:2 * PAD - w + TT][:, ::-1]
                out = xs[:, c % XD, d, e, :]
                wt = cw[:, e, w:w + 1]
                if w == 0:
                    if k == 0:
                        reach(dve, s["halo"], b, c + 1, 2, 2 if c + 1 == B * NT else 1)
                        reach(dve, s["halo"], b, c, 2, 2)
                        stored(dve, s[f"st_xs{c % XD}"], b, c, XD, 32)
                        reach(dve, s["xproj"], b, c - XD, 1, 1)
                        reach(dve, s["dtx"], b, c - XD, EB, EB)
                    dve.tensor_scalar(out, src, wt, None, ALU.mult).then_inc(s["conv_step"], 1)
                else:
                    reach(dve, s["conv_step"], b, c, 18, (w - 1) * 6 + k + 1)
                    ins = dve.scalar_tensor_tensor(out, src, wt, out, ALU.mult, ALU.add)
                    ins.then_inc(s["conv"] if w == 3 else s["conv_step"], 1)

            def step(b, T):
                for n in range(24):
                    if n == 8 and active(b, T - 1):
                        c = T - 1
                        reach(dve, s["rstd"], b, c, 1, 1)
                        dve.tensor_tensor(xt[:, c % XD], xt[:, c % XD], rstd[:, None, :].broadcast_to([CH, 2, TT]),
                                          ALU.mult).then_inc(s["normed"], 1)
                    if n == 12 and active(b, T):
                        c = T
                        reach(dve, s["mean"], b, c, 1, 1)
                        dve.tensor_tensor(xt[:, c % XD], xt[:, c % XD], p_stat[0:CH, None, :].broadcast_to([CH, 2, TT]),
                                          ALU.subtract).then_inc(s["centred"], 1)
                    if active(b, T - 3):
                        tap(b, T - 3, n // 6, n % 6)
                c = T - 6
                if active(b, c):
                    for e in range(EB):
                        reach(dve, s["dt"], b, c, EB, e + 1)
                        if e == 0:
                            stored(dve, s["st_dtx"], b, c, 1, 32)
                        dve.tensor_tensor(dtx[:, :, e, :], dt[:, c % 2, :, e, :], xs[:, c % XD, :, e, :], ALU.mult
                                          ).then_inc(s["dtx"], 1)
                c = T - 5
                if active(b, c):
                    for e in range(EB):
                        reach(dve, s["onep"], b, c, EB, e + 1)
                        dve.scalar_tensor_tensor(ev[:, c % 2, e], ew[:, e], 1.0, ev[:, c % 2, e],
                                                 ALU.subtract, ALU.subtract).then_inc(s["fix"], 1)

            steps(dve, step, 6)

        @block.tensor
        def _(pe):
            pe.wait_ge(s["weights"], 12 * 16)
            pe.wait_ge(s["const"], 2)
            for m in range(6):
                for h in range(2):
                    mm = pe.matmul(p_dbl[:, m:m + 1], w_in_sb[:, h, m * 128:(m + 1) * 128], bet[:, h:h + 1],
                                   start=(h == 0), stop=(h == 1))
            mm.then_inc(s["bias_mm"], 1)
            pe.wait_ge(s["bias"], 1)
            pe.wait_ge(s["wg"], 2)

            def statistics(rhs, done):
                for h in range(2):
                    mm = pe.matmul(p_stat[0:CH, :], ones[:, :], rhs[:, h, :], start=(h == 0), stop=(h == 1))
                mm.then_inc(done, 1)

            def project(b, c, blocks):
                for m in blocks:
                    name, cc, n = (("gate", c - 1, 2), ("gate", c - 1, 3), ("xr", c, 1), ("xr", c, 2),
                                   ("xr", c, 3), ("gate", c, 1))[m]
                    reach(pe, s[name], b, cc, EB, n)
                    for h in range(2):
                        mm = pe.matmul(p_in[m % 2][:, :], w_in_sb[:, h, m * 128:(m + 1) * 128],
                                       xt[:, c % XD, h, :], start=(h == 0), stop=(h == 1))
                    mm.then_inc(s["proj"], 1)

            def dt_projection(b, c, blocks):
                for e in blocks:
                    reach(pe, s["relu"], b, c, EB, e - 1)
                    for d in range(2):
                        mm = pe.matmul(p_dt[:, (EB * c + e) % 2, d, :], wdt[:, d, e * 128:(e + 1) * 128], dbl[:, :],
                                       start=True, stop=True)
                    mm.then_inc(s["dtproj"], 1)

            def x_projection(b, c):
                reach(pe, s["dbl"], b, c, 1, 0)
                for e in range(EB):
                    reach(pe, s["xs"], b, c, EB, e + 1)
                    for d in range(2):
                        mm = pe.matmul(p_dbl[:, :], wx[:, d, e, :], xs[:, c % XD, d, e, :],
                                       start=(e == 0 and d == 0), stop=(e == EB - 1 and d == 1))
                mm.then_inc(s["xproj"], 1)

            def step(b, T):
                if active(b, T - 5):
                    reach(pe, s["dbl"], b, T - 5, 1, 1)
                    dt_projection(b, T - 5, (0, 1))
                if active(b, T):
                    n = T // XD * 16 + 16
                    pe.wait_ge(s[f"x{T % XD}"], n if isinstance(b, int) else b * (NT // XD * 16) + n)
                    reach(pe, s["lnv"], b, T, 1, 0)
                    statistics(xt[:, T % XD], s["mean"])
                if active(b, T - 1):
                    reach(pe, s["normed"], b, T - 1, 1, 1)
                    project(b, T - 1, (0, 1))
                if active(b, T - 5):
                    dt_projection(b, T - 5, (2,))
                if active(b, T - 1):
                    project(b, T - 1, (2, 3, 4))
                if active(b, T):
                    reach(pe, s["squared"], b, T, 1, 1)
                    statistics(sq, s["var"])
                if active(b, T - 4):
                    x_projection(b, T - 4)
                if active(b, T - 1):
                    project(b, T - 1, (5,))

            steps(pe, step, 6)

    nc.clear_and_free_semaphores(list(s.values()))
    nc.all_engine_barrier()


def selective_scan(nc, sem, a_log, d_skip, dt_d, dtx_d, xs_d, bc_d, y_d):
    with ExitStack() as ctx:
        def sb(name, shape, dt=FP32):
            return ctx.enter_context(nc.sbuf_tensor("b_" + name, shape, dt))

        TPC = NST * EB
        TPS = NC * TPC
        NPS = NC * NST
        ND, NU, NH, NY = 4, 4, 4, 4

        ident = sb("ident", [128, 128])
        diag_d = sb("diag_d", [128, EB, 128])
        sel = sb("sel", [96, 2 * NST, 128], BF16)
        a_neg = sb("a_neg", [128, EB, NST])
        dsk = sb("dsk", [128, EB])
        dt = sb("dt", [128, 2, EB, CK])
        dtx = sb("dtx", [128, 2, EB, CK])
        xs = sb("xs", [128, EB, CK])
        bc = sb("bc", [96, 2, CK], BF16)
        decay = sb("decay", [128, ND, CK])
        inp = sb("inp", [128, NU, CK])
        hid = sb("hid", [128, NH, CK])
        hc = sb("hc", [128, NY, CK])
        b_row = sb("b_row", [128, 4, CK])
        c_row = sb("c_row", [128, 4, CK])
        carry = sb("carry", [128, TPC])
        y_sb = sb("y_sb", [128, EB, CK])
        p_row = ctx.enter_context(nc.psum_tensor("b_p_row", [128, CK], FP32))
        p_y = ctx.enter_context(nc.psum_tensor("b_p_y", [128, EB, CK], FP32))

        s = {k: sem("b_" + k) for k in (
            "a_loaded", "a_exp", "a_neg", "made", "ident", "sel", "diag", "dt0", "dt1", "dtx0", "dtx1", "xs",
            "bc0", "bc1", "spread", "taken", "decay", "input", "scan", "product", "summed", "skip",
            "carried", "y_out", "stored", "sp_go")}

        block = ctx.enter_context(nc.Block())

        def rows(engine, step, drain):
            for M in range(NPS):
                step(0, M)
            with engine.Fori(0, SEQ - 1) as q:
                for M in range(NPS, 2 * NPS):
                    step(q, M)
            for M in range(SEQ * NPS, SEQ * NPS + drain):
                step(0, M)

        def there(q, m):
            return not isinstance(q, int) or 0 <= m < SEQ * NPS

        def wait(engine, name, q, per_sequence, value):
            if not isinstance(q, int):
                assert value > 0
                engine.wait_ge(s[name], q * per_sequence + value)
            elif value > 0:
                engine.wait_ge(s[name], value)

        def one(dram, q, c):
            return dram[bass.ds(q, 1), c, :, :, :].rearrange("a p e t -> (a p) e t")

        def load(sp, q, c):
            sp.dma_start(bc[:, c % 2, :], bc_d[bass.ds(q, 1), c, :, :].rearrange("a p t -> (a p) t")
                         ).then_inc(s[f"bc{c % 2}"], 16)
            sp.dma_start(dt[:, c % 2, :, :], one(dt_d, q, c)).then_inc(s[f"dt{c % 2}"], 16)
            sp.dma_start(dtx[:, c % 2, :, :], one(dtx_d, q, c)).then_inc(s[f"dtx{c % 2}"], 16)

        def load_x(sp, q, c):
            sp.dma_start(xs[:, :, :], one(xs_d, q, c)).then_inc(s["xs"], 16)

        def turn(sp, q, c, last):
            hold(sp, s["sp_go"], s["skip"], q * NC + c + 1)
            if c + 1 < NC:
                load_x(sp, q, c + 1)
            elif not last:
                load_x(sp, q + 1, 0)
            if c + 2 < NC or not last:
                hold(sp, s["sp_go"], s["decay"], q * TPS + (c + 1) * TPC)
                hold(sp, s["sp_go"], s["input"], q * TPS + (c + 1) * TPC)
                hold(sp, s["sp_go"], s["spread"], q * (2 * NPS) + (c + 1) * 2 * NST)
                load(sp, q + (c + 2) // NC, (c + 2) % NC)
            hold(sp, s["sp_go"], s["y_out"], q * (NC * EB) + (c + 1) * EB)
            sp.dma_start(one(y_d, q, c), y_sb[:, :, :]).then_inc(s["stored"], 16)

        @block.sync
        def _(sp):
            sp.dma_start(a_neg[:, :, :], a_log.rearrange("(e p) n -> p e n", p=128)).then_inc(s["a_loaded"], 16)
            sp.dma_start(dsk[:, :], d_skip.rearrange("(e p) -> p e", p=128),
                         allow_slow_non_contiguous=True).then_inc(s["a_loaded"], 16)
            load(sp, 0, 0)
            load_x(sp, 0, 0)
            load(sp, 0, 1)
            with sp.Fori(0, SEQ - 1) as q:
                for c in range(NC):
                    turn(sp, q, c, False)
            for c in range(NC):
                turn(sp, SEQ - 1, c, True)
            hold(sp, s["sp_go"], s["stored"], SEQ * NC * 16)

        @block.gpsimd
        def _(pool):
            pool.memset(ident[:, :], 0.0).then_inc(s["made"], 1)
            pool.memset(sel[:, :, :], 0.0).then_inc(s["made"], 1)
            pool.wait_ge(s["made"], 2)
            pool.affine_select(out=ident[:, :], in_=ident[:, :], compare_op=ALU.not_equal, fill=1.0, base=0,
                               pattern=[[-1, 128]], channel_multiplier=1).then_inc(s["ident"], 1)
            for k in range(3):
                pool.affine_select(out=sel[:, :, :], in_=sel[:, :, :], compare_op=ALU.not_equal, fill=1.0,
                                   base=-32 * k, pattern=[[-1, 2 * NST], [0, 128]],
                                   channel_multiplier=1).then_inc(s["sel"], 1)
                pool.wait_ge(s["sel"], k + 1)

            def step(q, m):
                c = m // NST
                for e in range(EB):
                    k = m * EB + e
                    if k % TPC == 0:
                        wait(pool, f"dtx{c % 2}", q, NC // 2 * 16, (c // 2 + 1) * 16)
                    if e == 0:
                        wait(pool, "taken", q, 2 * NPS, 2 * m + 1)
                    wait(pool, "scan", q, TPS, k - NU + 1)
                    pool.tensor_tensor(inp[:, k % NU, :], dtx[:, c % 2, e, :], b_row[:, m % 4, :],
                                       ALU.mult).then_inc(s["input"], 1)

            rows(pool, step, 0)

        @block.scalar
        def _(act):
            act.wait_ge(s["a_loaded"], 32)
            act.activation(a_neg[:, :, :], a_neg[:, :, :], ACT.Exp).then_inc(s["a_exp"], 1)
            act.wait_ge(s["a_exp"], 1)
            act.activation(a_neg[:, :, :], a_neg[:, :, :], ACT.Copy, scale=-1.0).then_inc(s["a_neg"], 1)
            act.wait_ge(s["a_neg"], 1)

            def take(q, m, row):
                wait(act, "spread", q, 2 * NPS, 2 * m + row + 1)
                if row == 0:
                    wait(act, "input", q, TPS, (m - 3) * EB)
                    out = b_row[:, m % 4, :]
                else:
                    wait(act, "product", q, TPS, (m - 3) * EB)
                    out = c_row[:, m % 4, :]
                act.activation(out, p_row[:, :], ACT.Copy).then_inc(s["taken"], 1)

            def keep_state(q, k):
                wait(act, "scan", q, TPS, k + 1)
                act.activation(carry[:, k % TPC:k % TPC + 1], hid[:, k % NH, CK - 1:CK],
                               ACT.Copy).then_inc(s["carried"], 1)

            def y_out(q, c):
                wait(act, "summed", q, TPS, (c + 1) * TPC)
                wait(act, "stored", q, NC * 16, c * 16)
                for e in range(EB):
                    act.activation(y_sb[:, e, :], p_y[:, e, :], ACT.Copy).then_inc(s["y_out"], 1)

            def step(q, M):
                m = M - 1
                c, n = m // NST, m % NST
                for e in range(EB):
                    k = EB * m + e
                    if there(q, m):
                        if k % TPC == 0:
                            wait(act, f"dt{c % 2}", q, NC // 2 * 16, (c // 2 + 1) * 16)
                        wait(act, "scan", q, TPS, k - ND + 1)
                        act.activation(decay[:, k % ND, :], dt[:, c % 2, e, :], ACT.Exp,
                                       scale=a_neg[:, e, n:n + 1]).then_inc(s["decay"], 1)
                    if there(q, (k - 2) // EB):
                        keep_state(q, k - 2)
                    if e >= 1 and there(q, M):
                        take(q, M, e - 1)
                if n == 0 and m > 0:
                    y_out(q, c - 1)

            rows(act, step, 2)

        @block.vector
        def _(dve):
            dve.wait_ge(s["a_loaded"], 32)
            dve.wait_ge(s["ident"], 1)
            for e in range(EB):
                dve.tensor_scalar(diag_d[:, e, :], ident[:, :], dsk[:, e:e + 1], None, ALU.mult).then_inc(s["diag"], 1)

            def product(q, k):
                m = k // EB
                wait(dve, "scan", q, TPS, k + 1)
                wait(dve, "taken", q, 2 * NPS, 2 * m + 2)
                wait(dve, "summed", q, TPS, k - NY + 1)
                dve.tensor_tensor(hc[:, k % NY, :], hid[:, k % NH, :], c_row[:, m % 4, :],
                                  ALU.mult).then_inc(s["product"], 1)

            def step(q, m):
                for k in range(EB * m, EB * m + EB):
                    c = k // TPC
                    if there(q, m):
                        wait(dve, "decay", q, TPS, k + 1)
                        wait(dve, "input", q, TPS, k + 1)
                        wait(dve, "carried", q, TPS, k - NH + 1)
                        wait(dve, "product", q, TPS, k - NH + 1)
                        start = 0.0 if c % NC == 0 else carry[:, k % TPC:k % TPC + 1]
                        dve.tensor_tensor_scan(hid[:, k % NH, :], decay[:, k % ND, :], inp[:, k % NU, :], start,
                                               ALU.mult, ALU.add).then_inc(s["scan"], 1)
                    if there(q, (k - 1) // EB):
                        product(q, k - 1)

            rows(dve, step, 1)

        @block.tensor
        def _(pe):
            pe.wait_ge(s["sel"], 3)
            pe.wait_ge(s["diag"], EB)

            def spread(q, m, row):
                c, n = m // NST, m % NST
                if row == 0 and n == 0:
                    wait(pe, f"bc{c % 2}", q, NC // 2 * 16, (c // 2 + 1) * 16)
                wait(pe, "taken", q, 2 * NPS, 2 * m + row)
                for h in range(2):
                    mm = pe.matmul(p_row[:, h * 512:(h + 1) * 512], sel[:, n + NST * row, :],
                                   bc[:, c % 2, h * 512:(h + 1) * 512], start=True, stop=True)
                mm.then_inc(s["spread"], 1)

            def skip(q, c):
                wait(pe, "xs", q, NC * 16, (c + 1) * 16)
                for e in range(EB):
                    wait(pe, "y_out", q, NC * EB, (c - 1) * EB + e + 1)
                    for h in range(2):
                        mm = pe.matmul(p_y[:, e, h * 512:(h + 1) * 512], diag_d[:, e, :],
                                       xs[:, e, h * 512:(h + 1) * 512], start=True, stop=False)
                mm.then_inc(s["skip"], 1)

            def add_state(q, k):
                e, last = k % EB, k % TPC >= TPC - EB
                wait(pe, "product", q, TPS, k + 1)
                for h in range(2):
                    mm = pe.matmul(p_y[:, e, h * 512:(h + 1) * 512], ident[:, :],
                                   hc[:, k % NY, h * 512:(h + 1) * 512], start=False, stop=last)
                mm.then_inc(s["summed"], 1)

            def step(q, M):
                m = M - 2
                if there(q, M):
                    spread(q, M, 0)
                if there(q, m):
                    if m % NST == 0:
                        skip(q, m // NST)
                    add_state(q, EB * m)
                if there(q, M):
                    spread(q, M, 1)
                if there(q, m):
                    add_state(q, EB * m + 1)
                    add_state(q, EB * m + 2)

            rows(pe, step, 2)

    nc.clear_and_free_semaphores(list(s.values()))
    nc.all_engine_barrier()


def mamba_output(nc, sem, x, w_out, y_d, gate_d, x1_d):
    with ExitStack() as ctx:
        def sb(name, shape, dt=FP32):
            return ctx.enter_context(nc.sbuf_tensor("c_" + name, shape, dt))

        D = 4
        w_sb = sb("w", [128, EB, C])
        yf = sb("yf", [128, D, EB, TT])
        yr = sb("yr", [128, D, EB, TT])
        gt = sb("gt", [128, D, EB, TT])
        xt = sb("xt", [CH, D, 2, TT])
        out = sb("out", [CH, D, 2, TT])
        p_o = ctx.enter_context(nc.psum_tensor("c_p_o", [128, 4, 2, TT], FP32))
        s = {k: sem("c_" + k) for k in ("weights", "in0", "in1", "in2", "in3", "both", "gated", "mm", "out",
                                        "st0", "st1", "st2", "st3", "sp_go")}
        block = ctx.enter_context(nc.Block())
        x_v = x.rearrange("b (h p) t -> b p h t", h=2)
        o_v = x1_d.rearrange("b (h p) t -> b p h t", h=2)
        NL = 4
        LATE = 3

        @block.sync
        def _(sp):
            sp.dma_start(w_sb[:, :, :], w_out.rearrange("(e p) n -> p e n", p=128)).then_inc(s["weights"], 16)

            def load(b, c):
                q, j = split_tile(b, c)
                jr = NT - 1 - j
                i = c % D
                ld = s[f"in{i}"]
                reach(sp, s["out"], b, c - D, 2, 2)
                sp.sem_inc(s["sp_go"], 1)
                sp.dma_start(yf[:, i, :, :], y_d[bass.ds(q, 1), j // 2, :, :, j % 2 * TT:(j % 2 + 1) * TT].rearrange(
                    "a p e t -> (a p) e t")).then_inc(ld, 16)
                sp.dma_start(yr[:, i, :, :], y_d[bass.ds(q + B, 1), jr // 2, :, :, jr % 2 * TT:(jr % 2 + 1) * TT
                                                 ].rearrange("a p e t -> (a p) e t")).then_inc(ld, 16)
                sp.dma_start(gt[:, i, :, :], gate_d[bass.ds(q, 1), j, :, :, :].rearrange("a p e t -> (a p) e t")
                             ).then_inc(ld, 16)
                sp.dma_start(xt[:, i, :, :], x_v[bass.ds(q, 1), :, :, j * TT:(j + 1) * TT].rearrange(
                    "a p h t -> (a p) h t")).then_inc(ld, 16)

            def step(b, T):
                if active(b, T):
                    load(b, T)
                c = T - LATE
                if active(b, c):
                    q, j = split_tile(b, c)
                    reach(sp, s["out"], b, c, 2, 2)
                    sp.sem_inc(s["sp_go"], 1)
                    sp.dma_start(o_v[bass.ds(q, 1), :, :, j * TT:(j + 1) * TT].rearrange("a p h t -> (a p) h t"),
                                 out[:, c % D, :, :]).then_inc(s[f"st{c % D}"], 16)

            steps(sp, step, LATE)
            for i in range(D):
                sp.wait_ge(s[f"st{i}"], B * NT // D * 16)

        @block.vector
        def _(dve):
            def step(b, T):
                c = T
                if active(b, c):
                    i = c % D
                    stored(dve, s[f"in{i}"], b, c + D, D, 16 * NL)
                    dve.tensor_tensor(yf[:, i, :, :], yf[:, i, :, :], yr[:, i, :, ::-1], ALU.add).then_inc(s["both"], 1)
                    reach(dve, s["both"], b, c, 1, 1)
                    dve.tensor_tensor(yf[:, i, :, :], yf[:, i, :, :], gt[:, i, :, :], ALU.mult).then_inc(s["gated"], 1)
                c = T - 1
                if active(b, c):
                    i = c % D
                    stored(dve, s[f"st{i}"], b, c, D, 16)
                    for m in range(2):
                        reach(dve, s["mm"], b, c, 2, m + 1)
                        dve.scalar_tensor_tensor(out[:, i, m, :], p_o[0:CH, c % 4, m, :], 0.5, xt[:, i, m, :],
                                                 ALU.mult, ALU.add).then_inc(s["out"], 1)

            steps(dve, step, 1)

        @block.tensor
        def _(pe):
            pe.wait_ge(s["weights"], 16)

            def step(b, c):
                reach(pe, s["gated"], b, c, 1, 1)
                reach(pe, s["out"], b, c - 4, 2, 2)
                for m in range(2):
                    for e in range(EB):
                        mm = pe.matmul(p_o[0:CH, c % 4, m, :], w_sb[:, e, m * CH:(m + 1) * CH], yf[:, c % D, e, :],
                                       start=(e == 0), stop=(e == EB - 1))
                    mm.then_inc(s["mm"], 1)

            steps(pe, step, 0)

    nc.clear_and_free_semaphores(list(s.values()))
    nc.all_engine_barrier()


CB = 64
WINDOWS = (4, 8, 12)
STEP = tuple(64 // n for n in WINDOWS)
SIDE = tuple(64 // n + 64 % n for n in WINDOWS)
AREA = tuple(k * k for k in SIDE)
NWIN = tuple(n * n for n in WINDOWS)
FLAT = tuple(AREA[j] * NWIN[j] for j in range(3))
IMG = 64


def windows_cut(nc, sem, x1_d, w1t, b1, pat_d):
    with ExitStack() as ctx:
        def sb(name, shape, dt=FP32):
            return ctx.enter_context(nc.sbuf_tensor("d_" + name, shape, dt))

        w = sb("w", [CH, 2, CB])
        bias = sb("bias", [CB, 1])
        xt = sb("xt", [CH, 4, 2, TT])
        xc = sb("xc", [CB, 2, L])
        flat = [sb(f"flat{j}", [CB, FLAT[j]]) for j in range(3)]
        p = ctx.enter_context(nc.psum_tensor("d_p", [CB, 4, TT], FP32))
        s = {k: sem("d_" + k) for k in ("weights", "x0", "x1", "x2", "x3", "mm", "conv", "cut0", "cut1", "cut2",
                                        "st0", "st1", "st2", "sp_go", "pe_go", "pool_go")}
        block = ctx.enter_context(nc.Block())
        x_v = x1_d.rearrange("b (g p) t -> b p g t", g=2)

        def cutting(eng, copy, b, j, par):
            n, k, st = WINDOWS[j], SIDE[j], STEP[j]
            src0 = xc[:, par, :]
            d0 = flat[j][:, :]
            for i in range(k):
                src = bass.AP(src0.tensor, src0.offset + i * IMG, [src0.ap[0], [st * IMG, n], [1, k], [st, n]])
                dst = bass.AP(d0.tensor, d0.offset + i * k * n * n, [d0.ap[0], [n, n], [n * n, k], [1, n]])
                copy(dst, src).then_inc(s[f"cut{j}"], 1)

        @block.sync
        def _(sp):
            sp.dma_start(w[:, :, :], w1t.rearrange("(g p) n -> p g n", g=2)).then_inc(s["weights"], 16)
            sp.dma_start(bias[:, :], b1.rearrange("(p a) -> p a", a=1)).then_inc(s["weights"], 16)

            def load_image(b):
                for t in range(NT):
                    if not isinstance(b, int):
                        hold(sp, s["sp_go"], s["mm"], b * NT + (t - 3))
                    elif t >= 4:
                        hold(sp, s["sp_go"], s["mm"], t - 3)
                    sp.dma_start(xt[:, t % 4, :, :], x_v[bass.ds(b, 1), :, :, t * TT:(t + 1) * TT].rearrange(
                        "a p g t -> (a p) g t")).then_inc(s[f"x{t % 4}"], 16)

            def store(b):
                for j in range(3):
                    hold(sp, s["sp_go"], s[f"cut{j}"], (b + 1) * SIDE[j])
                    sp.dma_start(pat_d[j][bass.ds(b, 1), :].rearrange("a (c f) -> (a c) f", c=CB),
                                 flat[j][:, :]).then_inc(s[f"st{j}"], 16)

            load_image(0)
            with sp.Fori(0, B - 1) as b:
                load_image(b + 1)
                store(b)
            store(B - 1)
            for j in range(3):
                hold(sp, s["sp_go"], s[f"st{j}"], B * 16)

        @block.scalar
        def _(act):
            act.wait_ge(s["weights"], 32)
            with act.Fori(0, B // 2) as bb:
                for par in range(2):
                    b = bb * 2 + par
                    for t in range(NT):
                        act.wait_ge(s["mm"], b * NT + t + 1)
                        if t == 0:
                            act.wait_ge(s["cut0"], bb * (2 * SIDE[0]))
                            act.wait_ge(s["cut1"], bb * (2 * SIDE[1]))
                            act.wait_ge(s["cut2"], bb * (2 * SIDE[2]))
                        act.activation(xc[:, par, t * TT:(t + 1) * TT], p[:, t % 4, :], ACT.Identity,
                                       bias=bias[:, 0:1]).then_inc(s["conv"], 1)

        @block.gpsimd
        def _(pool):
            with pool.Fori(0, B // 2) as bb:
                for par in range(2):
                    b = bb * 2 + par
                    pool.wait_ge(s["conv"], (b + 1) * NT)
                    pool.wait_ge(s["st2"], b * 16)
                    pool.sem_inc(s["pool_go"], 1)
                    cutting(pool, lambda o, i: pool.tensor_scalar(o, i, 1.0, 0.0, ALU.mult, ALU.add), b, 2, par)

        @block.vector
        def _(dve):
            with dve.Fori(0, B // 2) as bb:
                for par in range(2):
                    b = bb * 2 + par
                    dve.wait_ge(s["conv"], (b + 1) * NT)
                    for j in range(2):
                        dve.wait_ge(s[f"st{j}"], b * 16)
                        cutting(dve, dve.tensor_copy, b, j, par)

        @block.tensor
        def _(pe):
            pe.wait_ge(s["weights"], 32)
            with pe.Fori(0, B) as b:
                for t in range(NT):
                    pe.wait_ge(s[f"x{t % 4}"], b * (NT // 4 * 16) + (t // 4 + 1) * 16)
                    pe.wait_ge(s["conv"], freed(b, t, 4, 1, NT))
                    pe.sem_inc(s["pe_go"], 1)
                    for g in range(2):
                        mm = pe.matmul(p[:, t % 4, :], w[:, g, :], xt[:, t % 4, g, :], start=(g == 0), stop=(g == 1))
                    mm.then_inc(s["mm"], 1)

    nc.clear_and_free_semaphores(list(s.values()))
    nc.all_engine_barrier()


def windows_attend(nc, sem, w2t, b2, wpos, bpos, wse1t, wse2t, pat_d, att_d):
    with ExitStack() as ctx:
        def sb(name, shape, dt=FP32):
            return ctx.enter_context(nc.sbuf_tensor("e_" + name, shape, dt))

        HW = tuple(n // 2 for n in NWIN)
        GW = tuple(512 // a for a in AREA)
        NG = tuple(HW[j] // GW[j] for j in range(3))
        groups = [(j, g) for j in range(3) for g in range(NG[j])]
        NGR = len(groups)
        NSC = 4
        pe_taps = ((0, 0), (-1, -1), (-1, 1), (1, -1), (1, 1))
        dve_taps = ((-1, 0), (1, 0), (0, -1), (0, 1))
        NT_D = len(dve_taps)

        def within(k, dy, dx):
            y0, y1, x0, x1 = max(0, -dy), k - max(0, dy), max(0, -dx), k - max(0, dx)
            return (slice(y0, y1), slice(x0, x1)), (slice(y0 + dy, y1 + dy), slice(x0 + dx, x1 + dx))

        ident = sb("ident", [128, 128])
        w2 = sb("w2", [128, 128])
        se1 = sb("se1", [128, 8])
        se2 = sb("se2", [8, 128])
        b2s = sb("b2s", [128, 1])
        bps = sb("bps", [128, 1])
        wp = sb("wp", [128, 9])
        dw = sb("dw", [128, 9, 128])
        u = [[sb(f"u{j}_{par}", [128, HW[j], AREA[j]]) for j in range(3)] for par in range(2)]
        scaled = sb("scaled", [128, NSC, 512])
        total = sb("total", [128, 2, max(HW)])
        mean_y = sb("mean_y", [128, max(HW)])
        hidden = sb("hidden", [8, max(HW)])
        gain = [sb(f"gain{j}", [128, HW[j]]) for j in range(3)]
        NB = 3
        p_y = ctx.enter_context(nc.psum_tensor("e_p_y", [128, NB, 512], FP32))
        p_d = ctx.enter_context(nc.psum_tensor("e_p_d", [128, NB, 512], FP32))
        p_se = ctx.enter_context(nc.psum_tensor("e_p_se", [128, 512], FP32))
        s = {k: sem("e_" + k) for k in (
            "made", "ident", "weights", "dw", "u00", "u10", "u20", "u01", "u11", "u21", "total", "se1", "mean", "se2", "hidden", "se3",
            "gain", "mm_y", "mm", "scaled", "tapped", "att", "st00", "st10", "st20", "st01", "st11", "st21", "sp_go", "pe_go")}
        block = ctx.enter_context(nc.Block())
        NW = 12

        def windows(n):
            j, g = groups[n]
            return slice(g * GW[j], (g + 1) * GW[j])

        def grouped(tile, n, depth):
            j = groups[n][0]
            return tile[:, n % depth, 0:GW[j] * AREA[j]].rearrange("p (w a) -> p w a", a=AREA[j])

        def halves(dram, b, j, h):
            v = dram[j].rearrange("b (h w c p) -> b h c w p", h=2, w=HW[j], c=CB)
            return v[bass.ds(b, 1), h, :, :, :].rearrange("a c w p -> (a c) w p")

        @block.sync
        def _(sp):
            hold(sp, s["sp_go"], s["made"], 4)
            for h in range(2):
                r = slice(64 * h, 64 * h + 64)
                sp.dma_start(w2[r, r], w2t).then_inc(s["weights"], 16)
                sp.dma_start(se1[r, 4 * h:4 * h + 4], wse1t).then_inc(s["weights"], 16)
                sp.dma_start(se2[4 * h:4 * h + 4, r], wse2t).then_inc(s["weights"], 16)
                sp.dma_start(b2s[r, :], b2.rearrange("(p a) -> p a", a=1)).then_inc(s["weights"], 16)
                sp.dma_start(bps[r, :], bpos.rearrange("(p a) -> p a", a=1)).then_inc(s["weights"], 16)
                sp.dma_start(wp[r, :], wpos).then_inc(s["weights"], 16)

            def load(bb, par):
                for j in range(3):
                    hold(sp, s["sp_go"], s[f"st{j}{par}"], bb * 32)
                    for h in range(2):
                        sp.dma_start(u[par][j][64 * h:64 * h + 64, :, :], halves(pat_d, 2 * bb + par, j, h)
                                     ).then_inc(s[f"u{j}{par}"], 16)

            def store(bb, par):
                b = 2 * bb + par
                for j in range(3):
                    hold(sp, s["sp_go"], s["att"], b * NGR + sum(NG[:j + 1]))
                    for h in range(2):
                        sp.dma_start(halves(att_d, b, j, h), u[par][j][64 * h:64 * h + 64, :, :]
                                     ).then_inc(s[f"st{j}{par}"], 16)

            for j in range(3):
                for h in range(2):
                    sp.dma_start(u[0][j][64 * h:64 * h + 64, :, :], halves(pat_d, 0, j, h)).then_inc(s[f"u{j}0"], 16)
            with sp.Fori(0, B // 2 - 1) as bb:
                load(bb, 1)
                store(bb, 0)
                load(bb + 1, 0)
                store(bb, 1)
            load(B // 2 - 1, 1)
            store(B // 2 - 1, 0)
            store(B // 2 - 1, 1)
            for j in range(3):
                for par in range(2):
                    hold(sp, s["sp_go"], s[f"st{j}{par}"], B // 2 * 32)

        @block.gpsimd
        def _(pool):
            for t in (w2, se1, se2, ident):
                pool.memset(t[:, :], 0.0).then_inc(s["made"], 1)
            pool.wait_ge(s["made"], 4)
            pool.affine_select(out=ident[:, :], in_=ident[:, :], compare_op=ALU.not_equal, fill=1.0, base=0,
                               pattern=[[-1, 128]], channel_multiplier=1).then_inc(s["ident"], 1)

        @block.scalar
        def _(act):
            act.wait_ge(s["weights"], NW * 16)
            with act.Fori(0, B) as b:
                for j in range(3):
                    n = HW[j]
                    act.wait_ge(s["se1"], b * 3 + j + 1)
                    act.activation(mean_y[:, 0:n], p_se[:, 0:n], ACT.Identity, bias=b2s[:, 0:1],
                                   scale=1.0 / AREA[j]).then_inc(s["mean"], 1)
                    act.wait_ge(s["se2"], b * 3 + j + 1)
                    act.activation(hidden[:, 0:n], p_se[0:8, 128:128 + n], ACT.Relu).then_inc(s["hidden"], 1)
                    act.wait_ge(s["se3"], b * 3 + j + 1)
                    act.wait_ge(s["scaled"], b * NGR)
                    act.activation(gain[j][:, :], p_se[:, 256:256 + n], ACT.Sigmoid).then_inc(s["gain"], 1)

        @block.vector
        def _(dve):
            dve.wait_ge(s["weights"], NW * 16)
            dve.wait_ge(s["ident"], 1)
            for t in range(9):
                dve.tensor_scalar(dw[:, t, :], ident[:, :], wp[:, t:t + 1], None, ALU.mult).then_inc(s["dw"], 1)
            with dve.Fori(0, B // 2) as bb:
                for par in range(2):
                    b = bb * 2 + par
                    for j in range(3):
                        dve.wait_ge(s[f"u{j}{par}"], (bb + 1) * 32)
                        if j >= 2:
                            dve.wait_ge(s["se1"], b * 3 + j - 1)
                        else:
                            dve.wait_ge(s["se1"], b * 3)
                        dve.tensor_reduce(total[:, j % 2, 0:HW[j]], u[par][j][:, :, :], AX.X, ALU.add).then_inc(s["total"], 1)
                    for first in range(0, NGR, 2):
                        pair = (first, first + 1)
                        for n in pair:
                            j, g = groups[n]
                            if g == 0:
                                dve.wait_ge(s["gain"], b * 3 + j + 1)
                            dve.wait_ge(s["mm_y"], b * NGR + n + 1)
                            dve.wait_ge(s["att"], freed(b, n, NSC, 1, NGR))
                            dve.scalar_tensor_tensor(
                                grouped(scaled, n, NSC), grouped(p_y, n, NB), b2s[:, 0:1],
                                gain[j][:, windows(n), None].broadcast_to([128, GW[j], AREA[j]]),
                                ALU.add, ALU.mult).then_inc(s["scaled"], 1)
                        for t, (dy, dx) in enumerate(dve_taps):
                            for i, n in enumerate(pair):
                                j, k = groups[n][0], SIDE[groups[n][0]]
                                (ys, xs), (yn, xn) = within(k, dy, dx)
                                if t == 0:
                                    dve.wait_ge(s["scaled"], b * NGR + n + 1)
                                else:
                                    dve.wait_ge(s["tapped"], (b * NGR + first) * NT_D + 2 * (t - 1) + i + 1)
                                acc, src = grouped(scaled, n, NSC), u[par][j][:, windows(n), :]
                                if dx == 0:
                                    acc, src = acc[:, :, ys.start * k:ys.stop * k], src[:, :, yn.start * k:yn.stop * k]
                                else:
                                    acc, src = (v.rearrange("p w (y x) -> p (w y) x", x=k)[:, :, c]
                                                for v, c in ((acc, xs), (src, xn)))
                                w = (dy + 1) * 3 + dx + 1
                                dve.scalar_tensor_tensor(acc, src, wp[:, w:w + 1], acc, ALU.mult, ALU.add
                                                         ).then_inc(s["tapped"], 1)
                        for i, n in enumerate(pair):
                            j = groups[n][0]
                            dve.wait_ge(s["mm"], b * NGR + n + 1)
                            dve.wait_ge(s["tapped"], (b * NGR + first) * NT_D + 2 * (NT_D - 1) + i + 1)
                            dve.scalar_tensor_tensor(u[par][j][:, windows(n), :], grouped(p_d, n, NB), bps[:, 0:1],
                                                     grouped(scaled, n, NSC), ALU.add, ALU.add).then_inc(s["att"], 1)

        @block.tensor
        def _(pe):
            pe.wait_ge(s["weights"], NW * 16)
            pe.wait_ge(s["dw"], 9)

            def squeeze(b, j):
                n = HW[j]
                k = b * 3 + j
                pe.wait_ge(s["total"], k + 1)
                pe.wait_ge(s["gain"], k)
                pe.matmul(p_se[:, 0:n], w2[:, :], total[:, j % 2, 0:n], start=True, stop=True).then_inc(s["se1"], 1)
                pe.wait_ge(s["mean"], k + 1)
                pe.matmul(p_se[0:8, 128:128 + n], se1[:, :], mean_y[:, 0:n], start=True, stop=True).then_inc(s["se2"], 1)
                pe.wait_ge(s["hidden"], k + 1)
                pe.matmul(p_se[:, 256:256 + n], se2[:, :], hidden[:, 0:n], start=True, stop=True).then_inc(s["se3"], 1)

            with pe.Fori(0, B // 2) as bb:
                for par in range(2):
                    b = bb * 2 + par
                    for n, (j, g) in enumerate(groups):
                        if g == 0:
                            squeeze(b, j)
                            pe.wait_ge(s[f"u{j}{par}"], (bb + 1) * 32)
                        k = SIDE[j]
                        pe.wait_ge(s["scaled"], freed(b, n, NB, 1, NGR))
                        pe.matmul(grouped(p_y, n, NB), w2[:, :], u[par][j][:, windows(n), :], start=True, stop=True
                                  ).then_inc(s["mm_y"], 1)
                        pe.wait_ge(s["att"], freed(b, n, NB, 1, NGR))
                        src = u[par][j][:, windows(n), :].rearrange("p w (y x) -> p w y x", x=k)
                        dst = grouped(p_d, n, NB).rearrange("p w (y x) -> p w y x", x=k)
                        for t, (dy, dx) in enumerate(pe_taps):
                            (ys, xs), (yn, xn) = within(k, dy, dx)
                            mm = pe.matmul(dst[:, :, ys, xs], dw[:, (dy + 1) * 3 + dx + 1, :], src[:, :, yn, xn],
                                           start=(t == 0), stop=(t == len(pe_taps) - 1))
                        mm.then_inc(s["mm"], 1)

    nc.clear_and_free_semaphores(list(s.values()))
    nc.all_engine_barrier()


def windows_fold(nc, sem, x1_d, w3t, b3, att_d, x2_d):
    with ExitStack() as ctx:
        def sb(name, shape, dt=FP32):
            return ctx.enter_context(nc.sbuf_tensor("f_" + name, shape, dt))

        w = sb("w", [128, 2, C])
        bias = sb("bias", [CH, 2])
        xt = sb("xt", [128, 2, 2, L])
        flat01 = sb("flat01", [128, 2, FLAT[0]])
        flat2 = sb("flat2", [CB, FLAT[2]])
        fold = sb("fold", [CB, L])
        out = sb("out", [CH, 2, 2, TT])
        p = ctx.enter_context(nc.psum_tensor("f_p", [CH, 4, TT], FP32))
        s = {k: sem("f_" + k) for k in ("zeroed", "weights", "x0", "x1", "in00", "in01", "in10", "in11", "in2", "clear", "add0", "add1", "add2", "half",
                                        "x_done", "mm", "out", "st0", "st1", "sp_go")}
        block = ctx.enter_context(nc.Block())
        o_v = x2_d.rearrange("b (h p) t -> b p h t", h=2)
        n2, k2, st2 = WINDOWS[2], SIDE[2], STEP[2]
        OVER = k2 - st2
        N_ADD2 = 2 * k2

        def view(img, flat_j, j, i, c0, c1):
            n, k, st = WINDOWS[j], SIDE[j], STEP[j]
            im = bass.AP(img.tensor, img.offset + i * IMG + c0, [img.ap[0], [st * IMG, n], [1, c1 - c0], [st, n]])
            fl = bass.AP(flat_j.tensor, flat_j.offset + (i * k + c0) * n * n,
                         [flat_j.ap[0], [n, n], [n * n, c1 - c0], [1, n]])
            return im, fl

        halves = (slice(0, CB), slice(CB, 128))

        @block.sync
        def _(sp):
            hold(sp, s["sp_go"], s["zeroed"], 3)
            sp.dma_start(w[:, 0, :], w3t[0:128, :]).then_inc(s["weights"], 16)
            sp.dma_start(w[0:CB, 1, :], w3t[128:, :]).then_inc(s["weights"], 16)
            sp.dma_start(bias[:, :], b3.rearrange("(h p) -> p h", h=2), allow_slow_non_contiguous=True).then_inc(s["weights"], 16)

            def store(b, t):
                hold(sp, s["sp_go"], s["out"], b * (NT * 2) + (t + 1) * 2)
                sp.dma_start(o_v[bass.ds(b, 1), :, :, t * TT:(t + 1) * TT].rearrange("a p h t -> (a p) h t"),
                             out[:, t % 2, :, :]).then_inc(s[f"st{t % 2}"], 16)

            def load(bb, par):
                b = bb * 2 + par
                hold(sp, s["sp_go"], s["add2"], b * N_ADD2)
                sp.dma_start(flat2[:, :], att_d[2][bass.ds(b, 1), :].rearrange("a (c f) -> (a c) f", c=CB)
                             ).then_inc(s["in2"], 16)
                if not isinstance(bb, int) or bb:
                    hold(sp, s["sp_go"], s["mm"], (b - 1) * (NT * 2))
                    for j in range(2):
                        hold(sp, s["sp_go"], s[f"add{j}"], (b - 1) * SIDE[j])
                sp.dma_start(xt[:, par, 0, :], x1_d[bass.ds(b, 1), 0:128, :].rearrange("a p t -> (a p) t")
                             ).then_inc(s[f"x{par}"], 16)
                sp.dma_start(xt[0:CB, par, 1, :], x1_d[bass.ds(b, 1), 128:, :].rearrange("a p t -> (a p) t")
                             ).then_inc(s[f"x{par}"], 16)
                for j in range(2):
                    sp.dma_start(flat01[halves[j], par, :], att_d[j][bass.ds(b, 1), :].rearrange(
                        "a (c f) -> (a c) f", c=CB)).then_inc(s[f"in{j}{par}"], 16)

            def store_image(b):
                for t in range(NT):
                    store(b, t)

            load(0, 0)
            with sp.Fori(0, B // 2 - 1) as bb:
                load(bb, 1)
                store_image(bb * 2)
                load(bb + 1, 0)
                store_image(bb * 2 + 1)
            load(B // 2 - 1, 1)
            store_image(B - 2)
            store_image(B - 1)
            for i in range(2):
                hold(sp, s["sp_go"], s[f"st{i}"], B * NT // 2 * 16)

        @block.gpsimd
        def _(pool):
            pool.memset(w[CB:, 1, :], 0.0).then_inc(s["zeroed"], 1)
            for par in range(2):
                pool.memset(xt[CB:, par, 1, :], 0.0).then_inc(s["zeroed"], 1)
            with pool.Fori(0, B // 2) as bb:
                for par in range(2):
                    b = bb * 2 + par
                    pool.wait_ge(s[f"x{par}"], (bb + 1) * 32)
                    pool.wait_ge(s[f"in0{par}"], (bb + 1) * 16)
                    for i in range(SIDE[0]):
                        im, fl = view(xt[halves[0], par, 0, :], flat01[halves[0], par, :], 0, i, 0, SIDE[0])
                        pool.tensor_tensor(im, im, fl, ALU.add).then_inc(s["add0"], 1)

        @block.vector
        def _(dve):
            with dve.Fori(0, B // 2) as bb:
                for par in range(2):
                    b = bb * 2 + par
                    dve.wait_ge(s["x_done"], b)
                    dve.memset(fold[:, :], 0.0).then_inc(s["clear"], 1)
                    dve.wait_ge(s["clear"], b + 1)
                    dve.wait_ge(s["in2"], (b + 1) * 16)
                    a = 0
                    for c0, c1 in ((0, st2), (st2, k2)):
                        for i in range(k2):
                            im, fl = view(fold[:, :], flat2[:, :], 2, i, c0, c1)
                            if i == st2 or (i == 0 and c0):
                                dve.wait_ge(s["add2"], b * N_ADD2 + a)
                            dve.tensor_tensor(im, im, fl, ALU.add).then_inc(s["add2"], 1)
                            a += 1
                    dve.wait_ge(s["add2"], b * N_ADD2 + a)
                    f0 = fold[:, :]
                    for i, dims in enumerate(([[st2 * IMG, n2 - 1], [1, OVER * IMG]],
                                              [[IMG, IMG], [st2, n2 - 1], [1, OVER]])):
                        v = bass.AP(f0.tensor, f0.offset + (st2 * IMG if i == 0 else st2), [f0.ap[0]] + dims)
                        dve.tensor_scalar(v, v, 0.5, None, ALU.mult).then_inc(s["half"], 1)
                        dve.wait_ge(s["half"], 2 * b + i + 1)
                    dve.wait_ge(s[f"x{par}"], (bb + 1) * 32)
                    dve.tensor_tensor(xt[0:CB, par, 1, :], xt[0:CB, par, 1, :], fold[:, :], ALU.add
                                      ).then_inc(s["x_done"], 1)
                    dve.wait_ge(s[f"in1{par}"], (bb + 1) * 16)
                    for i in range(SIDE[1]):
                        im, fl = view(xt[halves[1], par, 0, :], flat01[halves[1], par, :], 1, i, 0, SIDE[1])
                        dve.tensor_tensor(im, im, fl, ALU.add).then_inc(s["add1"], 1)

        @block.tensor
        def _(pe):
            pe.wait_ge(s["weights"], 48)
            with pe.Fori(0, B // 2) as bb:
                for par in range(2):
                    b = bb * 2 + par
                    pe.wait_ge(s["add0"], (b + 1) * SIDE[0])
                    pe.wait_ge(s["x_done"], b + 1)
                    pe.wait_ge(s["add1"], (b + 1) * SIDE[1])
                    for t in range(NT):
                        for m in range(2):
                            n = 2 * t + m
                            pe.wait_ge(s["out"], freed(b, n, 4, 1, NT * 2))
                            for g in range(2):
                                mm = pe.matmul(p[:, n % 4, :], w[:, g, m * CH:(m + 1) * CH],
                                               xt[:, par, g, t * TT:(t + 1) * TT], start=(g == 0), stop=(g == 1))
                            mm.then_inc(s["mm"], 1)

        @block.scalar
        def _(act):
            act.wait_ge(s["weights"], 48)
            with act.Fori(0, B) as b:
                for n in range(2 * NT):
                    t, m = n // 2, n % 2
                    act.wait_ge(s["mm"], b * (NT * 2) + n + 1)
                    if m == 0:
                        act.wait_ge(s[f"st{t % 2}"], b * (NT // 2 * 16) + t // 2 * 16)
                    act.activation(out[:, t % 2, m, :], p[:, n % 4, :], ACT.Identity,
                                   bias=bias[:, m:m + 1]).then_inc(s["out"], 1)

    nc.clear_and_free_semaphores(list(s.values()))
    nc.all_engine_barrier()


def gated_attention(nc, sem, x_in, w_query, w_key, w_value, w_out, rowmax_d, out_d):
    D = w_query.shape[1]
    G = 4
    DP = 32
    R3 = 3 * DP
    VC = DP
    KB = L // 128
    PAIR = 2 * TT
    NSLOT = 3
    UNITS = KB // 2
    QUADS = NT * UNITS // 2
    NP = 6
    LAG = 2

    SPAN = NT * UNITS
    LEAD, GAP = 8, 2
    MAXES = KB * (L // PAIR)
    FIRST_MAX = LEAD + GAP * NT + 3
    TAIL = SPAN + LAG + 2
    TURN_AT = SPAN - 8
    EARLY = NT - 2

    def schedule(second, first):
        plan = []
        for n in range(TAIL if second else 0):
            if n < SPAN:
                plan.append(("s", n))
            if first:
                t = (n - LEAD) // GAP
                if (n - LEAD) % GAP == 0 and 0 <= t < NT:
                    plan.append(("qk", t))
                if (n - LEAD) % GAP == 1 and 0 <= t <= NT:
                    plan.append(("split", t))
                if FIRST_MAX <= n < TURN_AT:
                    lo, hi = (MAXES * k // (TURN_AT - FIRST_MAX) for k in (n - FIRST_MAX, n - FIRST_MAX + 1))
                    plan += [("max", k) for k in range(lo, hi)]
                if n == TURN_AT:
                    plan.append(("turn", 0))
            for what, lag in (("weigh", LAG), ("o", LAG + 1), ("gate", 10), ("finish", 11)):
                m = n - lag
                if 0 <= m < SPAN and (m % 2 if what == "weigh" else m % UNITS == UNITS - 1):
                    plan.append((what, m if what == "weigh" else m // UNITS))
        if first and not second:
            for t in range(NT + 1):
                plan += [("qk", t)] * (t < NT) + [("split", t)]
            plan += [("max", k) for k in range(MAXES)]
            plan.append(("turn", 0))
        if second:
            plan.append(("gate", NT - 1))
        if first:
            plan.append(("v", 0))
        if second:
            plan.append(("finish", NT - 1))
        return plan

    EMPTIED_BY = {"qk": "act", "s": "act", "max": "dve", "v": "dve", "o": "dve"}

    class Passes:
        def __init__(self, second, first, base):
            self.plan = schedule(second, first)
            self.second, self.first, self.base = second, first, base
            self.order = [e for e in self.plan if e[0] in EMPTIED_BY]
            self.at = {key: n for n, key in enumerate(self.order)}
            self.emptied_by = [EMPTIED_BY[what] for what, _ in self.order]
            self.takes = {r: self.emptied_by.count(r) for r in ("act", "dve")}
            self.uses = len(self.order)

        def count(self, r, key):
            return self.base(r) + self.emptied_by[:self.at[key] + 1].count(r)

        def filled(self, key):
            return self.base("uses") + self.at[key] + 1

    def sizes(k):
        return {"act": k.takes["act"], "dve": k.takes["dve"], "uses": k.uses}

    opening = sizes(Passes(False, True, None))
    merged = sizes(Passes(True, True, None))

    def run(engine, program):
        def at_image(b, par, first):
            return program(Passes(True, first, lambda r: opening[r] + b * merged[r]), b, par)

        program(Passes(False, True, lambda r: 0), -1, 1)
        with engine.Fori(0, B // 2 - 1) as bb:
            for par in range(2):
                at_image(bb * 2 + par, par, True)
        at_image(B - 2, 0, True)
        at_image(B - 1, 1, False)

    def wait(engine, semaphore, value):
        if not isinstance(value, int) or value > 0:
            engine.wait_ge(semaphore, value)

    with ExitStack() as ctx:
        def sb(name, shape, dt=FP32):
            return ctx.enter_context(nc.sbuf_tensor("g_" + name, shape, dt))

        ident = sb("ident", [128, 128])
        wq = sb("wq", [CH, 2, R3])
        wk = sb("wk", [CH, 2, R3])
        wv = sb("wv", [CH, 2, D])
        wo = sb("wo", [128, C])
        den_sel = sb("den_sel", [128, CH])
        less = sb("less", [128, 3])
        x = sb("x", [CH, 2, 2, L])
        k_hhh = sb("k_hhh", [128, 2, L], BF16)
        second = sb("second", [128, 2, 2, L], BF16)
        q_hmh = sb("q_hmh", [R3, 2, L], BF16)
        q_high = sb("q_high", [R3, 2, TT], BF16)
        raw = sb("raw", [R3, 2, 2, TT])
        rest = sb("rest", [R3, 2, 2, TT])
        mid = sb("mid", [R3, 2, 2, TT], BF16)
        va = sb("va", [128, KB, DP])
        part_max = sb("part_max", [128, KB, L // PAIR])
        neg_max = sb("neg_max", [128, KB])
        max_t = sb("max_t", [KB, 3, 128], BF16)
        max_rest = sb("max_rest", [KB, 128])
        prob = sb("prob", [128, NP, PAIR])
        o_sb = sb("o_sb", [128, 2, TT])
        recip = sb("recip", [CH, TT])
        normed = sb("normed", [CH, 2, 2, TT])
        out = sb("out", [CH, 2, 2, TT])
        p_s = ctx.enter_context(nc.psum_tensor("g_p_s", [128, NSLOT, PAIR], FP32))
        p_o = ctx.enter_context(nc.psum_tensor("g_p_o", [128, TT], FP32))
        p_m = ctx.enter_context(nc.psum_tensor("g_p_m", [128, TT], FP32))
        s = {k: sem("g_" + k) for k in (
            "made", "ident", "weights", "x0", "x1", "filled", "emptied_by_act", "emptied_by_dve", "high", "rest", "mid", "split", "max",
            "max_mm", "max_step", "max_t", "max_st", "max_row", "weighed", "o_sb", "den", "recip", "normed", "gate",
            "out", "st0", "st1", "sp_go", "pe_go", "pool_go")}
        block = ctx.enter_context(nc.Block())
        x_v = x_in.rearrange("b (h p) t -> b p h t", h=2)
        o_v = out_d.rearrange("b (h p) t -> b p h t", h=2)

        def filled(eng, st, key):
            eng.wait_ge(s["filled"], st.filled(key))

        def slot(st, key):
            return p_s[:, st.at[key] % NSLOT, :]

        loads = [(wv[:, :, :], w_value.rearrange("(h p) n -> p h n", h=2))]
        for g in range(3):
            c = slice(DP * g, DP * g + D)
            loads.append((wq[:, :, c], w_query.rearrange("(h p) n -> p h n", h=2)))
            loads.append((wk[:, :, c], w_key.rearrange("(h p) n -> p h n", h=2)))
        for g in range(G):
            loads.append((wo[DP * g:DP * g + D, :], w_out))
        NL = len(loads)
        n_made = 8

        @block.sync
        def _(sp):
            hold(sp, s["sp_go"], s["made"], n_made)
            for dst, src in loads:
                sp.dma_start(dst, src).then_inc(s["weights"], 16)

            def load(q, par):
                sp.dma_start(x[:, par, :, :], x_v[bass.ds(q, 1), :, :, :].rearrange("a p h t -> (a p) h t")
                             ).then_inc(s[f"x{par}"], 16)

            def store(b, t):
                hold(sp, s["sp_go"], s["out"], b * NT + t + 1)
                sp.dma_start(o_v[bass.ds(b, 1), :, :, t * TT:(t + 1) * TT].rearrange("a p h t -> (a p) h t"),
                             out[:, t % 2, :, :]).then_inc(s[f"st{t % 2}"], 16)

            def passes(st, b, par):
                q, nxt = b + 1, 1 - par
                if st.second and st.first:
                    hold(sp, s["sp_go"], s["out"], b * NT)
                    load(q, nxt)
                if st.second:
                    for t in range(EARLY):
                        store(b, t)
                if st.first:
                    hold(sp, s["sp_go"], s["max_t"], q + 1)
                    sp.dma_start(rowmax_d[bass.ds(q, 1), :, :].rearrange("a r (k p) -> (a k) r p", p=128),
                                 max_t[:, :, :]).then_inc(s["max_st"], 16)
                    hold(sp, s["sp_go"], s["max_st"], (q + 1) * 16)
                    sp.dma_start(second[R3:R3 + 3, nxt, 0, :], rowmax_d[bass.ds(q, 1), :, :].rearrange(
                        "a r t -> (a r) t")).then_inc(s["max_row"], 16)
                if st.second:
                    for t in range(EARLY, NT):
                        store(b, t)

            load(0, 0)
            run(sp, passes)
            for i in range(2):
                hold(sp, s["sp_go"], s[f"st{i}"], B * NT // 2 * 16)

        @block.gpsimd
        def _(pool):
            for t in (ident, den_sel, wo, less):
                pool.memset(t[:, :], 0.0).then_inc(s["made"], 1)
            for t in (wq, wk, va):
                pool.memset(t[:, :, :], 0.0).then_inc(s["made"], 1)
            pool.wait_ge(s["made"], n_made - 1)
            pool.memset(k_hhh[R3:128, :, :], 1.0).then_inc(s["made"], 1)
            pool.wait_ge(s["made"], n_made)
            pool.affine_select(out=ident[:, :], in_=ident[:, :], compare_op=ALU.not_equal, fill=1.0, base=0,
                               pattern=[[-1, 128]], channel_multiplier=1).then_inc(s["ident"], 1)
            pool.memset(va[:, :, D:D + 1], 1.0).then_inc(s["ident"], 1)
            for n, (c, g) in enumerate(((0, 1), (0, 2), (1, 2), (2, 1))):
                pool.wait_ge(s["ident"], n + 2)
                pool.memset(less[DP * g:DP * g + DP, c:c + 1], -1.0).then_inc(s["ident"], 1)
            pool.wait_ge(s["ident"], 6)
            for g in range(G):
                pool.affine_select(out=den_sel[:, :], in_=den_sel[:, :], compare_op=ALU.not_equal, fill=1.0,
                                   base=-(DP * g + D), pattern=[[0, CH]], channel_multiplier=1).then_inc(s["ident"], 1)
                pool.wait_ge(s["ident"], 7 + g)
            with pool.Fori(0, B) as b:
                for t in range(NT):
                    pool.wait_ge(s["rest"], b * NT + t + 1)
                    pool.wait_ge(s["split"], freed(b, t, 2, 1, NT))
                    pool.sem_inc(s["pool_go"], 1)
                    pool.tensor_scalar(mid[:, t % 2, :, :], rest[:, t % 2, :, :], 1.0, 0.0, ALU.mult, ALU.add
                                       ).then_inc(s["mid"], 1)

        N_ID = 6 + G

        @block.scalar
        def _(act):
            act.wait_ge(s["ident"], N_ID)
            act.wait_ge(s["weights"], NL * 16)

            def projected(st, q, par, t):
                filled(act, st, ("qk", t))
                cols = slice(t * TT, (t + 1) * TT)
                both = slot(st, ("qk", t))[0:R3, :]
                wait(act, s["rest"], freed(q, t, 2, 1, NT))
                act.activation(q_high[:, t % 2, :], both[:, 0:TT], ACT.Copy)
                act.activation(k_hhh[0:R3, par, cols], both[:, TT:], ACT.Copy).then_inc(s["high"], 1)
                wait(act, s["split"], freed(q, t, 2, 1, NT))
                act.activation(raw[:, t % 2, :, :], both.rearrange("p (i t) -> p i t", i=2), ACT.Copy
                               ).then_inc(s["emptied_by_act"], 1)

            def weights_of(st, b, n):
                filled(act, st, ("s", n))
                wait(act, s["weighed"], b * QUADS + ((n - NP) // 2 + 1 if n >= NP else 0))
                act.activation(prob[:, n % NP, :], slot(st, ("s", n)), ACT.Exp).then_inc(s["emptied_by_act"], 1)

            def sums_out(b, t):
                act.wait_ge(s["weighed"], b * QUADS + (t + 1) * (UNITS // 2))
                wait(act, s["den"], freed(b, t, 2, 1, NT))
                act.activation(o_sb[:, t % 2, :], p_o[:, :], ACT.Copy).then_inc(s["o_sb"], 1)

            def gate_of(b, t):
                act.wait_ge(s["normed"], b * NT + t + 1)
                act.activation(normed[:, t % 2, :, :], normed[:, t % 2, :, :], ACT.Sigmoid).then_inc(s["gate"], 1)

            def passes(st, b, par):
                for what, n in st.plan:
                    if what == "qk":
                        projected(st, b + 1, 1 - par, n)
                    elif what == "s":
                        weights_of(st, b, n)
                    elif what == "weigh" and n % UNITS == UNITS - 1:
                        sums_out(b, n // UNITS)
                    elif what == "gate":
                        gate_of(b, n)

            run(act, passes)

        @block.vector
        def _(dve):
            dve.wait_ge(s["ident"], N_ID)
            dve.wait_ge(s["weights"], NL * 16)

            def split(st, q, par, t):
                if t < NT:
                    cols = slice(t * TT, (t + 1) * TT)
                    dve.wait_ge(s["emptied_by_act"], st.count("act", ("qk", t)))
                    dve.wait_ge(s["high"], q * NT + t + 1)
                    wait(dve, s["mid"], freed(q, t, 2, 1, NT))
                    v, high = raw[:, t % 2, 0, :], q_high[:, t % 2, :]
                    dve.scalar_tensor_tensor(q_hmh[:, par, cols], high, less[0:R3, 2:3], v, ALU.mult, ALU.add)
                    dve.scalar_tensor_tensor(rest[:, t % 2, 0, :], high, less[0:R3, 0:1], v, ALU.mult, ALU.add)
                    dve.tensor_tensor(rest[:, t % 2, 1, :], raw[:, t % 2, 1, :], k_hhh[0:R3, par, cols], ALU.subtract
                                      ).then_inc(s["rest"], 1)
                if t >= 1:
                    cols = slice((t - 1) * TT, t * TT)
                    dve.wait_ge(s["mid"], q * NT + t)
                    dve.scalar_tensor_tensor(second[0:R3, par, :, cols], mid[:, (t - 1) % 2, :, :], less[0:R3, 1:2],
                                             rest[:, (t - 1) % 2, :, :], ALU.mult, ALU.add).then_inc(s["split"], 1)

            def maximum(st, q, k):
                filled(dve, st, ("max", k))
                if k == 0:
                    wait(dve, s["max"], q * 1)
                i, h = k // (L // PAIR), k % (L // PAIR)
                dve.tensor_reduce(part_max[:, i, h:h + 1], slot(st, ("max", k)), AX.X, ALU.max).then_inc(s["emptied_by_dve"], 1)

            def maxima_out(st, q):
                dve.wait_ge(s["emptied_by_dve"], st.count("dve", ("max", MAXES - 1)))
                wait(dve, s["max_mm"], q * 1)
                dve.tensor_reduce(neg_max[:, :], part_max[:, :, :], AX.X, ALU.max, negate=True).then_inc(s["max"], 1)
                dve.wait_ge(s["max_mm"], q + 1)
                wait(dve, s["max_st"], q * 16)
                high, middle, low = (max_t[:, i, :] for i in range(3))
                dve.tensor_copy(high, p_m[0:KB, 0:128]).then_inc(s["max_step"], 1)
                dve.wait_ge(s["max_step"], q * 3 + 1)
                dve.tensor_tensor(max_rest[:, :], p_m[0:KB, 0:128], high, ALU.subtract).then_inc(s["max_step"], 1)
                dve.wait_ge(s["max_step"], q * 3 + 2)
                dve.tensor_copy(middle, max_rest[:, :]).then_inc(s["max_step"], 1)
                dve.wait_ge(s["max_step"], q * 3 + 3)
                dve.tensor_tensor(low, max_rest[:, :], middle, ALU.subtract).then_inc(s["max_t"], 1)

            def values_out(st, q):
                filled(dve, st, ("v", 0))
                wait(dve, s["weighed"], q * QUADS)
                dve.tensor_copy(va[:, :, 0:D], slot(st, ("v", 0)).rearrange("p (k c) -> p k c", c=DP)[:, :, 0:D]
                                ).then_inc(s["emptied_by_dve"], 1)

            def normalise(st, b, t):
                key = ("o", t)
                dve.wait_ge(s["den"], b * NT + t + 1)
                wait(dve, s["normed"], b * NT + t)
                dve.reciprocal(recip[:, :], p_m[0:CH, :]).then_inc(s["recip"], 1)
                dve.wait_ge(s["recip"], b * NT + t + 1)
                filled(dve, st, key)
                wait(dve, s["out"], freed(b, t, 2, 1, NT))
                dve.tensor_tensor(normed[:, t % 2, :, :], slot(st, key)[0:CH, :].rearrange("p (h t) -> p h t", h=2),
                                  recip[:, None, :].broadcast_to([CH, 2, TT]), ALU.mult).then_inc(s["emptied_by_dve"], 1)
                dve.wait_ge(s["emptied_by_dve"], st.count("dve", key))
                dve.sem_inc(s["normed"], 1)

            def finish(b, par, t):
                cols = slice(t * TT, (t + 1) * TT)
                wait(dve, s[f"st{t % 2}"], b * (NT // 2 * 16) + t // 2 * 16)
                dve.wait_ge(s["gate"], b * NT + t + 1)
                dve.scalar_tensor_tensor(out[:, t % 2, :, :], normed[:, t % 2, :, :], 1.0, x[:, par, :, cols],
                                         ALU.add, ALU.mult).then_inc(s["out"], 1)

            def passes(st, b, par):
                for what, n in st.plan:
                    if what == "split":
                        split(st, b + 1, 1 - par, n)
                    elif what == "max":
                        maximum(st, b + 1, n)
                    elif what == "turn":
                        maxima_out(st, b + 1)
                    elif what == "v":
                        values_out(st, b + 1)
                    elif what == "o":
                        normalise(st, b, n)
                    elif what == "finish":
                        finish(b, par, n)

            run(dve, passes)

        @block.tensor
        def _(pe):
            pe.wait_ge(s["ident"], N_ID)
            pe.wait_ge(s["weights"], NL * 16)

            def claim(st, key):
                n = st.at[key] - NSLOT
                if n >= 0:
                    pe.wait_ge(s[f"emptied_by_{st.emptied_by[n]}"], st.count(st.emptied_by[n], st.order[n]))
                else:
                    wait(pe, s["emptied_by_act"], st.base("act"))
                    wait(pe, s["emptied_by_dve"], st.base("dve"))
                pe.sem_inc(s["pe_go"], 1)

            def project(st, par, t):
                key = ("qk", t)
                claim(st, key)
                for i, w in enumerate((wq, wk)):
                    for h in range(2):
                        mm = pe.matmul(slot(st, key)[0:R3, i * TT:(i + 1) * TT], w[:, h, :],
                                       x[:, par, h, t * TT:(t + 1) * TT], start=(h == 0), stop=(h == 1))
                mm.then_inc(s["filled"], 1)

            def project_values(st, par):
                key = ("v", 0)
                claim(st, key)
                for kb in range(KB):
                    for h in range(2):
                        mm = pe.matmul(slot(st, key)[:, kb * DP:kb * DP + D], x[:, par, h, kb * 128:(kb + 1) * 128],
                                       wv[:, h, :], start=(h == 0), stop=(h == 1))
                mm.then_inc(s["filled"], 1)

            def scores_for_max(st, q, par, k):
                key = ("max", k)
                i, h = k // (L // PAIR), k % (L // PAIR)
                claim(st, key)
                if i == 0:
                    pe.wait_ge(s["split"], q * NT + 2 * h + 2)
                    pe.sem_inc(s["pe_go"], 1)
                rows = slice(i * 128, (i + 1) * 128)
                for j in range(2):
                    c = slice(h * PAIR + j * TT, h * PAIR + (j + 1) * TT)
                    to = slot(st, key)[:, j * TT:(j + 1) * TT]
                    pe.matmul(to, second[0:R3, par, 0, rows], k_hhh[0:R3, par, c], start=True, stop=False)
                    mm = pe.matmul(to, q_hmh[:, par, rows], second[0:R3, par, 1, c], start=False, stop=True)
                mm.then_inc(s["filled"], 1)

            def scores(st, b, par, n):
                t, u = n // UNITS, n % UNITS
                key = ("s", n)
                claim(st, key)
                if n == 0:
                    pe.wait_ge(s["max_row"], (b + 1) * 16)
                    pe.sem_inc(s["pe_go"], 1)
                c = slice(t * TT, (t + 1) * TT)
                for j in range(2):
                    k = slice((2 * u + j) * 128, (2 * u + j + 1) * 128)
                    to = slot(st, key)[:, j * TT:(j + 1) * TT]
                    pe.matmul(to, k_hhh[0:R3 + 3, par, k], second[0:R3 + 3, par, 0, c], start=True, stop=False)
                    mm = pe.matmul(to, second[0:R3, par, 1, k], q_hmh[:, par, c], start=False, stop=True)
                mm.then_inc(s["filled"], 1)

            def weigh(st, b, n):
                t, u = n // UNITS, n % UNITS
                pe.wait_ge(s["emptied_by_act"], st.count("act", ("s", n)))
                if u == 1:
                    wait(pe, s["o_sb"], b * NT + t)
                pe.sem_inc(s["pe_go"], 1)
                for g in range(G):
                    kb = 2 * (u - 1) + g
                    mm = pe.matmul(p_o[DP * g:DP * g + VC, :], va[:, kb, 0:VC],
                                   prob[:, (n - 1 + g // 2) % NP, g % 2 * TT:(g % 2 + 1) * TT],
                                   start=(kb < G), stop=(kb >= KB - G), tile_position=(0, DP * g))
                mm.then_inc(s["weighed"], 1)

            def project_out(st, b, t):
                key = ("o", t)
                pe.wait_ge(s["o_sb"], b * NT + t + 1)
                wait(pe, s["recip"], b * NT + t)
                if t == 0 or (t == NT - 1 and st.first):
                    pe.wait_ge(s["max_t"], b + 1 if t == 0 else b + 2)
                pe.sem_inc(s["pe_go"], 1)
                claim(st, key)
                pe.matmul(p_m[0:CH, :], den_sel[:, :], o_sb[:, t % 2, :], start=True, stop=True).then_inc(s["den"], 1)
                for m in range(2):
                    mm = pe.matmul(slot(st, key)[0:CH, m * TT:(m + 1) * TT], wo[:, m * CH:(m + 1) * CH],
                                   o_sb[:, t % 2, :], start=True, stop=True)
                mm.then_inc(s["filled"], 1)

            def turn(st, q):
                pe.wait_ge(s["max"], q + 1)
                wait(pe, s["recip"], q * NT - 1 if st.second else 0)
                pe.sem_inc(s["pe_go"], 1)
                pe.transpose(p_m[0:KB, 0:128], neg_max[:, :], ident[:, :]).then_inc(s["max_mm"], 1)

            def passes(st, b, par):
                q, nxt = b + 1, 1 - par
                for what, n in st.plan:
                    if what == "s":
                        scores(st, b, par, n)
                    elif what == "qk":
                        if n == 0:
                            pe.wait_ge(s[f"x{nxt}"], (q - nxt) * 8 + 16)
                            pe.sem_inc(s["pe_go"], 1)
                        project(st, nxt, n)
                    elif what == "max":
                        scores_for_max(st, q, nxt, n)
                    elif what == "weigh":
                        weigh(st, b, n)
                    elif what == "o":
                        project_out(st, b, n)
                    elif what == "turn":
                        turn(st, q)
                    elif what == "v":
                        project_values(st, nxt)

            run(pe, passes)

    nc.clear_and_free_semaphores(list(s.values()))
    nc.all_engine_barrier()


def attention(nc, sem, x_in, w_query, w_key, w_value, w_out, biases, out_d):
    D = w_query.shape[1]
    OC = D + 1
    VS = 128
    SCALE = float(D) ** -0.5
    KB = L // 128
    PAIR = 2 * TT
    PARTS = L // PAIR
    PB = PAIR // 128
    UNITS = KB * PARTS
    QT = TT // 128
    UT = QT * PARTS
    NSLOT = 3
    NP = 3
    VB = PAIR // VS
    TURN, WEIGH, MERGE, TURN_O, FINISH = 1, 2, 3, 4, 6
    STEPS = UNITS + FINISH

    def ends(n, lag, per):
        m = n - lag
        return m // per if 0 <= m < UNITS and m % per == per - 1 else None

    order = [("qk", t) for t in range(NT)]
    order += [("v", i) for i in range(KB // VB)]
    for n in range(STEPS):
        if n < UNITS:
            order.append(("s", n))
        if 0 <= n - TURN < UNITS:
            order.append(("t", n - TURN))
        if ends(n, TURN_O, UT) is not None:
            order.append(("n", ends(n, TURN_O, UT)))
        if ends(n, TURN_O + 1, UT) is not None:
            order.append(("o", ends(n, TURN_O + 1, UT)))
    emptied_by = ["dve" if what in ("v", "o") else "act" for what, _ in order]
    U = len(order)
    at = {key: n for n, key in enumerate(order)}
    takes = {r: emptied_by.count(r) for r in ("act", "dve")}

    with ExitStack() as ctx:
        def sb(name, shape, dt=FP32):
            return ctx.enter_context(nc.sbuf_tensor("h_" + name, shape, dt))

        ident = sb("ident", [128, 128])
        wq = sb("wq", [CH, 2, D])
        wk = sb("wk", [CH, 2, D])
        wv = sb("wv", [CH, 2, D])
        wo = sb("wo", [D, C])
        bias_q = sb("bias_q", [D, 1])
        bias_k = sb("bias_k", [D, 1])
        bias_v = sb("bias_v", [D, 1])
        bias_d = sb("bias_d", [CH, 2])
        bias_o = sb("bias_o", [CH, 2])
        x = sb("x", [CH, 2, 2, L])
        qa = sb("qa", [D, L])
        ka = sb("ka", [D, L])
        va = sb("va", [128, KB, OC])
        part_max = sb("part_max", [128, KB, PARTS])
        part_bias = sb("part_bias", [128, KB, PARTS])
        block_max = sb("block_max", [128, KB])
        block_bias = sb("block_bias", [128, KB])
        part_weight = sb("part_weight", [128, 2, PARTS])
        prob = sb("prob", [128, NP, PAIR])
        prob_t = sb("prob_t", [128, NP, PAIR])
        acc = sb("acc", [128, OC])
        recip = sb("recip", [128, 1])
        merged = sb("merged", [128, QT, D])
        o_t = sb("o_t", [D, TT])
        out = sb("out", [CH, 2, 2, TT])
        p_s = ctx.enter_context(nc.psum_tensor("h_p_s", [128, NSLOT, PAIR], FP32))
        p_o = ctx.enter_context(nc.psum_tensor("h_p_o", [128, 2, TT], FP32))
        s = {k: sem("h_" + k) for k in (
            "made", "ident", "weights", "bias_mm", "bias", "x0", "x1", "filled", "emptied_by_act", "emptied_by_dve", "max", "max_bias",
            "top", "top_bias", "part_weight", "weighed", "merge_step", "merged", "out", "st0", "st1", "sp_go",
            "pe_go")}
        block = ctx.enter_context(nc.Block())
        x_v = x_in.rearrange("b (h p) t -> b p h t", h=2)
        o_v = out_d.rearrange("b (h p) t -> b p h t", h=2)

        def filled(eng, b, key):
            eng.wait_ge(s["filled"], b * U + at[key] + 1)

        def slot(key):
            return p_s[:, at[key] % NSLOT, :]

        loads = [(dst[:, :, 0:D], src.rearrange("(h p) n -> p h n", h=2))
                 for dst, src in ((wq, w_query), (wk, w_key), (wv, w_value))]
        loads.append((wo[:, :], w_out))
        b_q, b_k, b_v, b_o = biases
        for dst, src in ((bias_q, b_q), (bias_k, b_k), (bias_v, b_v)):
            loads.append((dst[:, :], src.rearrange("(p a) -> p a", a=1)))
        NL = len(loads) + 1
        n_made = 1

        @block.sync
        def _(sp):
            hold(sp, s["sp_go"], s["made"], n_made)
            for dst, src in loads:
                sp.dma_start(dst, src).then_inc(s["weights"], 16)
            sp.dma_start(bias_d[:, :], b_o.rearrange("(h p) -> p h", h=2),
                         allow_slow_non_contiguous=True).then_inc(s["weights"], 16)
            with sp.Fori(0, B // 2) as bb:
                for par in range(2):
                    b = bb * 2 + par
                    hold(sp, s["sp_go"], s["out"], bb * (2 * NT))
                    sp.dma_start(x[:, par, :, :], x_v[bass.ds(b, 1), :, :, :].rearrange("a p h t -> (a p) h t")
                                 ).then_inc(s[f"x{par}"], 16)
                for par in range(2):
                    b = bb * 2 + par
                    for t in range(NT):
                        hold(sp, s["sp_go"], s["out"], b * NT + t + 1)
                        sp.dma_start(o_v[bass.ds(b, 1), :, :, t * TT:(t + 1) * TT].rearrange("a p h t -> (a p) h t"),
                                     out[:, t % 2, :, :]).then_inc(s[f"st{t % 2}"], 16)
            for i in range(2):
                hold(sp, s["sp_go"], s[f"st{i}"], B * NT // 2 * 16)

        @block.gpsimd
        def _(pool):
            pool.memset(ident[:, :], 0.0).then_inc(s["made"], 1)
            pool.wait_ge(s["made"], n_made)
            pool.affine_select(out=ident[:, :], in_=ident[:, :], compare_op=ALU.not_equal, fill=1.0, base=0,
                               pattern=[[-1, 128]], channel_multiplier=1).then_inc(s["ident"], 1)
            pool.memset(va[:, :, D:OC], 1.0).then_inc(s["ident"], 1)

        @block.scalar
        def _(act):
            act.wait_ge(s["weights"], NL * 16)
            act.wait_ge(s["bias_mm"], 1)
            for m in range(2):
                act.activation(bias_o[:, m:m + 1], p_o[0:CH, 0, m:m + 1], ACT.Identity,
                               bias=bias_d[:, m:m + 1]).then_inc(s["bias"], 1)

            def projected(b, t):
                key = ("qk", t)
                filled(act, b, key)
                cols = slice(t * TT, (t + 1) * TT)
                act.activation(qa[:, cols], slot(key)[0:D, 0:TT], ACT.Identity, bias=bias_q[:, 0:1])
                act.activation(ka[:, cols], slot(key)[0:D, TT:PAIR], ACT.Identity, bias=bias_k[:, 0:1]
                               ).then_inc(s["emptied_by_act"], 1)

            def weights_of(b, n):
                key = ("s", n)
                i, h = n // PARTS, n % PARTS
                filled(act, b, key)
                act.wait_ge(s["max_bias"], b * UNITS + n + 1)
                if n >= NP:
                    filled(act, b, ("t", n - NP))
                act.activation(prob[:, n % NP, :], slot(key), ACT.Exp, bias=part_bias[:, i, h:h + 1], scale=SCALE
                               ).then_inc(s["emptied_by_act"], 1)

            def weights_of_parts(b, i):
                act.wait_ge(s["top_bias"], b * KB + i + 1)
                act.wait_ge(s["merged"], freed(b, i, 2, 1, KB))
                act.activation(part_weight[:, i % 2, :], part_max[:, i, :], ACT.Exp, bias=block_bias[:, i:i + 1],
                               scale=SCALE).then_inc(s["part_weight"], 1)

            def turned(b, n):
                key = ("t", n)
                filled(act, b, key)
                act.wait_ge(s["weighed"], freed(b, n, NP, 1, UNITS))
                act.activation(prob_t[:, n % NP, :], slot(key), ACT.Copy).then_inc(s["emptied_by_act"], 1)

            with act.Fori(0, B) as b:
                act.wait_ge(s["weighed"], b * UNITS)
                for t in range(NT):
                    projected(b, t)
                for n in range(STEPS):
                    if n < UNITS:
                        weights_of(b, n)
                    if ends(n, 1, PARTS) is not None:
                        weights_of_parts(b, ends(n, 1, PARTS))
                    if 0 <= n - TURN < UNITS:
                        turned(b, n - TURN)
                    if ends(n, TURN_O, UT) is not None:
                        key = ("n", ends(n, TURN_O, UT))
                        filled(act, b, key)
                        act.activation(o_t[:, :], slot(key)[0:D, 0:TT], ACT.Copy).then_inc(s["emptied_by_act"], 1)

        @block.vector
        def _(dve):
            dve.wait_ge(s["ident"], 2)
            dve.wait_ge(s["weights"], NL * 16)
            dve.wait_ge(s["bias"], 2)

            def maximum(b, n):
                i, h = n // PARTS, n % PARTS
                k = b * UNITS + n + 1
                filled(dve, b, ("s", n))
                dve.tensor_reduce(part_max[:, i, h:h + 1], slot(("s", n)), AX.X, ALU.max).then_inc(s["max"], 1)
                dve.wait_ge(s["max"], k)
                dve.tensor_scalar(part_bias[:, i, h:h + 1], part_max[:, i, h:h + 1], -SCALE, None, ALU.mult
                                  ).then_inc(s["max_bias"], 1)
                if h == PARTS - 1:
                    dve.tensor_reduce(block_max[:, i:i + 1], part_max[:, i, :], AX.X, ALU.max, negate=True
                                      ).then_inc(s["top"], 1)
                    dve.wait_ge(s["top"], b * KB + i + 1)
                    dve.tensor_scalar(block_bias[:, i:i + 1], block_max[:, i:i + 1], SCALE, None, ALU.mult
                                      ).then_inc(s["top_bias"], 1)

            def merge(b, i):
                n0 = (b * KB + i) * (PARTS + 1)
                dve.wait_ge(s["weighed"], b * UNITS + (i + 1) * PARTS)
                dve.wait_ge(s["part_weight"], b * KB + i + 1)
                dve.wait_ge(s["merged"], b * KB + i)
                for h in range(PARTS):
                    part = p_o[:, i % 2, h * OC:(h + 1) * OC]
                    w = part_weight[:, i % 2, h:h + 1]
                    if h == 0:
                        dve.tensor_scalar(acc[:, :], part, w, None, ALU.mult).then_inc(s["merge_step"], 1)
                    else:
                        dve.wait_ge(s["merge_step"], n0 + h)
                        dve.scalar_tensor_tensor(acc[:, :], part, w, acc[:, :], ALU.mult, ALU.add
                                                 ).then_inc(s["merge_step"], 1)
                dve.wait_ge(s["merge_step"], n0 + PARTS)
                dve.reciprocal(recip[:, :], acc[:, D:OC]).then_inc(s["merge_step"], 1)
                dve.wait_ge(s["merge_step"], n0 + PARTS + 1)
                dve.tensor_scalar(merged[:, i % QT, :], acc[:, 0:D], recip[:, 0:1], None, ALU.mult
                                  ).then_inc(s["merged"], 1)

            def finish(b, par, t):
                key = ("o", t)
                cols = slice(t * TT, (t + 1) * TT)
                filled(dve, b, key)
                dve.wait_ge(s[f"st{t % 2}"], b * (NT // 2 * 16) + t // 2 * 16)
                for m in range(2):
                    ins = dve.scalar_tensor_tensor(out[:, t % 2, m, :], slot(key)[0:CH, m * TT:(m + 1) * TT],
                                                   bias_o[:, m:m + 1], x[:, par, m, cols], ALU.add, ALU.add)
                ins.then_inc(s["emptied_by_dve"], 1)
                dve.wait_ge(s["emptied_by_dve"], b * takes["dve"] + emptied_by[:at[key] + 1].count("dve"))
                dve.sem_inc(s["out"], 1)

            with dve.Fori(0, B // 2) as bb:
                for par in range(2):
                    b = bb * 2 + par
                    dve.wait_ge(s["weighed"], b * UNITS)
                    for i in range(KB // VB):
                        key = ("v", i)
                        filled(dve, b, key)
                        dve.tensor_copy(va[:, i * VB:(i + 1) * VB, 0:D],
                                        slot(key).rearrange("p (k c) -> p k c", c=VS)[:, :, 0:D]).then_inc(s["emptied_by_dve"], 1)
                    for n in range(STEPS):
                        if n < UNITS:
                            maximum(b, n)
                        if ends(n, MERGE, PARTS) is not None:
                            merge(b, ends(n, MERGE, PARTS))
                        if ends(n, FINISH, UT) is not None:
                            finish(b, par, ends(n, FINISH, UT))

        @block.tensor
        def _(pe):
            pe.wait_ge(s["ident"], 2)
            pe.wait_ge(s["weights"], NL * 16)
            for m in range(2):
                mm = pe.matmul(p_o[0:CH, 0, m:m + 1], wo[:, m * CH:(m + 1) * CH], bias_v[:, :], start=True, stop=True)
            mm.then_inc(s["bias_mm"], 1)
            pe.wait_ge(s["bias"], 2)

            def until_taken(b, key):
                r = emptied_by[at[key]]
                pe.wait_ge(s[f"emptied_by_{r}"], b * takes[r] + emptied_by[:at[key] + 1].count(r))
                pe.sem_inc(s["pe_go"], 1)

            def claim(b, key):
                if at[key] >= NSLOT:
                    until_taken(b, order[at[key] - NSLOT])
                else:
                    pe.wait_ge(s["emptied_by_act"], b * takes["act"])
                    pe.wait_ge(s["emptied_by_dve"], b * takes["dve"])
                    pe.sem_inc(s["pe_go"], 1)

            def project(b, par, t):
                key = ("qk", t)
                claim(b, key)
                for i, w in enumerate((wq, wk)):
                    for h in range(2):
                        mm = pe.matmul(slot(key)[0:D, i * TT:(i + 1) * TT], w[:, h, :],
                                       x[:, par, h, t * TT:(t + 1) * TT], start=(h == 0), stop=(h == 1))
                mm.then_inc(s["filled"], 1)

            def project_values(b, par, i):
                key = ("v", i)
                claim(b, key)
                for k in range(VB):
                    kb = i * VB + k
                    for h in range(2):
                        mm = pe.matmul(slot(key)[:, k * VS:k * VS + D], x[:, par, h, kb * 128:(kb + 1) * 128],
                                       wv[:, h, :], start=(h == 0), stop=(h == 1))
                mm.then_inc(s["filled"], 1)

            def scores(b, n):
                key = ("s", n)
                i, h = n // PARTS, n % PARTS
                claim(b, key)
                for j in range(2):
                    k = h * PAIR + j * TT
                    mm = pe.matmul(slot(key)[:, j * TT:(j + 1) * TT], qa[:, i * 128:(i + 1) * 128], ka[:, k:k + TT],
                                   start=True, stop=True)
                mm.then_inc(s["filled"], 1)

            def turn(b, n):
                key = ("t", n)
                until_taken(b, ("s", n))
                claim(b, key)
                for j in range(PB):
                    c = slice(j * 128, (j + 1) * 128)
                    mm = pe.transpose(slot(key)[:, c], prob[:, n % NP, c], ident[:, :])
                mm.then_inc(s["filled"], 1)

            def weigh(b, n):
                i, h = n // PARTS, n % PARTS
                until_taken(b, ("t", n))
                if h == 0:
                    pe.wait_ge(s["merged"], freed(b, i, 2, 1, KB))
                pe.sem_inc(s["pe_go"], 1)
                for j in range(PB):
                    mm = pe.matmul(p_o[:, i % 2, h * OC:(h + 1) * OC], prob_t[:, n % NP, j * 128:(j + 1) * 128],
                                   va[:, h * PB + j, :], start=(j == 0), stop=(j == PB - 1))
                mm.then_inc(s["weighed"], 1)

            def turn_out(b, t):
                key = ("n", t)
                pe.wait_ge(s["merged"], b * KB + (t + 1) * QT)
                claim(b, key)
                for i in range(QT):
                    mm = pe.transpose(slot(key)[0:D, i * 128:(i + 1) * 128], merged[:, i, :], ident[:, :])
                mm.then_inc(s["filled"], 1)

            def project_out(b, t):
                key = ("o", t)
                until_taken(b, ("n", t))
                claim(b, key)
                for m in range(2):
                    mm = pe.matmul(slot(key)[0:CH, m * TT:(m + 1) * TT], wo[:, m * CH:(m + 1) * CH], o_t[:, :],
                                   start=True, stop=True)
                mm.then_inc(s["filled"], 1)

            with pe.Fori(0, B // 2) as bb:
                for par in range(2):
                    b = bb * 2 + par
                    pe.wait_ge(s[f"x{par}"], (bb + 1) * 16)
                    for t in range(NT):
                        project(b, par, t)
                    for i in range(KB // VB):
                        project_values(b, par, i)
                    for n in range(STEPS):
                        if n < UNITS:
                            scores(b, n)
                        if 0 <= n - TURN < UNITS:
                            turn(b, n - TURN)
                        if 0 <= n - WEIGH < UNITS:
                            weigh(b, n - WEIGH)
                        if ends(n, TURN_O, UT) is not None:
                            turn_out(b, ends(n, TURN_O, UT))
                        if ends(n, TURN_O + 1, UT) is not None:
                            project_out(b, ends(n, TURN_O + 1, UT))

    nc.clear_and_free_semaphores(list(s.values()))
    nc.all_engine_barrier()


def four_layers(nc, x, v, out):
    def sem(name):
        return nc.alloc_semaphore(name=name)

    def scratch(name, shape, dt=FP32):
        return nc.dram_tensor(name, shape, dt, kind="Internal").ap()

    dt_d, dtx_d, xs_d, y_d = (scratch(n + "_scratch", (SEQ, NC, 128, EB, CK)) for n in ("dt", "dtx", "xs", "y"))
    bc_d = scratch("bc_scratch", (SEQ, NC, 96, CK), BF16)
    gate_d = scratch("gate_scratch", (B, NT, 128, EB, TT))
    x1_d, x2_d, x3_d = (scratch(f"x{n}_scratch", (B, C, L)) for n in (1, 2, 3))
    pat_d = [scratch(f"windows{j}_scratch", (B, CB * FLAT[j])) for j in range(3)]
    att_d = [scratch(f"attended{j}_scratch", (B, CB * FLAT[j])) for j in range(3)]
    max2_d = scratch("max2_scratch", (B, 3, L), BF16)

    mamba_inputs(nc, sem, x, v["gamma"], v["beta"], v["w_in"], v["conv_w"], v["conv_b"], v["w_xproj"], v["w_dt"],
                 v["b_dt"], dt_d, dtx_d, xs_d, bc_d, gate_d)
    selective_scan(nc, sem, v["a_log"], v["d"], dt_d, dtx_d, xs_d, bc_d, y_d)
    mamba_output(nc, sem, x, v["w_out"], y_d, gate_d, x1_d)
    windows_cut(nc, sem, x1_d, v["w1t"], v["b1"], pat_d)
    windows_attend(nc, sem, v["w2t"], v["b2"], v["wpos"], v["bpos"], v["wse1t"], v["wse2t"], pat_d, att_d)
    windows_fold(nc, sem, x1_d, v["w3t"], v["b3"], att_d, x2_d)
    gated_attention(nc, sem, x2_d, v["wqt"], v["wkt"], v["wvt"], v["wot"], max2_d, x3_d)
    n = v["wtt"].shape[1] // 3
    attention(nc, sem, x3_d, v["wtt"][:, 2 * n:], v["wtt"][:, 0:n], v["wtt"][:, n:2 * n], v["wdt"],
              (v["bt"][2 * n:], v["bt"][0:n], v["bt"][n:2 * n], v["bd"]), out)


_PLAIN = {"gamma": "L0_conv_gamma", "beta": "L0_conv_beta", "w_in": "L0_conv_W_in", "conv_w": "L0_conv_conv_w",
          "conv_b": "L0_conv_conv_b", "w_xproj": "L0_conv_W_xproj", "w_dt": "L0_conv_W_dt", "b_dt": "L0_conv_b_dt",
          "a_log": "L0_conv_A_log", "d": "L0_conv_D", "w_out": "L0_conv_W_out", "b1": "L1_conv_b1",
          "b2": "L1_conv_b2", "b3": "L1_conv_b3", "bpos": "L1_conv_bpos", "bt": "L3_conv_bt", "bd": "L3_conv_bd"}
_TURNED = {"w1t": "L1_conv_w1", "w2t": "L1_conv_w2", "w3t": "L1_conv_w3", "wse1t": "L1_conv_wse1",
           "wse2t": "L1_conv_wse2", "wqt": "L2_conv_Wq", "wkt": "L2_conv_Wk", "wvt": "L2_conv_Wv",
           "wot": "L2_conv_Wout", "wtt": "L3_conv_Wt", "wdt": "L3_conv_Wd"}


def kernel(**inputs):
    import numpy as _np
    import concourse.bacc as _bacc
    from concourse import mybir as _mybir
    from concourse.bass_utils import run_bass_kernel_spmd as _run

    nc = _bacc.Bacc("TRN2", target_bir_lowering=False, num_devices=1)
    arrays, views = {}, {}

    def put(name, a):
        a = _np.ascontiguousarray(a)
        arrays[f"in_{name}_dram"] = a
        views[name] = nc.dram_tensor(f"in_{name}_dram", a.shape, _mybir.dt.from_np(a.dtype), kind="ExternalInput").ap()

    x = inputs["x"]
    put("x", _np.asarray(x).reshape(x.shape[0], x.shape[1], -1))
    put("wpos", _np.asarray(inputs["L1_conv_wpos"]).reshape(-1, 9))
    for name, key in _PLAIN.items():
        put(name, inputs[key])
    for name, key in _TURNED.items():
        put(name, _np.asarray(inputs[key]).T)
    shape = views["x"].shape
    out = nc.dram_tensor("out_dram", shape, _mybir.dt.float32, kind="ExternalOutput").ap()
    four_layers(nc, views["x"], views, out)
    r = _run(nc, [arrays], core_ids=[0])
    return _np.asarray(r.results[0]["out_dram"]).reshape(x.shape)
```
